# Optimizing a Trainium2 kernel written in Bass

```python
import numpy as np
import jax
import jax.numpy as jnp

def _softmax(x, axis=-1):
    return jax.nn.softmax(x, axis=axis)

def _gelu(x):
    return jax.nn.gelu(x, approximate=True)

def _silu(x):
    return jax.nn.silu(x)

def _sigmoid(x):
    return jax.nn.sigmoid(x)

def _layernorm(x, axis=-1, eps=1e-05):
    m = jnp.mean(x, axis=axis, keepdims=True)
    v = jnp.var(x, axis=axis, keepdims=True)
    return (x - m) / jnp.sqrt(v + eps)

def _scatter_add(tgt, idx, src, axis=0):
    return tgt.at[idx].add(src)

def _segment_sum(src, seg, n):
    return jax.ops.segment_sum(src, seg, n)
kernel_name = 'mk_flamingo_gated_d2_seqx_r4_67ae4e'

def setup_inputs(seed: int=0):
    np.random.seed(seed)
    _w = jnp.asarray

    def _rec_inputs():
        import jax
        import jax.numpy as jnp
        _rk = jax.random.key(seed)
        x = 7.22e-05 + 1 * jax.random.normal(jax.random.fold_in(_rk, 1), (16, 128, 256), jnp.float32)
        _lenS = 128 - jax.random.randint(jax.random.fold_in(_rk, 7), (16,), 0, max(1, 128 // 4) + 1, jnp.int32)
        _lenS2 = 128 - jax.random.randint(jax.random.fold_in(_rk, 8), (16,), 0, max(1, 128 // 4) + 1, jnp.int32)
        _ctx_1024P = jax.random.normal(jax.random.fold_in(_rk, 11), (16, 16, 256), jnp.float32)
        _ctx_1024c = jax.random.dirichlet(jax.random.fold_in(_rk, 511), 0.3 * jnp.ones((16,), jnp.float32), (16, 128))
        _ctx_1024t = jnp.einsum('bsk,bkd->bsd', _ctx_1024c, _ctx_1024P)
        _ctx_1024t = _ctx_1024t * jax.lax.rsqrt(jnp.mean(jnp.square(_ctx_1024t)) + 1e-12) * 0.953939
        ctx_1024 = 4.13588e-05 + 0.999923 * (_ctx_1024t + 0.3 * jax.random.normal(jax.random.fold_in(_rk, 611), (16, 128, 256), jnp.float32))
        _validS = jnp.arange(128)[None, :] < _lenS[:, None]
        _validS2 = jnp.arange(128)[None, :] < _lenS2[:, None]
        _causal = jnp.tril(jnp.ones((128, 128), dtype=bool))
        mask_BxS_ik0 = jnp.where(jnp.broadcast_to(_validS[:, :], (16, 128)), 0, 1).astype(jnp.int32)
        _g = jax.random.normal(jax.random.fold_in(_rk, 9001), (2, 2), jnp.float32)
        _g = jnp.sign(_g) * jnp.maximum(jnp.abs(_g), 1.0) + (_g == 0) * 1.0
        g_xattn = _g[0]
        g_ffn = _g[1]
        return (x, ctx_1024, mask_BxS_ik0, g_xattn, g_ffn)
    x, ctx_1024, mask_BxS_ik0, g_xattn, g_ffn = _rec_inputs()

    def _L0_xattn_setup():
        import jax, jax.numpy as jnp
        import numpy as np
        D = 256
        H = 16
        HD = D // H
        key = jax.random.key(seed)
        ks = jax.random.split(key, 11)
        B, T = (4, 512)
        s = 1.0 / np.sqrt(D)
        inp = {'q': jax.random.normal(ks[0], (B, T, D), jnp.float32), 'k': jax.random.normal(ks[1], (B, T, D), jnp.float32), 'v': jax.random.normal(ks[2], (B, T, D), jnp.float32), 'Wq': jax.random.normal(ks[3], (D, D), jnp.float32) * s, 'bq': jnp.zeros((D,), jnp.float32), 'Wk': jax.random.normal(ks[4], (D, D), jnp.float32) * s, 'bk': jnp.zeros((D,), jnp.float32), 'Wv': jax.random.normal(ks[5], (D, D), jnp.float32) * s, 'bv': jnp.zeros((D,), jnp.float32), 'Wo': jax.random.normal(ks[6], (D, D), jnp.float32) * s, 'bo': jnp.zeros((D,), jnp.float32)}
        return inp
    _L0_xattn_all = _L0_xattn_setup()
    _L0_xattn_in = {k: v for k, v in _L0_xattn_all.items() if k in ('Wq', 'bq', 'Wk', 'bk', 'Wv', 'bv', 'Wo', 'bo')}
    del _L0_xattn_all

    def _L0_ffn_setup():
        import jax, jax.numpy as jnp
        import numpy as np
        B, S, D = (2, 256, 256)
        H = 128
        E = 16
        K = 2
        HS = 2 * H
        ROUTE_SCALE = 1.0

        def _gated_mlp_act(y):
            u, g = jnp.split(y, 2, axis=-1)
            return u * jax.nn.silu(g)
        key = jax.random.key(seed)
        ks = jax.random.split(key, 6)
        s = 0.02
        return {'x': jax.random.normal(ks[0], (B, S, D), dtype=jnp.float32), 'Wg': jax.random.normal(ks[1], (E, D), dtype=jnp.float32) * s, 'W1': jax.random.normal(ks[2], (E, D, 2 * H), dtype=jnp.float32) * s, 'W2': jax.random.normal(ks[3], (E, H, D), dtype=jnp.float32) * s, 'Ws1': jax.random.normal(ks[4], (D, 2 * HS), dtype=jnp.float32) * s, 'Ws2': jax.random.normal(ks[5], (HS, D), dtype=jnp.float32) * s}
    _L0_ffn_all = _L0_ffn_setup()
    _L0_ffn_in = {k: v for k, v in _L0_ffn_all.items() if k in ('Wg', 'W1', 'W2', 'Ws1', 'Ws2')}
    del _L0_ffn_all

    def _L1_xattn_setup():
        import jax, jax.numpy as jnp
        import numpy as np
        import math
        H = 16
        key = jax.random.key(seed)
        ks = jax.random.split(key, 12)
        B, S, D = (2, 512, 256)
        s = 1.0 / math.sqrt(D)
        return {'query': jax.random.normal(ks[0], (B, S, D), jnp.float32), 'key': jax.random.normal(ks[1], (B, S, D), jnp.float32), 'value': jax.random.normal(ks[2], (B, S, D), jnp.float32), 'Wq': jax.random.normal(ks[3], (D, D), jnp.float32) * s, 'bq': jax.random.normal(ks[4], (D,), jnp.float32) * 0.01, 'Wk': jax.random.normal(ks[5], (D, D), jnp.float32) * s, 'bk': jax.random.normal(ks[6], (D,), jnp.float32) * 0.01, 'Wv': jax.random.normal(ks[7], (D, D), jnp.float32) * s, 'bv': jax.random.normal(ks[8], (D,), jnp.float32) * 0.01, 'Wo': jax.random.normal(ks[9], (D, D), jnp.float32) * s, 'bo': jax.random.normal(ks[10], (D,), jnp.float32) * 0.01, 'mask': jax.random.randint(ks[11], (B, S), 0, 2, jnp.int32)}
    _L1_xattn_all = _L1_xattn_setup()
    _L1_xattn_in = {k: v for k, v in _L1_xattn_all.items() if k in ('Wq', 'bq', 'Wk', 'bk', 'Wv', 'bv', 'Wo', 'bo')}
    del _L1_xattn_all

    def _L1_ffn_setup():
        import jax, jax.numpy as jnp
        import numpy as np
        D_MODEL = 256
        D_FF = 1024
        NUM_EXPERTS = 8
        TOP_K = 2
        BATCH = 4
        SEQ = 512
        key = jax.random.key(seed)
        ks = jax.random.split(key, 8)
        s = 0.02
        x = jax.random.normal(ks[0], (BATCH, SEQ, D_MODEL), dtype=jnp.float32)
        router_w = jax.random.normal(ks[1], (D_MODEL, NUM_EXPERTS), dtype=jnp.float32) * s
        router_b = jnp.zeros((NUM_EXPERTS,), dtype=jnp.float32)
        W1 = jax.random.normal(ks[2], (NUM_EXPERTS, D_MODEL, D_FF), dtype=jnp.float32) * s
        b1 = jnp.zeros((NUM_EXPERTS, D_FF), dtype=jnp.float32)
        W2 = jax.random.normal(ks[3], (NUM_EXPERTS, D_FF, D_MODEL), dtype=jnp.float32) * s
        b2 = jnp.zeros((NUM_EXPERTS, D_MODEL), dtype=jnp.float32)
        return {'x': x, 'router_w': router_w, 'router_b': router_b, 'W1': W1, 'b1': b1, 'W2': W2, 'b2': b2}
    _L1_ffn_all = _L1_ffn_setup()
    _L1_ffn_in = {k: v for k, v in _L1_ffn_all.items() if k in ('router_w', 'router_b', 'W1', 'b1', 'W2', 'b2')}
    del _L1_ffn_all
    return {'x': x, 'ctx_1024': ctx_1024, 'mask_BxS_ik0': mask_BxS_ik0, 'g_xattn': g_xattn, 'g_ffn': g_ffn, 'L0_xattn_Wq': _L0_xattn_in['Wq'], 'L0_xattn_bq': _L0_xattn_in['bq'], 'L0_xattn_Wk': _L0_xattn_in['Wk'], 'L0_xattn_bk': _L0_xattn_in['bk'], 'L0_xattn_Wv': _L0_xattn_in['Wv'], 'L0_xattn_bv': _L0_xattn_in['bv'], 'L0_xattn_Wo': _L0_xattn_in['Wo'], 'L0_xattn_bo': _L0_xattn_in['bo'], 'L0_ffn_Wg': _L0_ffn_in['Wg'], 'L0_ffn_W1': _L0_ffn_in['W1'], 'L0_ffn_W2': _L0_ffn_in['W2'], 'L0_ffn_Ws1': _L0_ffn_in['Ws1'], 'L0_ffn_Ws2': _L0_ffn_in['Ws2'], 'L1_xattn_Wq': _L1_xattn_in['Wq'], 'L1_xattn_bq': _L1_xattn_in['bq'], 'L1_xattn_Wk': _L1_xattn_in['Wk'], 'L1_xattn_bk': _L1_xattn_in['bk'], 'L1_xattn_Wv': _L1_xattn_in['Wv'], 'L1_xattn_bv': _L1_xattn_in['bv'], 'L1_xattn_Wo': _L1_xattn_in['Wo'], 'L1_xattn_bo': _L1_xattn_in['bo'], 'L1_ffn_router_w': _L1_ffn_in['router_w'], 'L1_ffn_router_b': _L1_ffn_in['router_b'], 'L1_ffn_W1': _L1_ffn_in['W1'], 'L1_ffn_b1': _L1_ffn_in['b1'], 'L1_ffn_W2': _L1_ffn_in['W2'], 'L1_ffn_b2': _L1_ffn_in['b2']}

def reference(x, ctx_1024, mask_BxS_ik0, g_xattn, g_ffn, L0_xattn_Wq, L0_xattn_bq, L0_xattn_Wk, L0_xattn_bk, L0_xattn_Wv, L0_xattn_bv, L0_xattn_Wo, L0_xattn_bo, L0_ffn_Wg, L0_ffn_W1, L0_ffn_W2, L0_ffn_Ws1, L0_ffn_Ws2, L1_xattn_Wq, L1_xattn_bq, L1_xattn_Wk, L1_xattn_bk, L1_xattn_Wv, L1_xattn_bv, L1_xattn_Wo, L1_xattn_bo, L1_ffn_router_w, L1_ffn_router_b, L1_ffn_W1, L1_ffn_b1, L1_ffn_W2, L1_ffn_b2):
    import jax
    import jax.numpy as jnp

    def _L0_xattn_ref(q, k, v, Wq, bq, Wk, bk, Wv, bv, Wo, bo):
        import jax, jax.numpy as jnp
        import numpy as np
        D = 256
        H = 16
        HD = D // H
        B, Tq, _ = q.shape
        Tk = k.shape[1]
        qw = q @ Wq + bq
        kw = k @ Wk + bk
        vw = v @ Wv + bv
        qh = qw.reshape(B, Tq, H, HD)
        kh = kw.reshape(B, Tk, H, HD)
        vh = vw.reshape(B, Tk, H, HD)
        scale = 1.0 / np.sqrt(HD).astype(np.float32)
        logits = jnp.einsum('bqhd,bkhd->bhqk', qh, kh) * scale
        causal = jnp.tril(jnp.ones((Tq, Tk), bool))
        logits = jnp.where(causal, logits, -jnp.inf)
        attn = jax.nn.softmax(logits, axis=-1)
        out = jnp.einsum('bhqk,bkhd->bqhd', attn, vh).reshape(B, Tq, D)
        return out @ Wo + bo

    def _L0_ffn_ref(x, Wg, W1, W2, Ws1, Ws2):
        import jax, jax.numpy as jnp
        import numpy as np
        B, S, D = (2, 256, 256)
        H = 128
        E = 16
        K = 2
        HS = 2 * H
        ROUTE_SCALE = 1.0

        def _gated_mlp_act(y):
            u, g = jnp.split(y, 2, axis=-1)
            return u * jax.nn.silu(g)
        x_shape = x.shape
        xf = x.reshape(-1, D)
        scores = jax.nn.softmax(xf @ Wg.T, axis=-1)
        wk, idx = jax.lax.top_k(scores, K)
        wk = wk * ROUTE_SCALE
        cw = jnp.sum(jax.nn.one_hot(idx, E, dtype=xf.dtype) * wk[..., None], axis=1)
        h = _gated_mlp_act(jnp.einsum('td,edh->teh', xf, W1))
        z = jnp.einsum('te,teh,ehd->td', cw, h, W2)
        ys = _gated_mlp_act(xf @ Ws1) @ Ws2
        return (z + ys).reshape(x_shape)

    def _L1_xattn_ref(query, key, value, Wq, bq, Wk, bk, Wv, bv, Wo, bo, mask):
        import jax, jax.numpy as jnp
        import numpy as np
        import math
        H = 16
        B, S, D = query.shape
        dk = D // H

        def proj(x, W, b):
            return (x @ W.T + b).reshape(B, -1, H, dk).transpose(0, 2, 1, 3)
        q = proj(query, Wq, bq)
        k = proj(key, Wk, bk)
        v = proj(value, Wv, bv)
        scores = jnp.einsum('bhqd,bhkd->bhqk', q, k) / math.sqrt(dk)
        scores = jnp.where(mask[:, None, :, None] == 0, jnp.float32(-1000000000.0), scores)
        attn = jax.nn.softmax(scores, axis=-1)
        out = jnp.einsum('bhqk,bhkd->bhqd', attn, v)
        out = out.transpose(0, 2, 1, 3).reshape(B, S, D)
        return out @ Wo.T + bo

    def _L1_ffn_ref(x, router_w, router_b, W1, b1, W2, b2):
        import jax, jax.numpy as jnp
        import numpy as np
        D_MODEL = 256
        D_FF = 1024
        NUM_EXPERTS = 8
        TOP_K = 2
        BATCH = 4
        SEQ = 512
        logits = jnp.einsum('bsd,de->bse', x, router_w) + router_b
        topk_scores, topk_idx = jax.lax.top_k(logits, TOP_K)
        topk_gates = jax.nn.softmax(topk_scores, axis=-1)
        onehot = jax.nn.one_hot(topk_idx, NUM_EXPERTS, dtype=x.dtype)
        combine = jnp.einsum('bsk,bske->bse', topk_gates, onehot)
        combine_e = jnp.moveaxis(combine, -1, 0)

        def expert_step(acc, params):
            w1, bb1, w2, bb2, c = params
            h = jax.nn.relu(jnp.einsum('bsd,df->bsf', x, w1) + bb1)
            y = jnp.einsum('bsf,fd->bsd', h, w2) + bb2
            return (acc + y * c[..., None], None)
        out, _ = jax.lax.scan(expert_step, jnp.zeros_like(x), (W1, b1, W2, b2, combine_e))
        return out
    x = x + jnp.tanh(g_xattn[0]) * _L0_xattn_ref(_layernorm(x, axis=-1), ctx_1024, ctx_1024, L0_xattn_Wq, L0_xattn_bq, L0_xattn_Wk, L0_xattn_bk, L0_xattn_Wv, L0_xattn_bv, L0_xattn_Wo, L0_xattn_bo)
    x = x + jnp.tanh(g_ffn[0]) * _L0_ffn_ref(_layernorm(x, axis=-1), L0_ffn_Wg, L0_ffn_W1, L0_ffn_W2, L0_ffn_Ws1, L0_ffn_Ws2)
    x = x + jnp.tanh(g_xattn[1]) * _L1_xattn_ref(_layernorm(x, axis=-1), ctx_1024, ctx_1024, L1_xattn_Wq, L1_xattn_bq, L1_xattn_Wk, L1_xattn_bk, L1_xattn_Wv, L1_xattn_bv, L1_xattn_Wo, L1_xattn_bo, mask_BxS_ik0)
    x = x + jnp.tanh(g_ffn[1]) * _L1_ffn_ref(_layernorm(x, axis=-1), L1_ffn_router_w, L1_ffn_router_b, L1_ffn_W1, L1_ffn_b1, L1_ffn_W2, L1_ffn_b2)
    return x

_drawn_inputs = setup_inputs


def setup_inputs(seed=0):
    import zlib

    import numpy as np

    out = dict(_drawn_inputs(seed))
    spreads = {'g_ffn': (-1.0, 0.6),
     'L0_xattn_bq': (0.0, 0.396),
     'L0_xattn_bk': (0.0, 2.0),
     'L0_xattn_bv': (0.0, 0.1),
     'L0_xattn_bo': (0.0, 0.1),
     'L1_ffn_router_b': (0.0, 0.386),
     'L1_ffn_b1': (0.0, 1.183),
     'L1_ffn_b2': (0.0, 0.505)}
    factors = {'L0_ffn_Wg': 8.0,
     'L0_ffn_W1': 8.0,
     'L0_ffn_W2': 8.0,
     'L0_ffn_Ws1': 4.383,
     'L0_ffn_Ws2': 4.283,
     'L1_xattn_bq': 64.0,
     'L1_xattn_bk': 64.0,
     'L1_xattn_bv': 25.036,
     'L1_xattn_bo': 23.232,
     'L1_xattn_Wq': 3.315,
     'L1_xattn_Wk': 3.288,
     'L1_ffn_W1': 2.772}
    for name, (base, spread) in spreads.items():
        noise = np.random.default_rng([zlib.crc32(name.encode()), seed]).standard_normal(out[name].shape)
        drawn = base * np.exp(spread * noise) if base else spread * noise
        out[name] = jnp.asarray(drawn.astype(out[name].dtype))
    for name, factor in factors.items():
        out[name] = (out[name] * factor).astype(out[name].dtype)
    return out
```

```python
from contextlib import ExitStack

import concourse.bass as bass
from concourse import mybir

F32 = mybir.dt.float32
BF16 = mybir.dt.bfloat16
I32 = mybir.dt.int32
ALU = mybir.AluOpType
ACT = mybir.ActivationFunctionType
AX = mybir.AxisListType

P = 128
T = 16
D = 256
KT = D // P
H = 16
HD = D // H
GH = 4
G = H // GH
VW = HD + 1
EPS = 1e-5
NEG = -1e30
EXPERTS = (16, 8)
SLOT_TILES = (48, 40)
F0 = 128
F1 = 1024
FS = 256
SLAB = (KT * 2 * F0 + D, F1 + (F1 // P // 2) * D)


class Tile:

    def __init__(self, r, off):
        self.r, self.off = r, off

    def plus(self, k):
        return Tile(self.r, self.off + k)

    @property
    def v(self):
        return 2 * self.r + self.off

    @property
    def par(self):
        return self.off % 2

    @property
    def half(self):
        return self.r + self.off // 2


def at(ap, i):
    return ap[:, bass.ds(i, 1), :].rearrange("p a d -> p (a d)")


def need(eng, sem, v):
    if isinstance(v, int) and v <= 0:
        return
    eng.wait_ge(sem, v)


class Gate:

    def __init__(self, eng, passed):
        self.eng, self.passed, self.count, self.trips = eng, passed, 0, 1

    def __call__(self, *waits):
        for sem, v in waits:
            need(self.eng, sem, v)
        if not all(isinstance(v, int) for _, v in waits):
            self.eng.sem_inc(self.passed, 1)
            self.count += self.trips

    def close(self):
        if self.count:
            self.eng.wait_ge(self.passed, self.count)


def tiles(eng, n, first, last, step, gate=None):
    pairs = (n - first - last) // 2
    assert first + 2 * pairs + last == n
    for i in range(first):
        step(Tile(0, i))
    if gate:
        gate.trips = pairs
    with eng.Fori(0, pairs) as r:
        step(Tile(r, first))
        step(Tile(r, first + 1))
    if gate:
        gate.trips = 1
    for i in range(n - last, n):
        step(Tile(0, i))


def build(nc, A, out):
    with ExitStack() as ctx:
        def sb(name, shape, dt=F32):
            return ctx.enter_context(nc.sbuf_tensor(name, shape, dt))

        def sem(name):
            return ctx.enter_context(nc.semaphore(name))

        def sem2(name):
            return [sem(f"{name}{i}") for i in range(2)]

        bank = [ctx.enter_context(nc.psum_tensor(f"bank{i}", [P, 512], F32)) for i in range(8)]

        x = sb("x", [P, T, D])
        arena = sb("arena", [P, 65536], BF16)
        wat = sb("wat", [P, 4, KT, D])
        cf = sb("cf", [P, 208])
        cb = sb("cb", [P, 3 * P + GH * P], BF16)
        bqk = sb("bqk", [P, 2, 2, KT])
        bvo = sb("bvo", [P, 2, D])
        wr = sb("wr", [P, KT, 24])
        rb = sb("rb", [P, 8])
        gates = sb("gates", [P, 4])
        tgate = sb("tgate", [P, 4])
        qmask = sb("qmask", [P, T], I32)
        qscale = sb("qscale", [P, T])
        mhalf = sb("mhalf", [P, 1])
        b1 = sb("b1", [P, 8 * F1 // P])
        stats = sb("stats", [P, 6])
        meanvar = sb("meanvar", [P, 2])
        vareps = sb("vareps", [P, 1])
        rstd = sb("rstd", [P, 1])
        slot = sb("slot", [P, 2, T], I32)
        gsel = sb("gsel", [P, 2, T])
        tile_expert = sb("tile_expert", [P, 48], I32)

        ident = cf[:, 0:128]
        headrow = cf[:, 128:136]
        rev = (cf[:, 136:152], cf[:, 152:160])
        starts = cf[:, 160:208]
        identb, onesb, earlier = (cb[:, i * P:(i + 1) * P] for i in range(3))
        causal = cb[:, 3 * P:]

        work = sb("work", [P, 10824])
        used = [0]

        def part(cols):
            v = work[:, used[0]:used[0] + cols]
            used[0] += cols
            return v

        xn = [part(D) for _ in range(2)]
        xnT = [part(KT * P) for _ in range(2)]
        stage = part(SLAB[1])
        shared_cols = used[0]
        kbd = part(KT * 8 * P).rearrange("p (m h t) -> p m h t", m=KT, h=8)
        prob = [part(GH * P) for _ in range(2)]
        shifted = [part(GH * P) for _ in range(2)]
        cb32 = work[:, used[0] - 2 * GH * P:used[0] - 2 * GH * P + 7 * P]
        probT = [part(GH * P) for _ in range(2)]
        qT = [part(KT * P) for _ in range(2)]
        kT = part(KT * P)
        vaug = [part(H * VW).rearrange("p (h w) -> p h w", h=H) for _ in range(2)]
        ctxT = [part(KT * P) for _ in range(2)]
        on = part(D)
        oT = part(KT * P)
        proj = part(D)
        rsum = part(H)
        rowmax = [part(GH) for _ in range(2)]
        used[0] = shared_cols
        xs = part(T * D).bitcast(BF16).rearrange("p (t d) -> p t d", t=T)
        logit = part(T * 16)
        rtmp = [part(T * 16) for _ in range(6)]
        rsmall = part(16 * T)
        used[0] = shared_cols - SLAB[1]
        sh_hid = [part(FS) for _ in range(2)]
        sh_act = [part(FS) for _ in range(2)]
        sh_hhi = [part(FS // 2).bitcast(BF16) for _ in range(2)]
        sh_hlo = [part(FS // 2).bitcast(BF16) for _ in range(2)]
        assert used[0] <= shared_cols
        used[0] = 0
        rows = [part(D).bitcast(BF16) for _ in range(2)]
        rowsT = [part(D).bitcast(BF16) for _ in range(2)]
        hid = [part(F1) for _ in range(2)]
        sig = [part(F0) for _ in range(2)]
        hid_hi = [part(F1 // 2).bitcast(BF16) for _ in range(2)]
        hid_lo = [part(F1 // 2).bitcast(BF16) for _ in range(2)]
        yrow = [part(D) for _ in range(2)]
        b2 = part(8 * D).rearrange("p (e d) -> p e d", e=8)
        used[0] = 0
        ygot = [[part(D) for _ in range(2)] for _ in range(2)]

        whi, wlo = [], []
        for L in range(2):
            n = T * SLAB[L]
            whi.append(arena[:, 0:n].rearrange("p (s f) -> p s f", s=T))
            wlo.append(arena[:, n:2 * n].rearrange("p (s f) -> p s f", s=T))
        o = 2 * T * SLAB[0]
        xT = arena[:, o:o + T * 4 * P].rearrange("p (t c) -> p t c", t=T)
        o += T * 4 * P
        NS = KT * 2 * FS + KT * D
        shi, slo = arena[:, o:o + NS], arena[:, o + NS:o + 2 * NS]
        o += 2 * NS
        sstage = arena[:, o:o + 2 * NS].bitcast(F32)
        o += 2 * NS
        zeros = arena[:, o:o + 2048]

        xg = [nc.dram_tensor(f"xg{L}", [SLOT_TILES[L] * P, 2 * D], BF16, kind="Internal").ap() for L in range(2)]
        y = [nc.dram_tensor(f"y{L}", [SLOT_TILES[L] * P, D], F32, kind="Internal").ap() for L in range(2)]

        const_in = sem("const_in")
        wat_in = sem("wat_in")
        bv_in = sem("bv_in")
        ctx_in, x_in = sem2("ctx_in"), sem2("x_in")
        stage_in = sem("stage_in")
        sw_in = sem("sw_in")
        zero_set, zero_out = sem("zero_set"), sem("zero_out")
        set_ok, half_set, cb_ok = sem("set_ok"), sem("half_set"), sem("cb_ok")
        ones_ok = sem("ones_ok")
        st_ok, mv_ok, ve_ok, rstd_ok, xn_ok = (sem(s) for s in ("st_ok", "mv_ok", "ve_ok", "rstd_ok", "xn_ok"))
        pe_T, xnT_ok = sem("pe_T"), sem("xnT_ok")
        pe_k, pe_v, pe_q = sem("pe_k"), sem("pe_v"), sem("pe_q")
        k_ok, v_ok, q_ok = sem("k_ok"), sem("v_ok"), sem("q_ok")
        kbd0_ok, kbd1_ok = sem("kbd0_ok"), sem("kbd1_ok")
        pe_s, mx_ok, sc_ok, exp_ok = sem("pe_s"), sem("mx_ok"), sem("sc_ok"), sem("exp_ok")
        pe_pt, pt_ok, pe_pv = sem("pe_pt"), sem("pt_ok"), sem("pe_pv")
        rs_ok, o_ok, pe_oT, oT_ok, pe_o, t_ok, x_ok = (
            sem(s) for s in ("rs_ok", "o_ok", "pe_oT", "oT_ok", "pe_o", "t_ok", "x_ok"))
        hi_ok, lo_ok = sem("hi_ok"), sem("lo_ok")
        pe_lg, lg_ok, xthi_ok, xt_ok, xshi_ok, xs_ok = (
            sem(s) for s in ("pe_lg", "lg_ok", "xthi_ok", "xt_ok", "xshi_ok", "xs_ok"))
        dve_link = sem("dve_link")
        expo_ok, m_ok, pe_rank, slot_ok = sem("expo_ok"), sem("m_ok"), sem("pe_rank"), sem("slot_ok")
        scattered = sem("scattered")
        sh_up, sh_sig, sh_h, sh_hi, sh_lo, sh_dn, sh_x = (
            sem("sh_" + s) for s in ("up", "sig", "h", "hi", "lo", "dn", "x"))
        sws_ok = sem("sws_ok")
        ex = [{s: sem(f"ex{L}_{s}") for s in
               ("rows0", "rows1", "pe_rT", "rT", "up", "upb", "sig", "h", "ha", "hi", "lo", "dn", "y", "out0", "out1")}
              for L in range(2)]
        got = [sem2(f"got{L}_") for L in range(2)]
        half_ok, cx_ok = sem("half_ok"), sem("cx_ok")
        b2_in = sem("b2_in")
        stored = sem2("stored")
        gate_sem = {e: sem("gate_" + e) for e in ("act", "dve", "pe", "pool", "sp")}

        block = ctx.enter_context(nc.Block())

        @block.sync
        def _(sp):
            small = [(cf[:], A["cf"]), (cb32, A["cb"]), (bqk[:].rearrange("p l a k -> p (l a k)"), A["bqk"]),
                     (wr[:].rearrange("p k e -> p (k e)"), A["wr"]), (qmask[:], A["qmask"]), (b1[:], A["b1"]),
                     (gates[:, 0:2], A["g_xattn"].partition_broadcast(P)), (gates[:, 2:4], A["g_ffn"].partition_broadcast(P)),
                     (rb[:], A["L1_ffn_router_b"].partition_broadcast(P))]
            assert len(small) == SMALL

            def load_x(t):
                sp.dma_start(at(x, t.v), A["x"][bass.ds(t.v, 1)].rearrange("a p d -> (a p) d")).then_inc(x_in[t.par], 16)

            def load_ctx(L, t):
                n = t.plus(T * L)
                need(sp, pe_v, n.v - 1)
                sp.dma_start(ctxT[t.par], A["ctxT"][bass.ds(t.v, 1)].rearrange("a p d -> (a p) d")).then_inc(ctx_in[t.par], 16)

            def load_stage(L, t):
                n = t.plus(T * L)
                need(sp, hi_ok, n.v)
                need(sp, lo_ok, n.v)
                sp.dma_start(stage[:, 0:SLAB[L]], A[f"slab{L}"][bass.ds(t.v, 1)].rearrange("a p d -> (a p) d")).then_inc(stage_in, 16)

            def load_layer(L):
                sp.dma_start(wat[:].rearrange("p a k d -> p (a k d)"), A[f"wat{L}"]).then_inc(wat_in, 16)
                for i, name in enumerate(("bv", "bo")):
                    sp.dma_start(bvo[:, i, :], A[f"L{L}_xattn_{name}"].partition_broadcast(P)).then_inc(bv_in, 16)

            load_x(Tile(0, 0))
            for d, s in small:
                sp.dma_start(d, s).then_inc(const_in, 16)
            load_ctx(0, Tile(0, 0))
            load_layer(0)
            load_x(Tile(0, 1))
            load_ctx(0, Tile(0, 1))
            load_stage(0, Tile(0, 0))
            sp.dma_start(sstage, A["shared_w"]).then_inc(sw_in, 16)
            sp.wait_ge(zero_set, 1)
            for L in range(2):
                flat = xg[L].rearrange("(p a) d -> p (a d)", p=P)
                for c in range(0, flat.shape[1], 2048):
                    sp.dma_start(flat[:, c:c + 2048], zeros).then_inc(zero_out, 16)

            for L in range(2):
                if L:
                    sp.wait_ge(cx_ok, T)
                    load_ctx(1, Tile(0, 0))
                    load_ctx(1, Tile(0, 1))
                    load_stage(1, Tile(0, 0))

                def attend(t, L=L):
                    if not isinstance(t.v, int) or t.v + 2 < T:
                        if L == 0:
                            need(sp, x_in[t.par], 16 * (t.half + 1))
                            load_x(t.plus(2))
                        load_ctx(L, t.plus(2))
                    if not isinstance(t.v, int) or t.v + 1 < T:
                        load_stage(L, t.plus(1))
                tiles(sp, T, 1, 3, attend)
                sp.wait_ge(x_ok, T * (L + 1))
                if L == 0:
                    load_layer(1)
                if L == 1:
                    sp.wait_ge(scattered, 32 * T * 2)
                    sp.dma_start(b2, A["L1_ffn_b2"].rearrange("e d -> (e d)").partition_broadcast(P).rearrange("p (e d) -> p e d", e=8)).then_inc(b2_in, 16)
                s = ex[L]
                sp.wait_ge(scattered, 32 * T * (L + 1))
                if L == 0:
                    sp.wait_ge(sh_x, T)

                def load_rows(j, L=L, s=s):
                    need(sp, s["pe_rT"], j.v - 1)
                    src = xg[L].rearrange("(j p) d -> j p d", p=P)[bass.ds(j.v, 1)].rearrange("a p d -> (a p) d")
                    sp.dma_start(rows[j.par], src).then_inc(s[f"rows{j.par}"], 16)
                tiles(sp, SLOT_TILES[L], 2, 0, load_rows)

            def store(t):
                n = t.plus(T)
                need(sp, cx_ok, n.v + 1)
                sp.dma_start(out[bass.ds(t.v, 1)].rearrange("a p d -> (a p) d"), at(x, t.v)).then_inc(stored[t.par], 16)
            tiles(sp, T, 0, 0, store)
            for s in stored:
                sp.wait_ge(s, 16 * T // 2)

        @block.gpsimd
        def _(pool):
            gate = Gate(pool, gate_sem["pool"])
            pool.memset(zeros, 0.0).then_inc(zero_set, 1)
            pool.memset(mhalf[:], -0.5).then_inc(half_set, 1)
            pool.wait_ge(half_set, 1)

            def power(n):
                need(pool, ve_ok, n.v + 1)
                pool.tensor_tensor(rstd[:], vareps[:], mhalf[:], ALU.pow).then_inc(rstd_ok, 1)

            def keys1(L, t):
                n = t.plus(T * L)
                need(pool, k_ok, n.v + 1)
                need(pool, pe_s, 4 * n.v)
                pool.tensor_tensor(kbd[:, 1, :, :], kT[:, P:2 * P].unsqueeze(1).to_broadcast([P, 8, P]),
                                   headrow.unsqueeze(2).to_broadcast([P, 8, P]), ALU.mult).then_inc(kbd1_ok, 1)

            def split_lo(L, t):
                n = t.plus(T * L)
                gate((hi_ok, n.v + 1))
                pool.tensor_tensor(at(wlo[L], t.v), stage[:, 0:SLAB[L]], at(whi[L], t.v), ALU.subtract).then_inc(lo_ok, 1)

            pool.wait_ge(const_in, 16 * SMALL)
            for L in range(2):
                if L:
                    pool.wait_ge(cx_ok, T)
                power(Tile(0, 32 * L))
                keys1(L, Tile(0, 0))
                power(Tile(0, 32 * L + 1))

                def attend(t, L=L):
                    more = not isinstance(t.v, int)
                    if more or t.v + 1 < T:
                        keys1(L, t.plus(1))
                    if more or t.v + 2 < T:
                        power(t.plus(32 * L + 2))
                    split_lo(L, t)
                tiles(pool, T, 1, 3, attend, gate)

                pool.wait_ge(x_ok, T * (L + 1))
                if L == 0:
                    pool.wait_ge(sws_ok, 1)
                    pool.tensor_tensor(slo, sstage, shi, ALU.subtract).then_inc(sws_ok, 1)
                power(Tile(0, 32 * L + 16))

                def route(t, L=L):
                    n = t.plus(T * L)
                    if not isinstance(t.v, int) or t.v + 1 < T:
                        power(t.plus(32 * L + 17))
                    gate((xshi_ok, n.v + 1))
                    pool.tensor_tensor(at(xs, t.v)[:, D:2 * D], xn[t.par], at(xs, t.v)[:, 0:D], ALU.subtract).then_inc(xs_ok, 1)
                tiles(pool, T, 1, 1, route, gate)

                pool.wait_ge(slot_ok, L + 1)
                pool.wait_ge(xs_ok, T * (L + 1))
                pool.wait_ge(zero_out, 16 * ZERO_DMAS)
                for t in range(T):
                    for c in range(2):
                        pool.indirect_dma_start(xg[L], bass.IndirectOffsetOnAxis(ap=slot[:, c, t:t + 1], axis=0),
                                                xs[:, t, :], None).then_inc(scattered, 16)

                s = ex[L]

                def store_y(j, L=L, s=s):
                    gate((s["y"], j.v + 1))
                    dst = y[L].rearrange("(j p) d -> j p d", p=P)[bass.ds(j.v, 1)].rearrange("a p d -> (a p) d")
                    pool.dma_start(dst, yrow[j.par]).then_inc(s[f"out{j.par}"], 16)
                tiles(pool, SLOT_TILES[L], 0, 0, store_y, gate)
                for o in range(2):
                    pool.wait_ge(s[f"out{o}"], 16 * SLOT_TILES[L] // 2)

                for t in range(T):
                    need(pool, cx_ok, T * L + t - 1 if t >= 2 else 0)
                    for c in range(2):
                        pool.indirect_dma_start(ygot[t % 2][c], None, y[L],
                                                bass.IndirectOffsetOnAxis(ap=slot[:, c, t:t + 1], axis=0)).then_inc(got[L][t % 2], 16)
            gate.close()

        @block.scalar
        def _(act):
            gate = Gate(act, gate_sem["act"])

            def turned_x(n):
                need(act, pe_T, n.v + 1)

            def keys(L, t):
                n = t.plus(T * L)
                need(act, pe_k, n.v + 1)
                need(act, kbd0_ok, n.v)
                need(act, kbd1_ok, n.v)
                for m in range(KT):
                    i = act.activation(kT[:, m * P:(m + 1) * P], bank[6][:, m * P:(m + 1) * P], ACT.Identity,
                                       bias=bqk[:, L, 1, m:m + 1])
                i.then_inc(k_ok, 1)

            def queries(L, t):
                n = t.plus(T * L)
                need(act, pe_q, n.v + 1)
                need(act, pe_s, 4 * n.v - 4)
                for m in range(KT):
                    i = act.activation(qT[t.par][:, m * P:(m + 1) * P], bank[6][:, m * P:(m + 1) * P], ACT.Identity,
                                       bias=bqk[:, L, 0, m:m + 1])
                i.then_inc(q_ok, 1)

            def xnT_copy(L, t):
                n, m = t.plus(T * L), t.plus(32 * L)
                need(act, pe_T, m.v + 1)
                need(act, pe_q, n.v - 1)
                act.activation(xnT[t.par], bank[5][:, 0:KT * P], ACT.Copy).then_inc(xnT_ok, 1)

            def exps(L, t, g):
                n = t.plus(T * L)
                waits = ((sc_ok, 4 * n.v + g + 1), (pe_pt, 4 * n.v + g - 1))
                if L == 0:
                    for w in waits:
                        need(act, *w)
                    scale = 1.0 / 4
                else:
                    gate(*waits)
                    scale = qscale[:, bass.ds(t.v, 1)]
                act.activation(prob[g % 2], shifted[g % 2], ACT.Exp, scale=scale).then_inc(exp_ok, 1)

            def probT_copy(L, t, g):
                n = t.plus(T * L)
                need(act, pe_pt, 4 * n.v + g + 1)
                need(act, pe_pv, 4 * n.v + g - 1)
                act.activation(probT[g % 2], bank[2 + g % 2][:], ACT.Copy).then_inc(pt_ok, 1)

            def oT_copy(L, t):
                n = t.plus(T * L)
                need(act, pe_oT, n.v + 1)
                need(act, pe_o, n.v)
                act.activation(oT, bank[5][:, 0:KT * P], ACT.Copy).then_inc(oT_ok, 1)

            def split_hi(L, t):
                n = t.plus(T * L)
                gate((stage_in, 16 * (n.v + 1)))
                act.activation(at(whi[L], t.v), stage[:, 0:SLAB[L]], ACT.Copy).then_inc(hi_ok, 1)

            act.wait_ge(const_in, 16 * SMALL)
            act.activation(cb[:], cb32, ACT.Copy).then_inc(cb_ok, 1)
            act.activation(tgate[:], gates[:], ACT.Tanh).then_inc(set_ok, 1)
            for L in range(2):
                xnT_copy(L, Tile(0, 0))
                keys(L, Tile(0, 0))
                queries(L, Tile(0, 0))

                def attend(t, L=L):
                    more = not isinstance(t.v, int)
                    before, after = more or t.v > 0, more or t.v + 1 < T
                    if before:
                        probT_copy(L, t.plus(-1), 3)
                    if after:
                        xnT_copy(L, t.plus(1))
                    exps(L, t, 0)
                    probT_copy(L, t, 0)
                    if after:
                        keys(L, t.plus(1))
                    exps(L, t, 1)
                    probT_copy(L, t, 1)
                    if before:
                        oT_copy(L, t.plus(-1))
                    exps(L, t, 2)
                    probT_copy(L, t, 2)
                    if after:
                        queries(L, t.plus(1))
                    exps(L, t, 3)
                    split_hi(L, t)
                tiles(act, T, 1, 3, attend, gate)
                probT_copy(L, Tile(0, T - 1), 3)
                oT_copy(L, Tile(0, T - 1))
                act.wait_ge(x_ok, T * (L + 1))

                if L == 0:
                    act.wait_ge(sw_in, 16)
                    act.activation(shi, sstage, ACT.Copy).then_inc(sws_ok, 1)

                def route(t, L=L):
                    n, m = t.plus(T * L), t.plus(32 * L + 16)
                    need(act, pe_T, m.v + 1)
                    need(act, pe_lg, n.v - 1)
                    if L == 0:
                        need(act, xt_ok, t.v - 1)
                    act.activation(xnT[t.par], bank[t.par][:, 0:KT * P], ACT.Copy).then_inc(xnT_ok, 1)
                    if L == 0:
                        gate((xnT_ok, m.v + 1))
                        act.activation(at(xT, t.v)[:, 0:KT * P], xnT[t.par], ACT.Copy).then_inc(xthi_ok, 1)
                    act.activation(at(xs, t.v)[:, 0:D], xn[t.par], ACT.Copy).then_inc(xshi_ok, 1)
                tiles(act, T, 2, 0, route, gate)
                act.wait_ge(m_ok, 2 * L + 1)
                if L == 0:
                    act.activation(rtmp[1], rtmp[0], ACT.Exp).then_inc(expo_ok, 1)
                else:
                    act.activation(rsmall[:, 2 * T:3 * T], rsmall[:, T:2 * T], ACT.Exp).then_inc(expo_ok, 1)

                def shared(t):
                    need(act, sh_up, t.v + 1)
                    need(act, sh_h, t.v - 1)
                    act.activation(sh_act[t.par], bank[t.par][:, 2 * P:4 * P], ACT.Silu).then_inc(sh_sig, 1)
                    need(act, sh_h, t.v + 1)
                    need(act, sh_dn, t.v - 1)
                    act.activation(sh_hhi[t.par], sh_hid[t.par], ACT.Copy).then_inc(sh_hi, 1)
                if L == 0:
                    tiles(act, T, 2, 0, shared)

                s = ex[L]

                def turn(j, s=s):
                    need(act, s["pe_rT"], j.v + 1)
                    need(act, s["up"], j.v - 1)
                    act.activation(rowsT[j.par], bank[j.par][:, 0:2 * P].bitcast(BF16), ACT.Copy).then_inc(s["rT"], 1)

                def expert0(j, s=s):
                    if not isinstance(j.v, int) or j.v + 1 < SLOT_TILES[0]:
                        turn(j.plus(1))
                    need(act, s["up"], j.v + 1)
                    need(act, s["h"], j.v - 1)
                    act.activation(sig[j.par], bank[2 + j.par][:, P:2 * P], ACT.Silu).then_inc(s["sig"], 1)
                    need(act, s["h"], j.v + 1)
                    need(act, s["dn"], j.v - 1)
                    act.activation(hid_hi[j.par][:, 0:F0], hid[j.par][:, 0:F0], ACT.Copy).then_inc(s["hi"], 1)

                def expert1(j, s=s):
                    if not isinstance(j.v, int) or j.v + 1 < SLOT_TILES[1]:
                        turn(j.plus(1))
                    e = act.value_load(tile_expert[0:1, bass.ds(j.v, 1)], min_val=0, max_val=7)
                    gate((s["upb"], j.v + 1), (s["lo"], j.v - 1))
                    for m in range(4):
                        i = act.activation(hid[j.par][:, (4 + m) * P:(5 + m) * P], bank[3 + 2 * j.par][:, m * P:(m + 1) * P],
                                           ACT.Relu, bias=b1[:, bass.ds(e * 8 + (4 + m), 1)])
                    i.then_inc(s["ha"], 1)
                    need(act, s["ha"], j.v + 1)
                    need(act, s["h"], j.v + 1)
                    need(act, s["dn"], j.v - 1)
                    act.activation(hid_hi[j.par], hid[j.par], ACT.Copy).then_inc(s["hi"], 1)

                act.wait_ge(slot_ok, L + 1)
                turn(Tile(0, 0))
                tiles(act, SLOT_TILES[L], 2, 2, expert1 if L else expert0, gate)
                act.wait_ge(cx_ok, T * (L + 1))
            gate.close()

        @block.vector
        def _(dve):
            gate = Gate(dve, gate_sem["dve"])
            links = [0]

            def link(i):
                links[0] += 1
                i.then_inc(dve_link, 1)
                dve.wait_ge(dve_link, links[0])

            def moments(m, t, *waits):
                gate(*waits)
                dve.bn_stats(stats[:], at(x, t.v)).then_inc(st_ok, 1)
                gate((st_ok, m.v + 1))
                dve.bn_aggr(meanvar[:], stats[:]).then_inc(mv_ok, 1)
                need(dve, mv_ok, m.v + 1)
                dve.tensor_scalar(vareps[:], meanvar[:, 1:2], EPS, None, ALU.add).then_inc(ve_ok, 1)

            def normalise(m, t, *waits):
                need(dve, rstd_ok, m.v + 1)
                need(dve, pe_T, m.v - 1)
                for w in waits:
                    need(dve, *w)
                dve.tensor_scalar(xn[t.par], at(x, t.v), meanvar[:, 0:1], rstd[:], ALU.subtract, ALU.mult).then_inc(xn_ok, 1)

            def scores(L, t, g):
                n = t.plus(T * L)
                k = 4 * n.v + g
                s = bank[g % 2][:].rearrange("p (h t) -> p h t", h=GH)
                need(dve, pe_s, k + 1)
                dve.tensor_reduce(rowmax[g % 2], s, AX.X, ALU.max).then_inc(mx_ok, 1)
                need(dve, mx_ok, k + 1)
                need(dve, exp_ok, k - 1)
                dve.tensor_tensor(shifted[g % 2].rearrange("p (h t) -> p h t", h=GH), s,
                                  rowmax[g % 2].unsqueeze(2).to_broadcast([P, GH, P]), ALU.subtract).then_inc(sc_ok, 1)

            def keys0(L, t):
                n = t.plus(T * L)
                need(dve, k_ok, n.v + 1)
                need(dve, pe_s, 4 * n.v - 2)
                for h in range(8):
                    i = dve.tensor_scalar(kbd[:, 0, h, :], kT[:, 0:P], headrow[:, h:h + 1], None, ALU.mult)
                i.then_inc(kbd0_ok, 1)

            def values(L, t):
                n = t.plus(T * L)
                need(dve, pe_v, n.v + 1)
                need(dve, pe_pv, 4 * n.v - 4)
                dve.tensor_tensor(vaug[t.par][:, :, 0:HD], bank[7][:, 0:D].rearrange("p (h w) -> p h w", h=H),
                                  bvo[:, 0, :].rearrange("p (h w) -> p h w", h=H), ALU.add).then_inc(v_ok, 1)

            def divide(L, t):
                n = t.plus(T * L)
                o = bank[4][:, 0:H * VW].rearrange("p (h w) -> p h w", h=H)
                need(dve, pe_pv, 4 * n.v + 4)
                dve.reciprocal(rsum.unsqueeze(2), o[:, :, HD:VW]).then_inc(rs_ok, 1)
                need(dve, rs_ok, n.v + 1)
                need(dve, pe_oT, n.v)
                dve.tensor_tensor(on.rearrange("p (h w) -> p h w", h=H), o[:, :, 0:HD],
                                  rsum.unsqueeze(2).to_broadcast([P, H, HD]), ALU.mult).then_inc(o_ok, 1)

            def residual(L, t):
                n = t.plus(T * L)
                need(dve, pe_o, n.v + 1)
                dve.tensor_tensor(proj, bank[7][:, 0:D], bvo[:, 1, :], ALU.add).then_inc(t_ok, 1)
                need(dve, t_ok, n.v + 1)
                dve.scalar_tensor_tensor(out=at(x, t.v), in0=proj, scalar=tgate[:, L:L + 1], in1=at(x, t.v),
                                         op0=ALU.mult, op1=ALU.add).then_inc(x_ok, 1)

            dve.wait_ge(const_in, 16 * SMALL)
            dve.wait_ge(set_ok, 1)
            link(dve.tensor_scalar(qscale[:], qmask[:], 0.0, 0.25, ALU.not_equal, ALU.mult))
            for L in range(2):
                def loaded(t, L=L):
                    return ((x_in[t.par], 16 * (t.half + 1)),) if L == 0 else ()

                for i in range(2):
                    dve.memset(vaug[i][:, :, HD:VW], 1.0).then_inc(ones_ok, 1)
                t0, t1 = Tile(0, 0), Tile(0, 1)
                moments(t0.plus(32 * L), t0, *loaded(t0))
                normalise(t0.plus(32 * L), t0)
                if L == 0:
                    dve.wait_ge(bv_in, 32)
                keys0(L, t0)
                values(L, t0)
                moments(t1.plus(32 * L), t1, *loaded(t1))
                normalise(t1.plus(32 * L), t1)

                def attend(t, L=L, loaded=loaded):
                    more = not isinstance(t.v, int)
                    before, after, after2 = more or t.v > 0, more or t.v + 1 < T, more or t.v + 2 < T
                    scores(L, t, 0)
                    if after:
                        values(L, t.plus(1))
                    if before:
                        divide(L, t.plus(-1))
                    scores(L, t, 1)
                    if after:
                        keys0(L, t.plus(1))
                    scores(L, t, 2)
                    if after2:
                        moments(t.plus(32 * L + 2), t.plus(2), *loaded(t.plus(2)))
                    scores(L, t, 3)
                    if before:
                        residual(L, t.plus(-1))
                    if after2:
                        normalise(t.plus(32 * L + 2), t.plus(2))
                tiles(dve, T, 1, 3, attend, gate)
                divide(L, Tile(0, T - 1))
                residual(L, Tile(0, T - 1))
                dve.wait_ge(x_ok, T * (L + 1))

                base = 32 * L + 16
                moments(t0.plus(base), t0)
                normalise(t0.plus(base), t0)
                E = EXPERTS[L]
                lg = logit[:, 0:T * E].rearrange("p (t e) -> p t e", t=T)

                def route(t, L=L, base=base, E=E, lg=lg):
                    n = t.plus(T * L)
                    after = not isinstance(t.v, int) or t.v + 1 < T
                    if after:
                        moments(t.plus(base + 1), t.plus(1))
                        normalise(t.plus(base + 1), t.plus(1), (xs_ok, n.v))
                    if L == 0:
                        need(dve, xthi_ok, t.v + 1)
                        need(dve, xnT_ok, t.plus(base).v + 1)
                        dve.tensor_tensor(at(xT, t.v)[:, KT * P:], xnT[t.par], at(xT, t.v)[:, 0:KT * P],
                                          ALU.subtract).then_inc(xt_ok, 1)
                    need(dve, pe_lg, n.v + 1)
                    if L == 0:
                        dve.tensor_scalar(at(lg, t.v), bank[2 + t.par][:, 0:E], 0.0, None, ALU.add).then_inc(lg_ok, 1)
                    else:
                        dve.tensor_tensor(at(lg, t.v), bank[2 + t.par][:, 0:E], rb[:], ALU.add).then_inc(lg_ok, 1)
                tiles(dve, T, 1, 1, route, gate)

                dve.wait_ge(lg_ok, T * (L + 1))

                def te(v, E=E):
                    return v[:, 0:T * E].rearrange("p (t e) -> p t e", t=T)

                def over_e(v, E=E):
                    return v.unsqueeze(2).to_broadcast([P, T, E])

                def over_t(v, E=E):
                    return v.unsqueeze(1).to_broadcast([P, T, E])

                small = [rsmall[:, i * T:(i + 1) * T] for i in range(16)]
                score, oh1, oh2, tmp = te(rtmp[2]), te(rtmp[3]), te(rtmp[4]), te(rtmp[5])
                both = te(rtmp[0].bitcast(BF16))
                if L == 0:
                    link(dve.tensor_reduce(small[0], lg, AX.X, ALU.max))
                    dve.tensor_tensor(te(rtmp[0]), lg, over_e(small[0]), ALU.subtract).then_inc(m_ok, 1)
                    dve.wait_ge(expo_ok, 1)
                    link(dve.tensor_reduce(small[0], te(rtmp[1]), AX.X, ALU.add))
                    link(dve.reciprocal(small[1], small[0]))
                    link(dve.tensor_tensor(score, te(rtmp[1]), over_e(small[1]), ALU.mult))
                else:
                    score = lg
                best = (small[4], small[5])
                for c, oh in enumerate((oh1, oh2)):
                    link(dve.tensor_reduce(best[c], score, AX.X, ALU.max))
                    link(dve.tensor_tensor(tmp, score, over_e(best[c]), ALU.is_equal))
                    link(dve.tensor_tensor(tmp, tmp, over_t(rev[L]), ALU.mult))
                    link(dve.tensor_reduce(small[6], tmp, AX.X, ALU.max))
                    link(dve.tensor_tensor(oh, over_e(small[6]), over_t(rev[L]), ALU.is_equal))
                    if c == 0:
                        link(dve.scalar_tensor_tensor(out=te(rtmp[2]), in0=oh1, scalar=-3e38, in1=score,
                                                      op0=ALU.mult, op1=ALU.add))
                        score = te(rtmp[2])
                if L == 1:
                    dve.tensor_tensor(small[1], best[1], best[0], ALU.subtract).then_inc(m_ok, 1)
                link(dve.tensor_tensor(both, oh1, oh2, ALU.add))
                dve.tensor_scalar(small[6], small[6], 1.0, None, ALU.mult).then_inc(m_ok, 1)
                if L == 0:
                    for c in range(2):
                        dve.tensor_scalar(gsel[:, c, :], best[c], tgate[:, 2:3], None, ALU.mult)
                else:
                    dve.wait_ge(expo_ok, 2)
                    link(dve.tensor_scalar(small[3], small[2], 1.0, None, ALU.add))
                    link(dve.reciprocal(small[3], small[3]))
                    link(dve.tensor_scalar(gsel[:, 0, :], small[3], tgate[:, 3:4], None, ALU.mult))
                    dve.tensor_tensor(gsel[:, 1, :], gsel[:, 0, :], small[2], ALU.mult)
                dve.wait_ge(pe_rank, 2 * L + 2)
                count, whole = small[8][:, 0:E], small[9].bitcast(I32)[:, 0:E]
                link(dve.tensor_scalar(whole, bank[5][:, 0:E], float(P - 1), None, ALU.add))
                link(dve.tensor_scalar(whole, whole, 7, 7, ALU.logical_shift_right, ALU.logical_shift_left))
                ends = [small[10][:, 0:E], small[11][:, 0:E]]
                link(dve.tensor_copy(count, whole))
                link(dve.tensor_copy(ends[0], whole))
                step, a = 1, 0
                while step < E:
                    dve.tensor_copy(ends[1 - a][:, 0:step], ends[a][:, 0:step])
                    link(dve.tensor_tensor(ends[1 - a][:, step:E], ends[a][:, step:E], ends[a][:, 0:E - step], ALU.add))
                    step, a = 2 * step, 1 - a
                first = small[12][:, 0:E]
                link(dve.tensor_tensor(first, ends[a], count, ALU.subtract))
                link(dve.tensor_tensor(tmp, bank[4][:, 0:T * E].rearrange("p (t e) -> p t e", t=T), over_t(first), ALU.add))
                for c, oh in enumerate((oh1, oh2)):
                    link(dve.tensor_tensor(oh, oh, tmp, ALU.mult))
                    link(dve.tensor_reduce(small[13 + c], oh, AX.X, ALU.add))
                    link(dve.tensor_copy(slot[:, c, :], small[13 + c]))
                nj = SLOT_TILES[L]
                cmp = work[:, shared_cols + T * D + T * 16:][:, 0:nj * E].rearrange("p (j e) -> p j e", j=nj)
                link(dve.tensor_tensor(cmp, starts[:, 0:nj].unsqueeze(2).to_broadcast([P, nj, E]),
                                       ends[a].unsqueeze(1).to_broadcast([P, nj, E]), ALU.is_ge))
                te_f = rtmp[5][:, 0:nj]
                link(dve.tensor_reduce(te_f, cmp, AX.X, ALU.add))
                dve.tensor_scalar(tile_expert[:, 0:nj], te_f, float(E - 1), None, ALU.min).then_inc(slot_ok, 1)

                def shared_h(t):
                    need(dve, sh_sig, t.v + 1)
                    need(dve, sh_lo, t.v - 1)
                    dve.tensor_tensor(sh_hid[t.par], bank[t.par][:, 0:2 * P], sh_act[t.par], ALU.mult).then_inc(sh_h, 1)
                    need(dve, sh_hi, t.v + 1)
                    dve.tensor_tensor(sh_hlo[t.par], sh_hid[t.par], sh_hhi[t.par], ALU.subtract).then_inc(sh_lo, 1)

                def shared_x(t):
                    need(dve, sh_dn, t.v + 1)
                    dve.scalar_tensor_tensor(out=at(x, t.v), in0=bank[2 + t.par][:, 0:D], scalar=tgate[:, 2:3],
                                             in1=at(x, t.v), op0=ALU.mult, op1=ALU.add).then_inc(sh_x, 1)

                def shared(t):
                    shared_h(t)
                    if not isinstance(t.v, int) or t.v > 0:
                        shared_x(t.plus(-1))
                if L == 0:
                    tiles(dve, T, 2, 0, shared)
                    shared_x(Tile(0, T - 1))

                s = ex[L]

                def result(j, L=L, s=s):
                    if L:
                        e = dve.value_load(tile_expert[0:1, bass.ds(j.v, 1)], min_val=0, max_val=7)
                    need(dve, s["dn"], j.v + 1)
                    need(dve, s[f"out{j.par}"], 16 * j.half)
                    if L == 0:
                        dve.tensor_copy(yrow[j.par], bank[6 + j.par][:, 0:D]).then_inc(s["y"], 1)
                    else:
                        dve.tensor_tensor(yrow[j.par], bank[6 + j.par][:, 0:D], at(b2, e), ALU.add).then_inc(s["y"], 1)

                def expert0(j, s=s, result=result):
                    need(dve, s["sig"], j.v + 1)
                    need(dve, s["lo"], j.v - 1)
                    dve.tensor_tensor(hid[j.par][:, 0:F0], bank[2 + j.par][:, 0:P], sig[j.par], ALU.mult).then_inc(s["h"], 1)
                    need(dve, s["hi"], j.v + 1)
                    dve.tensor_tensor(hid_lo[j.par][:, 0:F0], hid[j.par][:, 0:F0], hid_hi[j.par][:, 0:F0],
                                      ALU.subtract).then_inc(s["lo"], 1)
                    if not isinstance(j.v, int) or j.v > 0:
                        result(j.plus(-1))

                def expert1(j, s=s, result=result):
                    e = dve.value_load(tile_expert[0:1, bass.ds(j.v, 1)], min_val=0, max_val=7)
                    need(dve, s["up"], j.v + 1)
                    need(dve, s["lo"], j.v - 1)
                    for m in range(4):
                        i = dve.tensor_scalar(hid[j.par][:, m * P:(m + 1) * P], bank[2 + 2 * j.par][:, m * P:(m + 1) * P],
                                              b1[:, bass.ds(e * 8 + m, 1)], 0.0, ALU.add, ALU.max)
                    i.then_inc(s["h"], 1)
                    if not isinstance(j.v, int) or j.v > 0:
                        result(j.plus(-1))
                    need(dve, s["hi"], j.v + 1)
                    dve.tensor_tensor(hid_lo[j.par], hid[j.par], hid_hi[j.par], ALU.subtract).then_inc(s["lo"], 1)

                dve.wait_ge(slot_ok, L + 1)
                if L == 1:
                    dve.wait_ge(b2_in, 16)
                tiles(dve, SLOT_TILES[L], 2, 0, expert1 if L else expert0, gate)
                result(Tile(0, SLOT_TILES[L] - 1))

                def combine(t, L=L):
                    n = t.plus(T * L)
                    need(dve, got[L][t.par], 32 * (t.half + 1))
                    for c, done in enumerate((half_ok, cx_ok)):
                        dve.scalar_tensor_tensor(out=at(x, t.v), in0=ygot[t.par][c], scalar=gsel[:, c, bass.ds(t.v, 1)],
                                                 in1=at(x, t.v), op0=ALU.mult, op1=ALU.add).then_inc(done, 1)
                        if c == 0:
                            need(dve, half_ok, n.v + 1)
                tiles(dve, T, 0, 0, combine)
                dve.wait_ge(cx_ok, T * (L + 1))
            gate.close()

        @block.tensor
        def _(pe):
            gate = Gate(pe, gate_sem["pe"])

            def turn_x(m, t, to):
                need(pe, xn_ok, m.v + 1)
                for k in range(KT):
                    i = pe.transpose(to[:, k * P:(k + 1) * P], xn[t.par][:, k * P:(k + 1) * P], ident)
                i.then_inc(pe_T, 1)

            def proj_k(L, t):
                n = t.plus(T * L)
                need(pe, ctx_in[t.par], 16 * (n.half + 1))
                need(pe, q_ok, n.v)
                for m in range(KT):
                    for k in range(KT):
                        i = pe.matmul(bank[6][:, m * P:(m + 1) * P], wat[:, 1, k, m * P:(m + 1) * P],
                                      ctxT[t.par][:, k * P:(k + 1) * P], start=(k == 0), stop=(k == KT - 1))
                i.then_inc(pe_k, 1)

            def proj_v(L, t):
                n = t.plus(T * L)
                need(pe, ctx_in[t.par], 16 * (n.half + 1))
                need(pe, x_ok, n.v - 2)
                for k in range(KT):
                    i = pe.matmul(bank[7][:, 0:D], ctxT[t.par][:, k * P:(k + 1) * P], wat[:, 2, k, :],
                                  start=(k == 0), stop=(k == KT - 1))
                i.then_inc(pe_v, 1)

            def proj_q(L, t):
                n, m_ = t.plus(T * L), t.plus(32 * L)
                need(pe, xnT_ok, m_.v + 1)
                need(pe, k_ok, n.v + 1)
                for m in range(KT):
                    for k in range(KT):
                        i = pe.matmul(bank[6][:, m * P:(m + 1) * P], wat[:, 0, k, m * P:(m + 1) * P],
                                      xnT[t.par][:, k * P:(k + 1) * P], start=(k == 0), stop=(k == KT - 1))
                i.then_inc(pe_q, 1)

            def score(L, t, g):
                n = t.plus(T * L)
                m = g // 2
                need(pe, q_ok, n.v + 1)
                need(pe, kbd1_ok if m else kbd0_ok, n.v + 1)
                need(pe, sc_ok, 4 * n.v + g - 1)
                i = pe.matmul(bank[g % 2][:], qT[t.par][:, m * P:(m + 1) * P],
                              kbd[:, m, 4 * (g % 2):4 * (g % 2) + 4, :].rearrange("p h t -> p (h t)"),
                              start=True, stop=(L == 1))
                if L == 0:
                    i = pe.matmul(bank[g % 2][:], identb, causal, start=False, stop=True)
                i.then_inc(pe_s, 1)

            def turn_p(L, t, g):
                n = t.plus(T * L)
                need(pe, exp_ok, 4 * n.v + g + 1)
                need(pe, pt_ok, 4 * n.v + g - 1)
                for h in range(GH):
                    i = pe.transpose(bank[2 + g % 2][:, h * P:(h + 1) * P], prob[g % 2][:, h * P:(h + 1) * P], ident)
                i.then_inc(pe_pt, 1)

            def weigh_v(L, t, g):
                n = t.plus(T * L)
                need(pe, pt_ok, 4 * n.v + g + 1)
                if g == 0:
                    need(pe, v_ok, n.v + 1)
                    need(pe, o_ok, n.v)
                for h in range(GH):
                    c = (GH * g + h) * VW
                    i = pe.matmul(bank[4][:, c:c + VW], probT[g % 2][:, h * P:(h + 1) * P], vaug[t.par][:, GH * g + h, :],
                                  start=True, stop=True)
                i.then_inc(pe_pv, 1)

            def turn_o(L, t, last):
                n = t.plus(T * L)
                need(pe, o_ok, n.v + 1)
                if last:
                    need(pe, oT_ok, n.v)
                else:
                    m_ = t.plus(32 * L)
                    need(pe, xnT_ok, m_.plus(3).v if not isinstance(t.v, int) or t.v + 2 < T else 32 * L + T)
                for k in range(KT):
                    i = pe.transpose(bank[5][:, k * P:(k + 1) * P], on[:, k * P:(k + 1) * P], ident)
                i.then_inc(pe_oT, 1)

            def proj_o(L, t, last):
                n = t.plus(T * L)
                need(pe, oT_ok, n.v + 1)
                if last:
                    need(pe, x_ok, n.v)
                else:
                    need(pe, v_ok, n.v + 3 if not isinstance(t.v, int) or t.v + 2 < T else T * (L + 1))
                for k in range(KT):
                    i = pe.matmul(bank[7][:, 0:D], oT[:, k * P:(k + 1) * P], wat[:, 3, k, :],
                                  start=(k == 0), stop=(k == KT - 1))
                i.then_inc(pe_o, 1)

            pe.wait_ge(const_in, 16 * SMALL)
            pe.wait_ge(cb_ok, 1)
            for L in range(2):
                pe.wait_ge(wat_in, 16 * (L + 1))
                pe.wait_ge(ones_ok, 2 * (L + 1))
                t0 = Tile(0, 0)
                turn_x(Tile(0, 32 * L), t0, bank[5])
                proj_k(L, t0)
                proj_v(L, t0)
                proj_q(L, t0)

                def attend(t, L=L):
                    more = not isinstance(t.v, int)
                    before, after = more or t.v > 0, more or t.v + 1 < T
                    score(L, t, 0)
                    if before:
                        turn_p(L, t.plus(-1), 3)
                    if after:
                        need(pe, oT_ok, t.plus(T * L - 1).v)
                        if isinstance(t.v, int) and t.v == 0:
                            need(pe, xnT_ok, 32 * L + 1)
                        turn_x(t.plus(32 * L + 1), t.plus(1), bank[5])
                        proj_v(L, t.plus(1))
                    if before:
                        weigh_v(L, t.plus(-1), 3)
                    score(L, t, 1)
                    turn_p(L, t, 0)
                    if after:
                        proj_k(L, t.plus(1))
                    weigh_v(L, t, 0)
                    score(L, t, 2)
                    turn_p(L, t, 1)
                    if before:
                        turn_o(L, t.plus(-1), False)
                    if after:
                        proj_q(L, t.plus(1))
                    weigh_v(L, t, 1)
                    score(L, t, 3)
                    turn_p(L, t, 2)
                    if before:
                        proj_o(L, t.plus(-1), False)
                    weigh_v(L, t, 2)
                tiles(pe, T, 1, 3, attend)
                last = Tile(0, T - 1)
                turn_p(L, last, 3)
                weigh_v(L, last, 3)
                turn_o(L, last, True)
                proj_o(L, last, True)
                pe.wait_ge(x_ok, T * (L + 1))

                E, e0 = EXPERTS[L], 16 * L

                def turn(t, L=L):
                    m_ = t.plus(32 * L + 16)
                    need(pe, xnT_ok, m_.v - 1)
                    turn_x(m_, t, bank[t.par])

                def route(t, L=L, E=E, e0=e0):
                    n = t.plus(T * L)
                    if not isinstance(t.v, int) or t.v + 1 < T:
                        turn(t.plus(1))
                    need(pe, xnT_ok, t.plus(32 * L + 16).v + 1)
                    need(pe, lg_ok, n.v - 1)
                    for k in range(KT):
                        i = pe.matmul(bank[2 + t.par][:, 0:E], xnT[t.par][:, k * P:(k + 1) * P], wr[:, k, e0:e0 + E],
                                      start=(k == 0), stop=(k == KT - 1))
                    i.then_inc(pe_lg, 1)
                turn(t0)
                tiles(pe, T, 1, 1, route)
                pe.wait_ge(m_ok, 2 * L + 2)
                both = rtmp[0].bitcast(BF16)[:, 0:T * E]
                for d in range(1, T):
                    pe.matmul(bank[4][:, d * E:T * E], onesb, both[:, 0:(T - d) * E], start=(d == 1), stop=False,
                              skip_group_check=True)
                i = pe.matmul(bank[4][:, 0:T * E], earlier, both, start=False, stop=True, skip_group_check=True)
                i.then_inc(pe_rank, 1)
                for t in range(T):
                    i = pe.matmul(bank[5][:, 0:E], onesb, both[:, t * E:(t + 1) * E], start=(t == 0), stop=(t == T - 1))
                i.then_inc(pe_rank, 1)

                w1h, w1l = (w[:, 0:KT * 2 * FS].rearrange("p (k f) -> p k f", k=KT) for w in (shi, slo))
                w2h, w2l = (w[:, KT * 2 * FS:].rearrange("p (k f) -> p k f", k=KT) for w in (shi, slo))

                def shared_down(t):
                    need(pe, sh_lo, t.v + 1)
                    need(pe, sh_x, t.v - 1)
                    for k in range(KT):
                        f = slice(k * P, (k + 1) * P)
                        for q, (a, b) in enumerate(((sh_hhi, w2h), (sh_hlo, w2h), (sh_hhi, w2l))):
                            i = pe.matmul(bank[2 + t.par][:, 0:D], a[t.par][:, f], b[:, k, :],
                                          start=(k == 0 and q == 0), stop=(k == KT - 1 and q == 2))
                    i.then_inc(sh_dn, 1)

                def shared(t):
                    need(pe, sh_h, t.v - 1)
                    xt = at(xT, t.v)
                    for m in range(4):
                        for k in range(KT):
                            hi, lo = xt[:, k * P:(k + 1) * P], xt[:, (KT + k) * P:(KT + k + 1) * P]
                            f = slice(m * P, (m + 1) * P)
                            for q, (w, v) in enumerate(((w1h, hi), (w1h, lo), (w1l, hi))):
                                i = pe.matmul(bank[t.par][:, m * P:(m + 1) * P], w[:, k, f], v,
                                              start=(k == 0 and q == 0), stop=(k == KT - 1 and q == 2))
                    i.then_inc(sh_up, 1)
                    if not isinstance(t.v, int) or t.v > 0:
                        shared_down(t.plus(-1))
                if L == 0:
                    pe.wait_ge(sws_ok, 2)
                    pe.wait_ge(slot_ok, 1)
                    tiles(pe, T, 2, 0, shared)
                    shared_down(Tile(0, T - 1))
                    pe.wait_ge(sh_x, T)

                s = ex[L]
                pe.wait_ge(slot_ok, L + 1)

                def turn_rows(j, s=s):
                    need(pe, s[f"rows{j.par}"], 16 * (j.half + 1))
                    need(pe, s["rT"], j.v - 1)
                    to = bank[j.par][:, 0:2 * P].bitcast(BF16)
                    for c in range(4):
                        i = pe.transpose(to[:, c * P:(c + 1) * P], rows[j.par][:, c * P:(c + 1) * P], identb)
                    i.then_inc(s["pe_rT"], 1)

                def expert_of(j, L=L):
                    return pe.value_load(tile_expert[0:1, bass.ds(j.v, 1)], min_val=0, max_val=EXPERTS[L] - 1)

                def up(e, j, L, m, to):
                    for k in range(KT):
                        if L == 0:
                            slab, f = e, slice(k * 2 * F0 + m * P, k * 2 * F0 + (m + 1) * P)
                        else:
                            slab, f = e * 2 + k, slice(m * P, (m + 1) * P)
                        hi, lo = rowsT[j.par][:, k * P:(k + 1) * P], rowsT[j.par][:, (KT + k) * P:(KT + k + 1) * P]
                        for q, (w, v) in enumerate(((whi, hi), (whi, lo), (wlo, hi))):
                            i = pe.matmul(to, at(w[L], slab)[:, f], v, start=(k == 0 and q == 0),
                                          stop=(k == KT - 1 and q == 2))
                    return i

                def down(j, L=L, s=s):
                    e = expert_of(j)
                    gate((s["lo"], j.v + 1), (s["y"], j.v - 1))
                    nk = 1 if L == 0 else F1 // P
                    for k in range(nk):
                        if L == 0:
                            slab, f = e, slice(KT * 2 * F0, KT * 2 * F0 + D)
                        else:
                            slab, f = e * 2 + k // 4, slice(F1 + (k % 4) * D, F1 + (k % 4 + 1) * D)
                        for q, (a, w) in enumerate(((hid_hi, whi), (hid_lo, whi), (hid_hi, wlo))):
                            i = pe.matmul(bank[6 + j.par][:, 0:D], a[j.par][:, k * P:(k + 1) * P], at(w[L], slab)[:, f],
                                          start=(k == 0 and q == 0), stop=(k == nk - 1 and q == 2))
                    i.then_inc(s["dn"], 1)

                def expert(j, L=L, s=s, down=down):
                    more = not isinstance(j.v, int)
                    if more or j.v + 1 < SLOT_TILES[L]:
                        turn_rows(j.plus(1))
                    e = expert_of(j)
                    if L == 0:
                        gate((s["rT"], j.v + 1), (s["h"], j.v - 1))
                        for m in range(2):
                            i = up(e, j, 0, m, bank[2 + j.par][:, m * P:(m + 1) * P])
                        i.then_inc(s["up"], 1)
                    else:
                        gate((s["rT"], j.v + 1), (s["h"], j.v - 1))
                        for m in range(4):
                            i = up(e, j, 1, m, bank[2 + 2 * j.par][:, m * P:(m + 1) * P])
                        i.then_inc(s["up"], 1)
                        gate((s["ha"], j.v - 1))
                        for m in range(4):
                            i = up(e, j, 1, 4 + m, bank[3 + 2 * j.par][:, m * P:(m + 1) * P])
                        i.then_inc(s["upb"], 1)
                    if more or j.v > 0:
                        down(j.plus(-1))
                turn_rows(Tile(0, 0))
                tiles(pe, SLOT_TILES[L], 2, 2, expert, gate)
                down(Tile(0, SLOT_TILES[L] - 1))
                pe.wait_ge(cx_ok, T * (L + 1))
            gate.close()


SMALL = 9
ZERO_DMAS = sum(n * P * 2 * D // P // 2048 for n in SLOT_TILES)


def laid_out(inputs):
    import numpy as np
    v = {k: np.asarray(a) for k, a in inputs.items()}
    c = np.ascontiguousarray
    f = {}
    for name in ("x", "g_xattn", "g_ffn", "L1_ffn_router_b", "L1_ffn_b2", "L0_xattn_bv", "L0_xattn_bo",
                 "L1_xattn_bv", "L1_xattn_bo"):
        f[name] = c(v[name])

    def down(w):
        return w.reshape(KT, P, -1).transpose(1, 0, 2)
    f["ctxT"] = c(v["ctx_1024"].reshape(T, P, KT, P).transpose(0, 3, 2, 1).reshape(T, P, KT * P))
    for L in range(2):
        w = [v[f"L{L}_xattn_W{n}"] for n in "qkvo"]
        if L:
            w = [a.T for a in w]
        f[f"wat{L}"] = c(np.stack([down(a) for a in w], 1).reshape(P, -1))
    f["bqk"] = c(np.stack([v[f"L{L}_xattn_b{n}"].reshape(KT, P).T for L in range(2) for n in "qk"], 1).reshape(P, -1))
    f["wr"] = c(np.concatenate([down(v["L0_ffn_Wg"].T), down(v["L1_ffn_router_w"])], 2).reshape(P, -1))
    f["qmask"] = c(v["mask_BxS_ik0"].T)
    f["b1"] = c(v["L1_ffn_b1"].reshape(8, F1 // P, P).transpose(2, 0, 1).reshape(P, -1))
    f["slab0"] = c(np.concatenate([v["L0_ffn_W1"].reshape(16, KT, P, 2 * F0).transpose(0, 2, 1, 3).reshape(16, P, -1),
                                   v["L0_ffn_W2"]], 2))
    f["slab1"] = c(np.concatenate([v["L1_ffn_W1"].reshape(16, P, F1),
                                   v["L1_ffn_W2"].reshape(16, 4, P, D).transpose(0, 2, 1, 3).reshape(16, P, 4 * D)], 2))
    f["shared_w"] = c(np.concatenate([down(v["L0_ffn_Ws1"]).reshape(P, -1), down(v["L0_ffn_Ws2"]).reshape(P, -1)], 1))
    p, q = np.arange(P)[:, None], np.arange(P)[None, :]
    f["cf"] = c(np.concatenate([np.eye(P), p // HD == np.arange(8)[None, :], np.broadcast_to(16 - np.arange(16), (P, 16)),
                                np.broadcast_to(8 - np.arange(8), (P, 8)), np.broadcast_to(128 * np.arange(48), (P, 48))],
                               1).astype(np.float32))
    f["cb"] = c(np.concatenate([np.eye(P), np.ones((P, P)), p < q, np.tile(np.where(q > p, NEG, 0.0), (1, GH))],
                               1).astype(np.float32))
    return f


def kernel(**inputs):
    import concourse.bacc as bacc
    from concourse.bass_utils import run_bass_kernel_spmd
    nc = bacc.Bacc("TRN2", target_bir_lowering=False, num_devices=1)
    arrays, args = {}, {}
    for name, a in laid_out(inputs).items():
        arrays[f"in_{name}"] = a
        args[name] = nc.dram_tensor(f"in_{name}", a.shape, mybir.dt.from_np(a.dtype), kind="ExternalInput").ap()
    o = nc.dram_tensor("out_x", (T, P, D), F32, kind="ExternalOutput").ap()
    build(nc, args, o)
    r = run_bass_kernel_spmd(nc, [arrays], core_ids=[0])
    return r.results[0]["out_x"]
```

```python
from contextlib import ExitStack

import concourse.bass as bass
from concourse import mybir

F32 = mybir.dt.float32
BF16 = mybir.dt.bfloat16
I32 = mybir.dt.int32
ALU = mybir.AluOpType
ACT = mybir.ActivationFunctionType
AX = mybir.AxisListType

P = 128
T = 16
D = 256
KT = D // P
H = 16
HD = D // H
GH = 4
G = H // GH
VW = HD + 1
EPS = 1e-5
NEG = -1e30
EXPERTS = (16, 8)
SLOT_TILES = (48, 40)
F0 = 128
F1 = 1024
FS = 256
ZERO_COLS = tuple(n * 2 * D // T for n in SLOT_TILES)
LAG = 3
PEEL = (4, 5)
SLAB = (KT * 2 * F0 + D, F1 + (F1 // P // 2) * D)


class Tile:

    def __init__(self, r, off, unroll=2):
        self.r, self.off, self.unroll = r, off, unroll

    def plus(self, k):
        return Tile(self.r, self.off + k, self.unroll)

    @property
    def v(self):
        return self.unroll * self.r + self.off

    @property
    def par(self):
        return self.off % 2

    @property
    def half(self):
        return self.unroll // 2 * self.r + self.off // 2

    @property
    def quarter(self):
        assert self.unroll == 4
        return self.r + self.off // 4


def at(ap, i):
    return ap[:, bass.ds(i, 1), :].rearrange("p a d -> p (a d)")


def need(eng, sem, v):
    if isinstance(v, int) and v <= 0:
        return
    eng.wait_ge(sem, v)


def column(ap, first, r, last, width):
    return ap[:, first:first + last + width][:, bass.ds(r, width)]


class Experts:

    def __init__(self, nc, eng, name, L):
        self.nc, self.eng, self.most = nc, eng, EXPERTS[L] - 1
        self.loaded = [eng.alloc_register(f"{name}{L}_{i}") for i in range(4)]
        self.kept = eng.alloc_register(f"{name}{L}_kept")

    def bounded(self, value, scale):
        return self.nc.s_assert_within(value, 0, self.most * scale,
                                       skip_runtime_bounds_check_because="the table holds expert numbers, clamped when it is made")

    def load(self, table, j, scale):
        self.eng.reg_load(self.loaded, table[0:1, bass.ds(j.v, 4)])
        return [self.bounded(self.eng.snap(self.bounded(self.eng.snap(r), 1) * scale), scale) for r in self.loaded]

    def keep(self, value):
        self.eng.reg_mov(self.kept, value)

    def last(self, scale):
        return self.bounded(self.eng.snap(self.kept), scale)


class Gate:

    def __init__(self, eng, passed):
        self.eng, self.passed, self.count, self.trips = eng, passed, 0, 1

    def __call__(self, *waits):
        for sem, v in waits:
            need(self.eng, sem, v)
        if not all(isinstance(v, int) for _, v in waits):
            self.eng.sem_inc(self.passed, 1)
            self.count += self.trips

    def close(self):
        if self.count:
            self.eng.wait_ge(self.passed, self.count)


def inside(t, k):
    return not isinstance(t.v, int) or 0 <= t.v + k < T


def tiles(eng, n, first, last, step, gate=None, unroll=2):
    trips = (n - first - last) // unroll
    assert first + unroll * trips + last == n
    for i in range(first):
        step(Tile(0, i, unroll))
    if gate:
        gate.trips = trips
    with eng.Fori(0, trips) as r:
        for i in range(unroll):
            step(Tile(r, first + i, unroll))
    if gate:
        gate.trips = 1
    for i in range(n - last, n):
        step(Tile(0, i, unroll))


def build(nc, A, out):
    with ExitStack() as ctx:
        def sb(name, shape, dt=F32):
            return ctx.enter_context(nc.sbuf_tensor(name, shape, dt))

        def sem(name):
            return ctx.enter_context(nc.semaphore(name))

        def sem2(name):
            return [sem(f"{name}{i}") for i in range(2)]

        bank = [ctx.enter_context(nc.psum_tensor(f"bank{i}", [P, 512], F32)) for i in range(8)]

        x = sb("x", [P, T, D])
        arena = sb("arena", [P, 65536], BF16)
        wat = sb("wat", [P, 4, KT, D])
        cf = sb("cf", [P, 208])
        cb = sb("cb", [P, 3 * P + GH * P], BF16)
        bqk = sb("bqk", [P, 2, 2, KT])
        bvo = sb("bvo", [P, 2, D])
        wr = sb("wr", [P, KT, 24])
        rb = sb("rb", [P, 8])
        gates = sb("gates", [P, 4])
        tgate = sb("tgate", [P, 4])
        qmask = sb("qmask", [P, T], I32)
        qscale = sb("qscale", [P, T])
        mhalf = sb("mhalf", [P, 1])
        b1 = sb("b1", [P, 8 * F1 // P])
        stats = [sb(f"stats{i}", [P, 6]) for i in range(2)]
        meanvar = [sb(f"meanvar{i}", [P, 2]) for i in range(2)]
        vareps = [sb(f"vareps{i}", [P, 1]) for i in range(2)]
        rstd = [sb(f"rstd{i}", [P, 1]) for i in range(2)]
        kept_rstd = sb("kept_rstd", [P, T])
        kept_shift = sb("kept_shift", [P, T])
        logit = sb("logit", [P, T * 16])
        slot = sb("slot", [P, 2, T], I32)
        gsel = sb("gsel", [P, 2, T])
        tile_expert = sb("tile_expert", [P, 48], I32)

        ident = cf[:, 0:128]
        headrow = cf[:, 128:136]
        rev = (cf[:, 136:152], cf[:, 152:160])
        starts = cf[:, 160:208]
        identb, onesb, earlier = (cb[:, i * P:(i + 1) * P] for i in range(3))
        causal = cb[:, 3 * P:]

        work = sb("work", [P, 10832])
        used = [0]

        def part(cols):
            v = work[:, used[0]:used[0] + cols]
            used[0] += cols
            return v

        xn = [part(D) for _ in range(4)]
        xnT = [part(KT * P) for _ in range(4)]
        stage = part(SLAB[1])
        shared_cols = used[0]
        kbd = part(KT * 8 * P).rearrange("p (m h t) -> p m h t", m=KT, h=8)
        prob = [part(GH * P) for _ in range(2)]
        cb32 = work[:, used[0] - 2 * GH * P:used[0] - 2 * GH * P + 7 * P]
        probT = [part(GH * P) for _ in range(2)]
        qT = [part(KT * P) for _ in range(2)]
        kT = part(KT * P)
        vaug = [part(H * VW).rearrange("p (h w) -> p h w", h=H) for _ in range(2)]
        ctxT = [part(KT * P) for _ in range(2)]
        on = part(D)
        oT = part(KT * P)
        proj = part(D)
        rsum = part(H)
        rowmax = [part(GH) for _ in range(2)]
        shift = [part(GH) for _ in range(2)]
        used[0] = shared_cols
        xs = part(T * D).bitcast(BF16).rearrange("p (t d) -> p t d", t=T)
        rtmp = [part(T * 16) for _ in range(6)]
        rsmall = part(16 * T)
        used[0] = shared_cols - SLAB[1]
        sh_hid = [part(FS) for _ in range(2)]
        sh_act = [part(FS) for _ in range(2)]
        sh_hhi = [part(FS // 2).bitcast(BF16) for _ in range(2)]
        sh_hlo = [part(FS // 2).bitcast(BF16) for _ in range(2)]
        sh_rowsT = [part(D).bitcast(BF16) for _ in range(2)]
        assert used[0] <= shared_cols
        used[0] = 0
        rows = [part(2 * D).bitcast(BF16).rearrange("p (i d) -> p i d", i=2) for _ in range(2)]
        rowsT = [part(D).bitcast(BF16) for _ in range(4)]
        hid = [part(F1) for _ in range(2)]
        sig = [part(2 * F0) for _ in range(2)]
        hid_hi = [part(F1 // 2).bitcast(BF16) for _ in range(2)]
        hid_lo = [part(F1 // 2).bitcast(BF16) for _ in range(2)]
        yrow = [part(2 * D).rearrange("p (i d) -> p i d", i=2) for _ in range(2)]
        hid0, hid0_hi, hid0_lo, sig0 = ([v[i % 2][:, i // 2 * F0:(i // 2 + 1) * F0] for i in range(4)]
                                        for v in (hid, hid_hi, hid_lo, sig))
        b2 = part(8 * D).rearrange("p (e d) -> p e d", e=8)
        used[0] = 0
        ygot = [[part(D) for _ in range(2)] for _ in range(2)]

        whi, wlo = [], []
        for L in range(2):
            n = T * SLAB[L]
            whi.append(arena[:, 0:n].rearrange("p (s f) -> p s f", s=T))
            wlo.append(arena[:, n:2 * n].rearrange("p (s f) -> p s f", s=T))
        o = 2 * T * SLAB[0]
        NS = KT * 2 * FS + KT * D
        shi, slo = arena[:, o:o + NS], arena[:, o + NS:o + 2 * NS]
        o += 2 * NS
        sstage = arena[:, o:o + 2 * NS].bitcast(F32)
        o += 2 * NS
        zeros = arena[:, o:o + ZERO_COLS[0]]

        xg = [nc.dram_tensor(f"xg{L}", [SLOT_TILES[L] * P, 2 * D], BF16, kind="Internal").ap() for L in range(2)]
        y = [nc.dram_tensor(f"y{L}", [SLOT_TILES[L] * P, D], F32, kind="Internal").ap() for L in range(2)]

        const_in = sem("const_in")
        wat_in = sem("wat_in")
        bv_in = sem("bv_in")
        ctx_in, x_in = sem2("ctx_in"), sem2("x_in")
        stage_in = sem("stage_in")
        sw_in = sem("sw_in")
        zero_set, zero_out = sem("zero_set"), sem("zero_out")
        set_ok, half_set, cb_ok = sem("set_ok"), sem("half_set"), sem("cb_ok")
        ones_ok = sem("ones_ok")
        st_ok, mv_ok, ve_ok, rstd_ok, xn_ok, pe_T, xnT_ok = (
            sem2(s) for s in ("st_ok", "mv_ok", "ve_ok", "rstd_ok", "xn_ok", "pe_T", "xnT_ok"))
        pe_k, pe_v, pe_q = sem("pe_k"), sem("pe_v"), sem("pe_q")
        k_ok, v_ok, q_ok = sem("k_ok"), sem("v_ok"), sem("q_ok")
        kbd0_ok, kbd1_ok = sem("kbd0_ok"), sem("kbd1_ok")
        pe_s, mx_ok, shift_ok, exp_ok = sem("pe_s"), sem("mx_ok"), sem("shift_ok"), sem("exp_ok")
        pe_pt, pt_ok, pe_pv = sem("pe_pt"), sem("pt_ok"), sem("pe_pv")
        rs_ok, o_ok, pe_oT, oT_ok, pe_o, t_ok, x_ok = (
            sem(s) for s in ("rs_ok", "o_ok", "pe_oT", "oT_ok", "pe_o", "t_ok", "x_ok"))
        hi_ok, lo_ok = sem("hi_ok"), sem("lo_ok")
        pe_lg, lg_ok, kept_ok, xr_ok, xshi_ok, xs_ok = (
            sem(s) for s in ("pe_lg", "lg_ok", "kept_ok", "xr_ok", "xshi_ok", "xs_ok"))
        dve_link = sem("dve_link")
        expo_ok, m_ok, pe_rank, slot_ok = sem("expo_ok"), sem("m_ok"), sem("pe_rank"), sem("slot_ok")
        scattered = sem("scattered")
        sh_peT, sh_T, sh_up, sh_sig, sh_h, sh_hi, sh_lo, sh_dn, sh_x = (
            sem("sh_" + s) for s in ("peT", "T", "up", "sig", "h", "hi", "lo", "dn", "x"))
        sws_ok = sem("sws_ok")
        ex = [{s: sem(f"ex{L}_{s}") for s in
               ("rows0", "rows1", "pe_rT", "rT", "up", "upb", "sig", "h", "ha", "hi", "lo", "dn", "y", "out0", "out1")}
              for L in range(2)]
        got = [sem2(f"got{L}_") for L in range(2)]
        half_ok, cx_ok = sem("half_ok"), sem("cx_ok")
        b2_in = sem("b2_in")
        stored = sem2("stored")
        gate_sem = {e: sem("gate_" + e) for e in ("act", "dve", "pe", "pool", "sp")}

        block = ctx.enter_context(nc.Block())

        @block.sync
        def _(sp):
            small = [(cf[:], A["cf"]), (cb32, A["cb"]), (bqk[:].rearrange("p l a k -> p (l a k)"), A["bqk"]),
                     (wr[:].rearrange("p k e -> p (k e)"), A["wr"]), (qmask[:], A["qmask"]), (b1[:], A["b1"]),
                     (gates[:, 0:2], A["g_xattn"].partition_broadcast(P)), (gates[:, 2:4], A["g_ffn"].partition_broadcast(P)),
                     (rb[:], A["L1_ffn_router_b"].partition_broadcast(P))]
            assert len(small) == SMALL

            def load_x(t):
                sp.dma_start(at(x, t.v), A["x"][bass.ds(t.v, 1)].rearrange("a p d -> (a p) d")).then_inc(x_in[t.par], 16)

            def load_ctx(L, t):
                n = t.plus(T * L)
                need(sp, pe_k, n.v - 1)
                sp.dma_start(ctxT[t.par], A["ctxT"][bass.ds(t.v, 1)].rearrange("a p d -> (a p) d")).then_inc(ctx_in[t.par], 16)

            def load_stage(L, t):
                n = t.plus(T * L)
                need(sp, hi_ok, n.v)
                need(sp, lo_ok, n.v)
                sp.dma_start(stage[:, 0:SLAB[L]], A[f"slab{L}"][bass.ds(t.v, 1)].rearrange("a p d -> (a p) d")).then_inc(stage_in, 16)

            def load_layer(L):
                sp.dma_start(wat[:].rearrange("p a k d -> p (a k d)"), A[f"wat{L}"]).then_inc(wat_in, 16)
                for i, name in enumerate(("bv", "bo")):
                    sp.dma_start(bvo[:, i, :], A[f"L{L}_xattn_{name}"].partition_broadcast(P)).then_inc(bv_in, 16)

            load_x(Tile(0, 0))
            for d, s in small:
                sp.dma_start(d, s).then_inc(const_in, 16)
            load_ctx(0, Tile(0, 0))
            load_layer(0)
            load_x(Tile(0, 1))
            load_ctx(0, Tile(0, 1))
            load_stage(0, Tile(0, 0))
            sp.dma_start(sstage, A["shared_w"]).then_inc(sw_in, 16)
            sp.wait_ge(zero_set, 1)

            for L in range(2):
                if L:
                    sp.wait_ge(cx_ok, T)
                    load_ctx(1, Tile(0, 0))
                    load_ctx(1, Tile(0, 1))
                    load_stage(1, Tile(0, 0))

                def attend(t, L=L):
                    if not isinstance(t.v, int) or t.v + 2 < T:
                        if L == 0:
                            need(sp, x_in[t.par], 16 * (t.half + 1))
                            load_x(t.plus(2))
                        load_ctx(L, t.plus(2))
                    if L == 0:
                        for M in range(2):
                            flat = xg[M].rearrange("(p a) d -> p (a d)", p=P).rearrange("p (t c) -> p t c", t=T)
                            sp.dma_start(at(flat, t.v), zeros[:, 0:ZERO_COLS[M]]).then_inc(zero_out, 16)
                    if not isinstance(t.v, int) or t.v + 1 < T:
                        load_stage(L, t.plus(1))
                tiles(sp, T, 1, 3, attend)
                sp.wait_ge(x_ok, T * (L + 1))
                if L == 0:
                    load_layer(1)
                if L == 1:
                    sp.wait_ge(scattered, 32 * T * 2)
                    sp.dma_start(b2, A["L1_ffn_b2"].rearrange("e d -> (e d)").partition_broadcast(P).rearrange("p (e d) -> p e d", e=8)).then_inc(b2_in, 16)
                s = ex[L]
                sp.wait_ge(scattered, 32 * T * (L + 1))
                if L == 0:
                    sp.wait_ge(sh_x, T)

                def load_rows(J, L=L, s=s):
                    need(sp, s["pe_rT"], 2 * J.v - 2)
                    src = xg[L].rearrange("(j i p) d -> j p i d", i=2, p=P)[bass.ds(J.v, 1)].rearrange("a p i d -> (a p) i d")
                    sp.dma_start(rows[J.par], src).then_inc(s[f"rows{J.par}"], 16)

                tiles(sp, SLOT_TILES[L] // 2, 2, 0, load_rows)

            def store(t):
                n = t.plus(T)
                need(sp, cx_ok, n.v + 1)
                sp.dma_start(out[bass.ds(t.v, 1)].rearrange("a p d -> (a p) d"), at(x, t.v)).then_inc(stored[t.par], 16)
            tiles(sp, T, 0, 0, store)
            for s in stored:
                sp.wait_ge(s, 16 * T // 2)

        @block.gpsimd
        def _(pool):
            gate = Gate(pool, gate_sem["pool"])
            pool.memset(zeros, 0.0).then_inc(zero_set, 1)
            pool.memset(mhalf[:], -0.5).then_inc(half_set, 1)
            pool.wait_ge(half_set, 1)

            def power(w, n):
                need(pool, ve_ok[w], n.v + 1)
                pool.tensor_tensor(rstd[w][:], vareps[w][:], mhalf[:], ALU.pow).then_inc(rstd_ok[w], 1)

            def keys1(L, t):
                n = t.plus(T * L)
                need(pool, k_ok, n.v + 1)
                need(pool, pe_s, 4 * n.v)
                pool.tensor_tensor(kbd[:, 1, :, :], kT[:, P:2 * P].unsqueeze(1).to_broadcast([P, 8, P]),
                                   headrow.unsqueeze(2).to_broadcast([P, 8, P]), ALU.mult).then_inc(kbd1_ok, 1)

            def split_lo(L, t):
                n = t.plus(T * L)
                gate((hi_ok, n.v + 1))
                pool.tensor_tensor(at(wlo[L], t.v), stage[:, 0:SLAB[L]], at(whi[L], t.v), ALU.subtract).then_inc(lo_ok, 1)

            pool.wait_ge(const_in, 16 * SMALL)
            for L in range(2):
                if L:
                    pool.wait_ge(cx_ok, T)
                power(0, Tile(0, T * L))
                keys1(L, Tile(0, 0))
                power(0, Tile(0, T * L + 1))

                def attend(t, L=L):
                    if inside(t, -2):
                        power(1, t.plus(T * L - 2))
                    if inside(t, -1):
                        split_lo(L, t.plus(-1))
                    if inside(t, 2):
                        power(0, t.plus(T * L + 2))
                    if inside(t, 1):
                        keys1(L, t.plus(1))
                tiles(pool, T + LAG, *PEEL, attend, gate)

                pool.wait_ge(x_ok, T * (L + 1))
                def low_rows(t, L=L):
                    n = t.plus(T * L)
                    gate((xshi_ok, n.v + 1))
                    pool.tensor_tensor(at(xs, t.v)[:, D:2 * D], xn[t.par], at(xs, t.v)[:, 0:D], ALU.subtract).then_inc(xs_ok, 1)
                tiles(pool, T, 0, 0, low_rows, gate)
                if L == 0:
                    pool.wait_ge(sws_ok, 1)
                    pool.tensor_tensor(slo, sstage, shi, ALU.subtract).then_inc(sws_ok, 1)

                pool.wait_ge(slot_ok, L + 1)
                pool.wait_ge(xs_ok, T * (L + 1))
                pool.wait_ge(zero_out, 16 * 2 * T)
                for t in range(T):
                    for c in range(2):
                        pool.indirect_dma_start(xg[L], bass.IndirectOffsetOnAxis(ap=slot[:, c, t:t + 1], axis=0),
                                                xs[:, t, :], None).then_inc(scattered, 16)

                s = ex[L]
                def store_y(J, L=L, s=s):
                    gate((s["y"], 2 * J.v + 2))
                    dst = y[L].rearrange("(j i p) d -> j p i d", i=2, p=P)[bass.ds(J.v, 1)].rearrange("a p i d -> (a p) i d")
                    pool.dma_start(dst, yrow[J.par]).then_inc(s[f"out{J.par}"], 16)
                tiles(pool, SLOT_TILES[L] // 2, 0, 0, store_y, gate)
                for o in range(2):
                    pool.wait_ge(s[f"out{o}"], 16 * SLOT_TILES[L] // 4)

                for t in range(T):
                    need(pool, cx_ok, T * L + t - 1 if t >= 2 else 0)
                    for c in range(2):
                        pool.indirect_dma_start(ygot[t % 2][c], None, y[L],
                                                bass.IndirectOffsetOnAxis(ap=slot[:, c, t:t + 1], axis=0)).then_inc(got[L][t % 2], 16)
            gate.close()

        @block.scalar
        def _(act):
            gate = Gate(act, gate_sem["act"])

            def keys(L, t):
                n = t.plus(T * L)
                need(act, pe_k, n.v + 1)
                need(act, kbd0_ok, n.v)
                need(act, kbd1_ok, n.v)
                for m in range(KT):
                    i = act.activation(kT[:, m * P:(m + 1) * P], bank[6][:, m * P:(m + 1) * P], ACT.Identity,
                                       bias=bqk[:, L, 1, m:m + 1])
                i.then_inc(k_ok, 1)

            def queries(L, t):
                n = t.plus(T * L)
                need(act, pe_q, n.v + 1)
                need(act, pe_s, 4 * n.v - 4)
                for m in range(KT):
                    i = act.activation(qT[t.par][:, m * P:(m + 1) * P], bank[6][:, m * P:(m + 1) * P], ACT.Identity,
                                       bias=bqk[:, L, 0, m:m + 1])
                i.then_inc(q_ok, 1)

            def xnT_copy(w, L, t):
                n = t.plus(T * L)
                need(act, pe_T[w], n.v + 1)
                need(act, pe_lg if w else pe_q, n.v - 1)
                act.activation(xnT[2 * w + t.par], bank[5][:, 0:KT * P], ACT.Copy).then_inc(xnT_ok[w], 1)

            def exps(L, t, g):
                n = t.plus(T * L)
                waits = ((shift_ok, 4 * n.v + g + 1), (pe_pt, 4 * n.v + g - 1))
                if L == 0:
                    for w in waits:
                        need(act, *w)
                    scale = 1.0 / 4
                else:
                    gate(*waits)
                    scale = qscale[:, bass.ds(t.v, 1)]
                for h in range(GH):
                    c = slice(h * P, (h + 1) * P)
                    i = act.activation(prob[g % 2][:, c], bank[g % 2][:, c], ACT.Exp, scale=scale, bias=shift[g % 2][:, h:h + 1])
                i.then_inc(exp_ok, 1)

            def probT_copy(L, t, g):
                n = t.plus(T * L)
                need(act, pe_pt, 4 * n.v + g + 1)
                need(act, pe_pv, 4 * n.v + g - 1)
                act.activation(probT[g % 2], bank[2 + g % 2][:], ACT.Copy).then_inc(pt_ok, 1)

            def oT_copy(L, t):
                n = t.plus(T * L)
                need(act, pe_oT, n.v + 1)
                need(act, pe_o, n.v)
                act.activation(oT, bank[5][:, 0:KT * P], ACT.Copy).then_inc(oT_ok, 1)

            def split_hi(L, t, half):
                n = t.plus(T * L)
                if half == 0:
                    gate((stage_in, 16 * (n.v + 1)))
                c = slice(half * SLAB[L] // 2, (half + 1) * SLAB[L] // 2)
                i = act.activation(at(whi[L], t.v)[:, c], stage[:, c], ACT.Copy)
                if half:
                    i.then_inc(hi_ok, 1)

            act.wait_ge(const_in, 16 * SMALL)
            act.activation(cb[:], cb32, ACT.Copy).then_inc(cb_ok, 1)
            act.activation(tgate[:], gates[:], ACT.Tanh).then_inc(set_ok, 1)
            for L in range(2):
                xnT_copy(0, L, Tile(0, 0))
                keys(L, Tile(0, 0))
                queries(L, Tile(0, 0))

                def attend(t, L=L):
                    if inside(t, 1):
                        xnT_copy(0, L, t.plus(1))
                    if inside(t, 0):
                        exps(L, t, 0)
                    if inside(t, -1):
                        probT_copy(L, t.plus(-1), 3)
                    if inside(t, 0):
                        exps(L, t, 1)
                    if inside(t, 1):
                        keys(L, t.plus(1))
                    if inside(t, 0):
                        probT_copy(L, t, 0)
                        exps(L, t, 2)
                        probT_copy(L, t, 1)
                    if inside(t, -1):
                        oT_copy(L, t.plus(-1))
                    if inside(t, 0):
                        split_hi(L, t, 0)
                    if inside(t, 1):
                        queries(L, t.plus(1))
                    if inside(t, 0):
                        exps(L, t, 3)
                        probT_copy(L, t, 2)
                    if inside(t, -2):
                        xnT_copy(1, L, t.plus(-2))
                    if inside(t, 0):
                        split_hi(L, t, 1)
                tiles(act, T + LAG, *PEEL, attend, gate)
                act.wait_ge(kept_ok, 2 * T * (L + 1))
                act.wait_ge(x_ok, T * (L + 1))
                if L == 0:
                    act.wait_ge(m_ok, 1)
                    act.activation(rtmp[1], rtmp[0], ACT.Exp).then_inc(expo_ok, 1)

                def high_rows(t, L=L):
                    n = t.plus(T * L)
                    gate((xs_ok, n.v - 1), (xshi_ok, n.v - 1))
                    act.activation(xn[t.par], at(x, t.v), ACT.Identity, scale=kept_rstd[:, bass.ds(t.v, 1)],
                                   bias=kept_shift[:, bass.ds(t.v, 1)]).then_inc(xr_ok, 1)
                    gate((xr_ok, n.v + 1))
                    act.activation(at(xs, t.v)[:, 0:D], xn[t.par], ACT.Copy).then_inc(xshi_ok, 1)
                tiles(act, T, 2, 0, high_rows, gate)
                if L == 0:
                    act.wait_ge(sw_in, 16)
                    act.activation(shi, sstage, ACT.Copy).then_inc(sws_ok, 1)
                if L == 1:
                    act.wait_ge(m_ok, 3)
                    act.activation(rsmall[:, 2 * T:3 * T], rsmall[:, T:2 * T], ACT.Exp).then_inc(expo_ok, 1)

                def shared_turn(t):
                    need(act, sh_peT, t.v + 1)
                    need(act, sh_up, t.v - 1)
                    act.activation(sh_rowsT[t.par], bank[4 + t.par][:, 0:2 * P].bitcast(BF16), ACT.Copy).then_inc(sh_T, 1)

                def shared(t):
                    if not isinstance(t.v, int) or t.v + 1 < T:
                        shared_turn(t.plus(1))
                    need(act, sh_up, t.v + 1)
                    need(act, sh_h, t.v - 1)
                    act.activation(sh_act[t.par], bank[t.par][:, 2 * P:4 * P], ACT.Silu).then_inc(sh_sig, 1)
                    need(act, sh_h, t.v + 1)
                    need(act, sh_dn, t.v - 1)
                    act.activation(sh_hhi[t.par], sh_hid[t.par], ACT.Copy).then_inc(sh_hi, 1)
                if L == 0:
                    shared_turn(Tile(0, 0))
                    tiles(act, T, 2, 2, shared)

                s = ex[L]

                def turn(j, s=s, L=L):
                    need(act, s["pe_rT"], j.v + 1)
                    need(act, s["upb" if L else "up"], j.v - 3)
                    act.activation(rowsT[j.off % 4], bank[j.par][:, 0:2 * P].bitcast(BF16), ACT.Copy).then_inc(s["rT"], 1)

                def expert0(j, s=s):
                    q = j.off % 4
                    need(act, s["up"], j.v + 1)
                    need(act, s["h"], j.v - 3)
                    act.activation(sig0[q], bank[2 + q][:, P:2 * P], ACT.Silu).then_inc(s["sig"], 1)
                    need(act, s["h"], j.v + 1)
                    need(act, s["dn"], j.v - 3)
                    act.activation(hid0_hi[q], hid0[q], ACT.Copy).then_inc(s["hi"], 1)
                    if not isinstance(j.v, int) or j.v + 2 < SLOT_TILES[0]:
                        turn(j.plus(2))

                experts, number = Experts(nc, act, "act_expert", L), []

                def expert1(j, s=s, experts=experts, number=number):
                    if not isinstance(j.v, int) or j.v + 2 < SLOT_TILES[1]:
                        turn(j.plus(2))
                    if j.off % 4 == 0:
                        number[:] = experts.load(tile_expert, j, F1 // P)
                    e = number[j.off % 4]
                    gate((s["upb"], j.v + 1), (s["lo"], j.v - 1))
                    for m in range(4):
                        i = act.activation(hid[j.par][:, (4 + m) * P:(5 + m) * P], bank[3 + 2 * j.par][:, m * P:(m + 1) * P],
                                           ACT.Relu, bias=column(b1, 4 + m, e, 7 * F1 // P, 1))
                    i.then_inc(s["ha"], 1)
                    need(act, s["ha"], j.v + 1)
                    need(act, s["h"], j.v + 1)
                    need(act, s["dn"], j.v - 1)
                    act.activation(hid_hi[j.par], hid[j.par], ACT.Copy).then_inc(s["hi"], 1)

                act.wait_ge(slot_ok, L + 1)
                turn(Tile(0, 0, 4))
                turn(Tile(0, 1, 4))
                tiles(act, SLOT_TILES[L], 4, 4, expert1 if L else expert0, gate, unroll=4)
                act.wait_ge(cx_ok, T * (L + 1))
            gate.close()

        @block.vector
        def _(dve):
            gate = Gate(dve, gate_sem["dve"])
            links = [0]

            def link(i):
                links[0] += 1
                i.then_inc(dve_link, 1)
                dve.wait_ge(dve_link, links[0])

            def moments(w, L, t, *waits):
                n = t.plus(T * L)
                gate(*waits)
                dve.bn_stats(stats[w][:], at(x, t.v)).then_inc(st_ok[w], 1)
                gate((st_ok[w], n.v + 1))
                dve.bn_aggr(meanvar[w][:], stats[w][:]).then_inc(mv_ok[w], 1)
                need(dve, mv_ok[w], n.v + 1)
                dve.tensor_scalar(vareps[w][:], meanvar[w][:, 1:2], EPS, None, ALU.add).then_inc(ve_ok[w], 1)

            def normalise(w, L, t):
                n = t.plus(T * L)
                need(dve, rstd_ok[w], n.v + 1)
                need(dve, pe_T[w], n.v - 1)
                dve.tensor_scalar(xn[2 * w + t.par], at(x, t.v), meanvar[w][:, 0:1], rstd[w][:], ALU.subtract,
                                  ALU.mult).then_inc(xn_ok[w], 1)
                if w:
                    dve.tensor_scalar(kept_rstd[:, bass.ds(t.v, 1)], rstd[w][:], 1.0, None, ALU.mult).then_inc(kept_ok, 1)
                    dve.tensor_scalar(kept_shift[:, bass.ds(t.v, 1)], meanvar[w][:, 0:1], rstd[w][:], -1.0, ALU.mult,
                                      ALU.mult).then_inc(kept_ok, 1)

            def scores(L, t, g):
                n = t.plus(T * L)
                k = 4 * n.v + g
                need(dve, pe_s, k + 1)
                dve.tensor_reduce(rowmax[g % 2], bank[g % 2][:].rearrange("p (h t) -> p h t", h=GH), AX.X,
                                  ALU.max).then_inc(mx_ok, 1)
                need(dve, mx_ok, k + 1)
                need(dve, exp_ok, k - 1)
                if L == 0:
                    dve.tensor_scalar(shift[g % 2], rowmax[g % 2], -1.0 / 4, None, ALU.mult).then_inc(shift_ok, 1)
                else:
                    dve.tensor_scalar(shift[g % 2], rowmax[g % 2], qscale[:, bass.ds(t.v, 1)], -1.0, ALU.mult,
                                      ALU.mult).then_inc(shift_ok, 1)

            def keys0(L, t):
                n = t.plus(T * L)
                need(dve, k_ok, n.v + 1)
                need(dve, pe_s, 4 * n.v - 2)
                dve.tensor_tensor(kbd[:, 0, :, :], kT[:, 0:P].unsqueeze(1).to_broadcast([P, 8, P]),
                                  headrow.unsqueeze(2).to_broadcast([P, 8, P]), ALU.mult).then_inc(kbd0_ok, 1)

            def values(L, t):
                n = t.plus(T * L)
                need(dve, pe_v, n.v + 1)
                need(dve, pe_pv, 4 * n.v - 4)
                dve.tensor_tensor(vaug[t.par][:, :, 0:HD], bank[7][:, 0:D].rearrange("p (h w) -> p h w", h=H),
                                  bvo[:, 0, :].rearrange("p (h w) -> p h w", h=H), ALU.add).then_inc(v_ok, 1)

            def divide(L, t):
                n = t.plus(T * L)
                o = bank[4][:, 0:H * VW].rearrange("p (h w) -> p h w", h=H)
                need(dve, pe_pv, 4 * n.v + 4)
                dve.reciprocal(rsum.unsqueeze(2), o[:, :, HD:VW]).then_inc(rs_ok, 1)
                need(dve, rs_ok, n.v + 1)
                need(dve, pe_oT, n.v)
                dve.tensor_tensor(on.rearrange("p (h w) -> p h w", h=H), o[:, :, 0:HD],
                                  rsum.unsqueeze(2).to_broadcast([P, H, HD]), ALU.mult).then_inc(o_ok, 1)

            def residual(L, t):
                n = t.plus(T * L)
                need(dve, pe_o, n.v + 1)
                dve.tensor_tensor(proj, bank[7][:, 0:D], bvo[:, 1, :], ALU.add).then_inc(t_ok, 1)
                need(dve, t_ok, n.v + 1)
                dve.scalar_tensor_tensor(out=at(x, t.v), in0=proj, scalar=tgate[:, L:L + 1], in1=at(x, t.v),
                                         op0=ALU.mult, op1=ALU.add).then_inc(x_ok, 1)

            dve.wait_ge(const_in, 16 * SMALL)
            def logits(L, t):
                n, E = t.plus(T * L), EXPERTS[L]
                lg = logit[:, 0:T * E].rearrange("p (t e) -> p t e", t=T)
                need(dve, pe_lg, n.v + 1)
                if L == 0:
                    dve.tensor_scalar(at(lg, t.v), bank[6][:, 0:E], 0.0, None, ALU.add).then_inc(lg_ok, 1)
                else:
                    dve.tensor_tensor(at(lg, t.v), bank[6][:, 0:E], rb[:], ALU.add).then_inc(lg_ok, 1)

            dve.wait_ge(set_ok, 1)
            link(dve.tensor_scalar(qscale[:], qmask[:], 0.0, 0.25, ALU.not_equal, ALU.mult))
            for L in range(2):
                def loaded(t, L=L):
                    return ((x_in[t.par], 16 * (t.half + 1)),) if L == 0 else ()

                for i in range(2):
                    dve.memset(vaug[i][:, :, HD:VW], 1.0).then_inc(ones_ok, 1)
                t0, t1 = Tile(0, 0), Tile(0, 1)
                moments(0, L, t0, *loaded(t0))
                normalise(0, L, t0)
                if L == 0:
                    dve.wait_ge(bv_in, 32)
                keys0(L, t0)
                values(L, t0)
                moments(0, L, t1, *loaded(t1))
                normalise(0, L, t1)

                def attend(t, L=L, loaded=loaded):
                    if inside(t, 0):
                        scores(L, t, 0)
                    if inside(t, -3):
                        logits(L, t.plus(-3))
                    if inside(t, -2):
                        moments(1, L, t.plus(-2), (x_ok, t.plus(T * L - 2).v + 1))
                    if inside(t, 0):
                        scores(L, t, 1)
                    if inside(t, -2):
                        normalise(1, L, t.plus(-2))
                    if inside(t, -1):
                        divide(L, t.plus(-1))
                    if inside(t, 0):
                        scores(L, t, 2)
                    if inside(t, 1):
                        values(L, t.plus(1))
                        keys0(L, t.plus(1))
                    if inside(t, 2):
                        moments(0, L, t.plus(2), *loaded(t.plus(2)))
                    if inside(t, 0):
                        scores(L, t, 3)
                    if inside(t, 2):
                        normalise(0, L, t.plus(2))
                    if inside(t, -1):
                        residual(L, t.plus(-1))
                tiles(dve, T + LAG, *PEEL, attend, gate)
                E = EXPERTS[L]
                lg = logit[:, 0:T * E].rearrange("p (t e) -> p t e", t=T)

                dve.wait_ge(lg_ok, T * (L + 1))

                def te(v, E=E):
                    return v[:, 0:T * E].rearrange("p (t e) -> p t e", t=T)

                def over_e(v, E=E):
                    return v.unsqueeze(2).to_broadcast([P, T, E])

                def over_t(v, E=E):
                    return v.unsqueeze(1).to_broadcast([P, T, E])

                small = [rsmall[:, i * T:(i + 1) * T] for i in range(16)]
                score, oh1, oh2, tmp = te(rtmp[2]), te(rtmp[3]), te(rtmp[4]), te(rtmp[5])
                both = te(rtmp[0].bitcast(BF16))
                if L == 0:
                    link(dve.tensor_reduce(small[0], lg, AX.X, ALU.max))
                    dve.tensor_tensor(te(rtmp[0]), lg, over_e(small[0]), ALU.subtract).then_inc(m_ok, 1)
                    dve.wait_ge(expo_ok, 1)
                    link(dve.tensor_reduce(small[0], te(rtmp[1]), AX.X, ALU.add))
                    link(dve.reciprocal(small[1], small[0]))
                    link(dve.tensor_tensor(score, te(rtmp[1]), over_e(small[1]), ALU.mult))
                else:
                    score = lg
                best = (small[4], small[5])
                for c, oh in enumerate((oh1, oh2)):
                    link(dve.tensor_reduce(best[c], score, AX.X, ALU.max))
                    link(dve.tensor_tensor(tmp, score, over_e(best[c]), ALU.is_equal))
                    link(dve.tensor_tensor(tmp, tmp, over_t(rev[L]), ALU.mult))
                    link(dve.tensor_reduce(small[6], tmp, AX.X, ALU.max))
                    link(dve.tensor_tensor(oh, over_e(small[6]), over_t(rev[L]), ALU.is_equal))
                    if c == 0:
                        link(dve.scalar_tensor_tensor(out=te(rtmp[2]), in0=oh1, scalar=-3e38, in1=score,
                                                      op0=ALU.mult, op1=ALU.add))
                        score = te(rtmp[2])
                if L == 1:
                    dve.tensor_tensor(small[1], best[1], best[0], ALU.subtract).then_inc(m_ok, 1)
                link(dve.tensor_tensor(both, oh1, oh2, ALU.add))
                dve.tensor_scalar(small[6], small[6], 1.0, None, ALU.mult).then_inc(m_ok, 1)
                if L == 0:
                    for c in range(2):
                        dve.tensor_scalar(gsel[:, c, :], best[c], tgate[:, 2:3], None, ALU.mult)
                dve.wait_ge(pe_rank, 2 * L + 2)
                count, whole = small[8][:, 0:E], small[9].bitcast(I32)[:, 0:E]
                link(dve.tensor_scalar(whole, bank[5][:, 0:E], float(P - 1), None, ALU.add))
                link(dve.tensor_scalar(whole, whole, 7, 7, ALU.logical_shift_right, ALU.logical_shift_left))
                ends = [small[10][:, 0:E], small[11][:, 0:E]]
                link(dve.tensor_copy(count, whole))
                link(dve.tensor_copy(ends[0], whole))
                step, a = 1, 0
                while step < E:
                    dve.tensor_copy(ends[1 - a][:, 0:step], ends[a][:, 0:step])
                    link(dve.tensor_tensor(ends[1 - a][:, step:E], ends[a][:, step:E], ends[a][:, 0:E - step], ALU.add))
                    step, a = 2 * step, 1 - a
                first = small[12][:, 0:E]
                link(dve.tensor_tensor(first, ends[a], count, ALU.subtract))
                link(dve.tensor_tensor(tmp, bank[4][:, 0:T * E].rearrange("p (t e) -> p t e", t=T), over_t(first), ALU.add))
                for c, oh in enumerate((oh1, oh2)):
                    link(dve.tensor_tensor(oh, oh, tmp, ALU.mult))
                    link(dve.tensor_reduce(small[13 + c], oh, AX.X, ALU.add))
                    link(dve.tensor_copy(slot[:, c, :], small[13 + c]))
                nj = SLOT_TILES[L]
                cmp = work[:, shared_cols + T * D:][:, 0:nj * E].rearrange("p (j e) -> p j e", j=nj)
                link(dve.tensor_tensor(cmp, starts[:, 0:nj].unsqueeze(2).to_broadcast([P, nj, E]),
                                       ends[a].unsqueeze(1).to_broadcast([P, nj, E]), ALU.is_ge))
                te_f = rtmp[5][:, 0:nj]
                link(dve.tensor_reduce(te_f, cmp, AX.X, ALU.add))
                dve.tensor_scalar(tile_expert[:, 0:nj], te_f, float(E - 1), None, ALU.min).then_inc(slot_ok, 1)
                if L == 1:
                    dve.wait_ge(expo_ok, 2)
                    link(dve.tensor_scalar(small[3], small[2], 1.0, None, ALU.add))
                    link(dve.reciprocal(small[3], small[3]))
                    link(dve.tensor_scalar(gsel[:, 0, :], small[3], tgate[:, 3:4], None, ALU.mult))
                    dve.tensor_tensor(gsel[:, 1, :], gsel[:, 0, :], small[2], ALU.mult)

                def shared_h(t):
                    need(dve, sh_sig, t.v + 1)
                    need(dve, sh_lo, t.v - 1)
                    dve.tensor_tensor(sh_hid[t.par], bank[t.par][:, 0:2 * P], sh_act[t.par], ALU.mult).then_inc(sh_h, 1)
                    need(dve, sh_hi, t.v + 1)
                    dve.tensor_tensor(sh_hlo[t.par], sh_hid[t.par], sh_hhi[t.par], ALU.subtract).then_inc(sh_lo, 1)

                def shared_x(t):
                    need(dve, sh_dn, t.v + 1)
                    dve.scalar_tensor_tensor(out=at(x, t.v), in0=bank[2 + t.par][:, 0:D], scalar=tgate[:, 2:3],
                                             in1=at(x, t.v), op0=ALU.mult, op1=ALU.add).then_inc(sh_x, 1)

                def shared(t):
                    shared_h(t)
                    if not isinstance(t.v, int) or t.v > 0:
                        shared_x(t.plus(-1))
                if L == 0:
                    tiles(dve, T, 2, 0, shared)
                    shared_x(Tile(0, T - 1))

                s = ex[L]

                experts, number = Experts(nc, dve, "dve_expert", L), {}

                def result(j, L=L, s=s, number=number):
                    need(dve, s["dn"], j.v + 1)
                    J = j.off % 4 // 2
                    need(dve, s[f"out{J}"], 16 * j.quarter)
                    to = yrow[J][:, j.par, :]
                    if L == 0:
                        dve.tensor_copy(to, bank[6 + j.par][:, 0:D]).then_inc(s["y"], 1)
                    else:
                        dve.tensor_tensor(to, bank[6 + j.par][:, 0:D], column(b2.rearrange("p e d -> p (e d)"), 0, number[j.off][1], 7 * D, D), ALU.add).then_inc(s["y"], 1)

                def expert0(j, s=s, result=result):
                    q = j.off % 4
                    need(dve, s["sig"], j.v + 1)
                    need(dve, s["lo"], j.v - 3)
                    dve.tensor_tensor(hid0[q], bank[2 + q][:, 0:P], sig0[q], ALU.mult).then_inc(s["h"], 1)
                    if not isinstance(j.v, int) or j.v > 0:
                        result(j.plus(-1))
                    need(dve, s["hi"], j.v + 1)
                    need(dve, s["dn"], j.v - 3)
                    dve.tensor_tensor(hid0_lo[q], hid0[q], hid0_hi[q], ALU.subtract).then_inc(s["lo"], 1)

                def expert1(j, s=s, result=result, experts=experts, number=number):
                    more = not isinstance(j.v, int)
                    if j.off == 4 and more or j.off == SLOT_TILES[1] - 4:
                        number[j.off - 1] = (None, experts.last(D))
                    if j.off % 4 == 0:
                        for i, e in enumerate(experts.load(tile_expert, j, 1)):
                            number[j.off + i] = [dve.snap(e * w) for w in (F1 // P, D)]
                    e = number[j.off][0]
                    need(dve, s["up"], j.v + 1)
                    need(dve, s["lo"], j.v - 1)
                    for m in range(4):
                        i = dve.tensor_scalar(hid[j.par][:, m * P:(m + 1) * P], bank[2 + 2 * j.par][:, m * P:(m + 1) * P],
                                              column(b1, m, e, 7 * F1 // P, 1), 0.0, ALU.add, ALU.max)
                    i.then_inc(s["h"], 1)
                    if not isinstance(j.v, int) or j.v > 0:
                        result(j.plus(-1))
                    need(dve, s["hi"], j.v + 1)
                    dve.tensor_tensor(hid_lo[j.par], hid[j.par], hid_hi[j.par], ALU.subtract).then_inc(s["lo"], 1)
                    if j.off in (3, 7) and (more or j.off == 3):
                        experts.keep(number[j.off][1])

                dve.wait_ge(slot_ok, L + 1)
                if L == 1:
                    dve.wait_ge(b2_in, 16)
                tiles(dve, SLOT_TILES[L], 4, 4, expert1 if L else expert0, gate, unroll=4)
                result(Tile(0, SLOT_TILES[L] - 1, 4))

                def combine(t, L=L):
                    n = t.plus(T * L)
                    need(dve, got[L][t.par], 32 * (t.half + 1))
                    for c, done in enumerate((half_ok, cx_ok)):
                        dve.scalar_tensor_tensor(out=at(x, t.v), in0=ygot[t.par][c], scalar=gsel[:, c, bass.ds(t.v, 1)],
                                                 in1=at(x, t.v), op0=ALU.mult, op1=ALU.add).then_inc(done, 1)
                        if c == 0:
                            need(dve, half_ok, n.v + 1)
                tiles(dve, T, 0, 0, combine)
                dve.wait_ge(cx_ok, T * (L + 1))
            gate.close()

        @block.tensor
        def _(pe):
            gate = Gate(pe, gate_sem["pe"])

            def turn_x(w, L, t):
                need(pe, xn_ok[w], t.plus(T * L).v + 1)
                for k in range(KT):
                    i = pe.transpose(bank[5][:, k * P:(k + 1) * P], xn[2 * w + t.par][:, k * P:(k + 1) * P], ident)
                i.then_inc(pe_T[w], 1)

            def proj_k(L, t):
                n = t.plus(T * L)
                need(pe, ctx_in[t.par], 16 * (n.half + 1))
                need(pe, q_ok, n.v)
                if inside(t, -4):
                    need(pe, lg_ok, n.v - 3)
                elif L:
                    need(pe, lg_ok, T)
                for m in range(KT):
                    for k in range(KT):
                        i = pe.matmul(bank[6][:, m * P:(m + 1) * P], wat[:, 1, k, m * P:(m + 1) * P],
                                      ctxT[t.par][:, k * P:(k + 1) * P], start=(k == 0), stop=(k == KT - 1))
                i.then_inc(pe_k, 1)

            def proj_v(L, t):
                n = t.plus(T * L)
                need(pe, ctx_in[t.par], 16 * (n.half + 1))
                need(pe, t_ok, n.v - 2 if inside(t, -3) else T * L)
                for k in range(KT):
                    i = pe.matmul(bank[7][:, 0:D], ctxT[t.par][:, k * P:(k + 1) * P], wat[:, 2, k, :],
                                  start=(k == 0), stop=(k == KT - 1))
                i.then_inc(pe_v, 1)

            def proj_q(L, t):
                n = t.plus(T * L)
                need(pe, xnT_ok[0], n.v + 1)
                need(pe, k_ok, n.v + 1)
                for m in range(KT):
                    for k in range(KT):
                        i = pe.matmul(bank[6][:, m * P:(m + 1) * P], wat[:, 0, k, m * P:(m + 1) * P],
                                      xnT[t.par][:, k * P:(k + 1) * P], start=(k == 0), stop=(k == KT - 1))
                i.then_inc(pe_q, 1)

            def score(L, t, g):
                n = t.plus(T * L)
                m = g // 2
                need(pe, q_ok, n.v + 1)
                need(pe, kbd1_ok if m else kbd0_ok, n.v + 1)
                need(pe, exp_ok, 4 * n.v + g - 1)
                i = pe.matmul(bank[g % 2][:], qT[t.par][:, m * P:(m + 1) * P],
                              kbd[:, m, 4 * (g % 2):4 * (g % 2) + 4, :].rearrange("p h t -> p (h t)"),
                              start=True, stop=(L == 1))
                if L == 0:
                    i = pe.matmul(bank[g % 2][:], identb, causal, start=False, stop=True)
                i.then_inc(pe_s, 1)

            def turn_p(L, t, g):
                n = t.plus(T * L)
                need(pe, exp_ok, 4 * n.v + g + 1)
                need(pe, pt_ok, 4 * n.v + g - 1)
                for h in range(GH):
                    i = pe.transpose(bank[2 + g % 2][:, h * P:(h + 1) * P], prob[g % 2][:, h * P:(h + 1) * P], ident)
                i.then_inc(pe_pt, 1)

            def weigh_v(L, t, g):
                n = t.plus(T * L)
                need(pe, pt_ok, 4 * n.v + g + 1)
                if g == 0:
                    need(pe, v_ok, n.v + 1)
                    need(pe, o_ok, n.v)
                for h in range(GH):
                    c = (GH * g + h) * VW
                    i = pe.matmul(bank[4][:, c:c + VW], probT[g % 2][:, h * P:(h + 1) * P], vaug[t.par][:, GH * g + h, :],
                                  start=True, stop=True)
                i.then_inc(pe_pv, 1)

            def turn_o(L, t):
                n = t.plus(T * L)
                need(pe, o_ok, n.v + 1)
                need(pe, xnT_ok[0], n.v + 3 if inside(t, 2) else T * (L + 1))
                for k in range(KT):
                    i = pe.transpose(bank[5][:, k * P:(k + 1) * P], on[:, k * P:(k + 1) * P], ident)
                i.then_inc(pe_oT, 1)

            def proj_o(L, t):
                n = t.plus(T * L)
                need(pe, oT_ok, n.v + 1)
                need(pe, v_ok, n.v + 3 if inside(t, 2) else T * (L + 1))
                for k in range(KT):
                    i = pe.matmul(bank[7][:, 0:D], oT[:, k * P:(k + 1) * P], wat[:, 3, k, :],
                                  start=(k == 0), stop=(k == KT - 1))
                i.then_inc(pe_o, 1)

            def route(L, t):
                n, E, e0 = t.plus(T * L), EXPERTS[L], 16 * L
                need(pe, xnT_ok[1], n.v + 1)
                need(pe, q_ok, n.v + 4 if inside(t, 3) else T * (L + 1))
                if not inside(t, 3):
                    need(pe, lg_ok, n.v)
                for k in range(KT):
                    i = pe.matmul(bank[6][:, 0:E], xnT[2 + t.par][:, k * P:(k + 1) * P], wr[:, k, e0:e0 + E],
                                  start=(k == 0), stop=(k == KT - 1))
                i.then_inc(pe_lg, 1)

            pe.wait_ge(const_in, 16 * SMALL)
            pe.wait_ge(cb_ok, 1)
            for L in range(2):
                pe.wait_ge(wat_in, 16 * (L + 1))
                pe.wait_ge(ones_ok, 2 * (L + 1))
                t0 = Tile(0, 0)
                E = EXPERTS[L]
                turn_x(0, L, t0)
                proj_v(L, t0)
                proj_k(L, t0)
                proj_q(L, t0)

                def attend(t, L=L):
                    if inside(t, 0):
                        score(L, t, 0)
                    if inside(t, -3):
                        route(L, t.plus(-3))
                    if inside(t, 1):
                        need(pe, xnT_ok[1], t.plus(T * L - 2).v if inside(t, -3) else T * L)
                        turn_x(0, L, t.plus(1))
                        proj_v(L, t.plus(1))
                    if inside(t, -1):
                        turn_p(L, t.plus(-1), 3)
                        weigh_v(L, t.plus(-1), 2)
                    if inside(t, 0):
                        score(L, t, 1)
                    if inside(t, 1):
                        proj_k(L, t.plus(1))
                    if inside(t, 0):
                        turn_p(L, t, 0)
                    if inside(t, -1):
                        weigh_v(L, t.plus(-1), 3)
                    if inside(t, 0):
                        score(L, t, 2)
                    if inside(t, 1):
                        proj_q(L, t.plus(1))
                    if inside(t, -1):
                        turn_o(L, t.plus(-1))
                    if inside(t, 0):
                        turn_p(L, t, 1)
                        weigh_v(L, t, 0)
                        score(L, t, 3)
                    if inside(t, -2):
                        need(pe, oT_ok, t.plus(T * L).v if inside(t, -1) else T * (L + 1))
                        turn_x(1, L, t.plus(-2))
                    if inside(t, -1):
                        proj_o(L, t.plus(-1))
                    if inside(t, 0):
                        turn_p(L, t, 2)
                        weigh_v(L, t, 1)
                tiles(pe, T + LAG, *PEEL, attend)

                pe.wait_ge(m_ok, 2 * L + 2)
                both = rtmp[0].bitcast(BF16)[:, 0:T * E]
                for d in range(1, T):
                    pe.matmul(bank[4][:, d * E:T * E], onesb, both[:, 0:(T - d) * E], start=(d == 1), stop=False,
                              skip_group_check=True)
                i = pe.matmul(bank[4][:, 0:T * E], earlier, both, start=False, stop=True, skip_group_check=True)
                i.then_inc(pe_rank, 1)
                for t in range(T):
                    i = pe.matmul(bank[5][:, 0:E], onesb, both[:, t * E:(t + 1) * E], start=(t == 0), stop=(t == T - 1))
                i.then_inc(pe_rank, 1)

                w1h, w1l = (w[:, 0:KT * 2 * FS].rearrange("p (k f) -> p k f", k=KT) for w in (shi, slo))
                w2h, w2l = (w[:, KT * 2 * FS:].rearrange("p (k f) -> p k f", k=KT) for w in (shi, slo))

                def shared_down(t):
                    need(pe, sh_lo, t.v + 1)
                    need(pe, sh_x, t.v - 1)
                    for k in range(KT):
                        f = slice(k * P, (k + 1) * P)
                        for q, (a, b) in enumerate(((sh_hhi, w2h), (sh_hlo, w2h), (sh_hhi, w2l))):
                            i = pe.matmul(bank[2 + t.par][:, 0:D], a[t.par][:, f], b[:, k, :],
                                          start=(k == 0 and q == 0), stop=(k == KT - 1 and q == 2))
                    i.then_inc(sh_dn, 1)

                def shared_turn(t):
                    need(pe, sh_T, t.v - 1)
                    gate((xs_ok, t.v + 1))
                    to = bank[4 + t.par][:, 0:2 * P].bitcast(BF16)
                    for c in range(4):
                        i = pe.transpose(to[:, c * P:(c + 1) * P], at(xs, t.v)[:, c * P:(c + 1) * P], identb)
                    i.then_inc(sh_peT, 1)

                def shared(t):
                    if not isinstance(t.v, int) or t.v + 1 < T:
                        shared_turn(t.plus(1))
                    need(pe, sh_T, t.v + 1)
                    need(pe, sh_h, t.v - 1)
                    xt = sh_rowsT[t.par]
                    for m in range(4):
                        for k in range(KT):
                            hi, lo = xt[:, k * P:(k + 1) * P], xt[:, (KT + k) * P:(KT + k + 1) * P]
                            f = slice(m * P, (m + 1) * P)
                            for q, (w, v) in enumerate(((w1h, hi), (w1h, lo), (w1l, hi))):
                                i = pe.matmul(bank[t.par][:, m * P:(m + 1) * P], w[:, k, f], v,
                                              start=(k == 0 and q == 0), stop=(k == KT - 1 and q == 2))
                    i.then_inc(sh_up, 1)
                    if not isinstance(t.v, int) or t.v > 0:
                        shared_down(t.plus(-1))
                if L == 0:
                    pe.wait_ge(sws_ok, 2)
                    pe.wait_ge(slot_ok, 1)
                    shared_turn(t0)
                    tiles(pe, T, 2, 2, shared, gate)
                    shared_down(Tile(0, T - 1))
                    pe.wait_ge(sh_x, T)

                s = ex[L]
                pe.wait_ge(slot_ok, L + 1)

                def turn_rows(j, s=s):
                    J = j.off % 4 // 2
                    need(pe, s[f"rows{J}"], 16 * (j.quarter + 1))
                    need(pe, s["rT"], j.v - 1)
                    to = bank[j.par][:, 0:2 * P].bitcast(BF16)
                    for c in range(4):
                        i = pe.transpose(to[:, c * P:(c + 1) * P], rows[J][:, j.par, c * P:(c + 1) * P], identb)
                    i.then_inc(s["pe_rT"], 1)

                slabs = SLAB[L] * (1 + L)
                most = (EXPERTS[L] - 1) * slabs
                w_hi, w_lo = (arena[:, i * T * SLAB[L]:(i + 1) * T * SLAB[L]] for i in range(2))

                def up(e, j, L, m, to):
                    for k in range(KT):
                        c = m * P + k * (SLAB[1] if L else 2 * F0)
                        hi, lo = (rowsT[j.off % 4][:, i * P:(i + 1) * P] for i in (k, KT + k))
                        for q, (w, v) in enumerate(((w_hi, hi), (w_hi, lo), (w_lo, hi))):
                            i = pe.matmul(to, column(w, c, e, most, P), v, start=(k == 0 and q == 0),
                                          stop=(k == KT - 1 and q == 2))
                    return i

                def down(e, j, L=L, s=s):
                    need(pe, s["y"], j.v - 1)
                    need(pe, s["lo"], j.v + 1)
                    nk = 1 if L == 0 else F1 // P
                    for k in range(nk):
                        if L == 0:
                            c = KT * 2 * F0
                            a_hi, a_lo = hid0_hi[j.off % 4], hid0_lo[j.off % 4]
                        else:
                            c = k // 4 * SLAB[1] + F1 + (k % 4) * D
                            a_hi, a_lo = (v[j.par][:, k * P:(k + 1) * P] for v in (hid_hi, hid_lo))
                        for q, (a, w) in enumerate(((a_hi, w_hi), (a_lo, w_hi), (a_hi, w_lo))):
                            i = pe.matmul(bank[6 + j.par][:, 0:D], a, column(w, c, e, most, D),
                                          start=(k == 0 and q == 0), stop=(k == nk - 1 and q == 2))
                    i.then_inc(s["dn"], 1)

                experts, number = Experts(nc, pe, "pe_expert", L), {}

                def expert(j, L=L, s=s, down=down, up=up, turn_rows=turn_rows, experts=experts, number=number, slabs=slabs):
                    more = not isinstance(j.v, int)
                    if j.off == 4 and more or j.off == SLOT_TILES[L] - 4:
                        number[j.off - 1] = experts.last(slabs)
                    if j.off % 4 == 0:
                        number.update((j.off + i, e) for i, e in enumerate(experts.load(tile_expert, j, slabs)))
                    e = number[j.off]
                    need(pe, s["h"], j.v - (1 if L else 3))
                    if more or j.v + 2 < SLOT_TILES[L]:
                        turn_rows(j.plus(2))
                    else:
                        need(pe, s["rT"], j.v + 1)
                    if L == 0:
                        for m in range(2):
                            i = up(e, j, 0, m, bank[2 + j.off % 4][:, m * P:(m + 1) * P])
                        i.then_inc(s["up"], 1)
                    else:
                        for m in range(4):
                            i = up(e, j, 1, m, bank[2 + 2 * j.par][:, m * P:(m + 1) * P])
                        i.then_inc(s["up"], 1)
                        gate((s["ha"], j.v - 1))
                        for m in range(4):
                            i = up(e, j, 1, 4 + m, bank[3 + 2 * j.par][:, m * P:(m + 1) * P])
                        i.then_inc(s["upb"], 1)
                    if more or j.v > 0:
                        down(number[j.off - 1], j.plus(-1))
                    if j.off in (3, 7) and (more or j.off == 3):
                        experts.keep(e)
                turn_rows(Tile(0, 0, 4))
                turn_rows(Tile(0, 1, 4))
                tiles(pe, SLOT_TILES[L], 4, 4, expert, gate, unroll=4)
                down(number[SLOT_TILES[L] - 1], Tile(0, SLOT_TILES[L] - 1, 4))
                pe.wait_ge(cx_ok, T * (L + 1))
            gate.close()


SMALL = 9


def laid_out(inputs):
    import numpy as np
    v = {k: np.asarray(a) for k, a in inputs.items()}
    c = np.ascontiguousarray
    f = {}
    for name in ("x", "g_xattn", "g_ffn", "L1_ffn_router_b", "L1_ffn_b2", "L0_xattn_bv", "L0_xattn_bo",
                 "L1_xattn_bv", "L1_xattn_bo"):
        f[name] = c(v[name])

    def down(w):
        return w.reshape(KT, P, -1).transpose(1, 0, 2)
    f["ctxT"] = c(v["ctx_1024"].reshape(T, P, KT, P).transpose(0, 3, 2, 1).reshape(T, P, KT * P))
    for L in range(2):
        w = [v[f"L{L}_xattn_W{n}"] for n in "qkvo"]
        if L:
            w = [a.T for a in w]
        f[f"wat{L}"] = c(np.stack([down(a) for a in w], 1).reshape(P, -1))
    f["bqk"] = c(np.stack([v[f"L{L}_xattn_b{n}"].reshape(KT, P).T for L in range(2) for n in "qk"], 1).reshape(P, -1))
    f["wr"] = c(np.concatenate([down(v["L0_ffn_Wg"].T), down(v["L1_ffn_router_w"])], 2).reshape(P, -1))
    f["qmask"] = c(v["mask_BxS_ik0"].T)
    f["b1"] = c(v["L1_ffn_b1"].reshape(8, F1 // P, P).transpose(2, 0, 1).reshape(P, -1))
    f["slab0"] = c(np.concatenate([v["L0_ffn_W1"].reshape(16, KT, P, 2 * F0).transpose(0, 2, 1, 3).reshape(16, P, -1),
                                   v["L0_ffn_W2"]], 2))
    f["slab1"] = c(np.concatenate([v["L1_ffn_W1"].reshape(16, P, F1),
                                   v["L1_ffn_W2"].reshape(16, 4, P, D).transpose(0, 2, 1, 3).reshape(16, P, 4 * D)], 2))
    f["shared_w"] = c(np.concatenate([down(v["L0_ffn_Ws1"]).reshape(P, -1), down(v["L0_ffn_Ws2"]).reshape(P, -1)], 1))
    p, q = np.arange(P)[:, None], np.arange(P)[None, :]
    f["cf"] = c(np.concatenate([np.eye(P), p // HD == np.arange(8)[None, :], np.broadcast_to(16 - np.arange(16), (P, 16)),
                                np.broadcast_to(8 - np.arange(8), (P, 8)), np.broadcast_to(128 * np.arange(48), (P, 48))],
                               1).astype(np.float32))
    f["cb"] = c(np.concatenate([np.eye(P), np.ones((P, P)), p < q, np.tile(np.where(q > p, NEG, 0.0), (1, GH))],
                               1).astype(np.float32))
    return f


def kernel(**inputs):
    import concourse.bacc as bacc
    from concourse.bass_utils import run_bass_kernel_spmd
    nc = bacc.Bacc("TRN2", target_bir_lowering=False, num_devices=1)
    arrays, args = {}, {}
    for name, a in laid_out(inputs).items():
        arrays[f"in_{name}"] = a
        args[name] = nc.dram_tensor(f"in_{name}", a.shape, mybir.dt.from_np(a.dtype), kind="ExternalInput").ap()
    o = nc.dram_tensor("out_x", (T, P, D), F32, kind="ExternalOutput").ap()
    build(nc, args, o)
    r = run_bass_kernel_spmd(nc, [arrays], core_ids=[0])
    return r.results[0]["out_x"]
```

```python
from contextlib import ExitStack

import concourse.bass as bass
from concourse import mybir

F32 = mybir.dt.float32
BF16 = mybir.dt.bfloat16
I32 = mybir.dt.int32
ALU = mybir.AluOpType
ACT = mybir.ActivationFunctionType
AX = mybir.AxisListType

P = 128
T = 16
D = 256
KT = D // P
H = 16
HD = D // H
GH = 4
G = H // GH
VW = HD + 1
EPS = 1e-5
NEG = -1e30
EXPERTS = (16, 8)
SLOT_TILES = (48, 40)
F0 = 128
F1 = 1024
FS = 256
REGION = T * P + P
SPARE = tuple(n - 2 * T for n in SLOT_TILES)
LAG = 5
PEEL = (7, 8)
LINKS = 14
SLAB = (KT * 2 * F0 + D, F1 + (F1 // P // 2) * D)


class Tile:

    def __init__(self, r, off, unroll=2):
        self.r, self.off, self.unroll = r, off, unroll

    def plus(self, k):
        return Tile(self.r, self.off + k, self.unroll)

    @property
    def v(self):
        return self.unroll * self.r + self.off

    @property
    def par(self):
        return self.off % 2

    @property
    def half(self):
        return self.unroll // 2 * self.r + self.off // 2

    @property
    def quarter(self):
        assert self.unroll == 4
        return self.r + self.off // 4


def at(ap, i):
    return ap[:, bass.ds(i, 1), :].rearrange("p a d -> p (a d)")


def need(eng, sem, v):
    if isinstance(v, int) and v <= 0:
        return
    eng.wait_ge(sem, v)


def column(ap, first, r, last, width):
    return ap[:, first:first + last + width][:, bass.ds(r, width)]


class Experts:

    def __init__(self, nc, eng, name, L):
        self.nc, self.eng, self.most = nc, eng, EXPERTS[L] - 1
        self.loaded = [eng.alloc_register(f"{name}{L}_{i}") for i in range(4)]
        self.kept = [eng.alloc_register(f"{name}{L}_kept{i}") for i in range(2)]

    def bounded(self, value, scale):
        return self.nc.s_assert_within(value, 0, self.most * scale,
                                       skip_runtime_bounds_check_because="the table holds expert numbers, clamped when it is made")

    def load(self, table, j, scale):
        self.eng.reg_load(self.loaded, table[0:1, bass.ds(j.v, 4)])
        return [self.bounded(self.eng.snap(self.bounded(self.eng.snap(r), 1) * scale), scale) for r in self.loaded]

    def keep(self, value, back=1):
        self.eng.reg_mov(self.kept[back - 1], value)

    def last(self, scale, back=1):
        return self.bounded(self.eng.snap(self.kept[back - 1]), scale)


class Gate:

    def __init__(self, eng, passed):
        self.eng, self.passed, self.count, self.trips = eng, passed, 0, 1

    def __call__(self, *waits):
        for sem, v in waits:
            need(self.eng, sem, v)
        if not all(isinstance(v, int) for _, v in waits):
            self.eng.sem_inc(self.passed, 1)
            self.count += self.trips

    def close(self):
        if self.count:
            self.eng.wait_ge(self.passed, self.count)


def slab_half(L, half):
    return slice(half * SLAB[L] // 2, (half + 1) * SLAB[L] // 2)


def inside(t, k):
    return not isinstance(t.v, int) or 0 <= t.v + k < T


def tiles(eng, n, first, last, step, gate=None, unroll=2):
    trips = (n - first - last) // unroll
    assert first + unroll * trips + last == n
    for i in range(first):
        step(Tile(0, i, unroll))
    if gate:
        gate.trips = trips
    with eng.Fori(0, trips) as r:
        for i in range(unroll):
            step(Tile(r, first + i, unroll))
    if gate:
        gate.trips = 1
    for i in range(n - last, n):
        step(Tile(0, i, unroll))


def build(nc, A, out):
    with ExitStack() as ctx:
        def sb(name, shape, dt=F32):
            return ctx.enter_context(nc.sbuf_tensor(name, shape, dt))

        def sem(name):
            return ctx.enter_context(nc.semaphore(name))

        def sem2(name):
            return [sem(f"{name}{i}") for i in range(2)]

        bank = [ctx.enter_context(nc.psum_tensor(f"bank{i}", [P, 512], F32)) for i in range(8)]

        x = sb("x", [P, T, D])
        arena = sb("arena", [P, 65536], BF16)
        wat = sb("wat", [P, 4, KT, D])
        cf = sb("cf", [P, 224])
        cb = sb("cb", [P, 3 * P + GH * P], BF16)
        bqk = sb("bqk", [P, 2, 2, KT])
        bvo = sb("bvo", [P, 2, D])
        wr = sb("wr", [P, KT, 24])
        rb = sb("rb", [P, 8])
        gates = sb("gates", [P, 4])
        tgate = sb("tgate", [P, 4])
        qmask = sb("qmask", [P, T], I32)
        qscale = sb("qscale", [P, T])
        mhalf = sb("mhalf", [P, 1])
        b1 = sb("b1", [P, 8 * F1 // P])
        stats = [sb(f"stats{i}", [P, 6]) for i in range(2)]
        meanvar = [sb(f"meanvar{i}", [P, 2]) for i in range(2)]
        vareps = [sb(f"vareps{i}", [P, 1]) for i in range(2)]
        rstd = [sb(f"rstd{i}", [P, 1]) for i in range(2)]
        kept_rstd = sb("kept_rstd", [P, T])
        kept_shift = sb("kept_shift", [P, T])
        row = sb("row", [P, 2, T])
        slot = sb("slot", [P, 2, T], I32)
        best = sb("best", [P, 2, T])
        slot_pair = sb("slot_pair", [P, 2, 2], I32)
        taken = sb("taken", [P, 16])
        tail = sb("tail", [P, 16], I32)
        zeros = sb("zeros", [P, 2 * D], BF16)
        choice = sb("choice", [P, 16 * 17 + 6])
        gsel = sb("gsel", [P, 2, T])
        slot_now = sb("slot_now", [P, 2], I32)
        tile_row = sb("tile_row", [P, 48], I32)
        tile_expert = sb("tile_expert", [P, 48], I32)

        ident = cf[:, 0:128]
        headrow = cf[:, 128:136]
        rev = (cf[:, 136:152], cf[:, 152:160])
        starts = cf[:, 160:208]
        region = cf[:, 208:224]
        identb, onesb, earlier = (cb[:, i * P:(i + 1) * P] for i in range(3))
        causal = cb[:, 3 * P:]

        work = sb("work", [P, 10832 + 4 * D])
        used = [0]

        def part(cols):
            v = work[:, used[0]:used[0] + cols]
            used[0] += cols
            return v

        xn = [part(D) for _ in range(4)]
        xnT = [part(KT * P) for _ in range(4)]
        stage = part(SLAB[1])
        shared_cols = used[0]
        kbd = part(KT * 8 * P).rearrange("p (m h t) -> p m h t", m=KT, h=8)
        prob = [part(GH * P) for _ in range(2)]
        cb32 = work[:, used[0] - 2 * GH * P:used[0] - 2 * GH * P + 7 * P]
        probT = [part(GH * P) for _ in range(2)]
        qT = [part(KT * P) for _ in range(2)]
        kT = part(KT * P)
        vaug = [part(H * VW).rearrange("p (h w) -> p h w", h=H) for _ in range(2)]
        ctxT = [part(KT * P) for _ in range(2)]
        on = part(D)
        oT = part(KT * P)
        proj = on
        rsum = part(H)
        rowmax = [part(GH) for _ in range(2)]
        shift = [part(GH) for _ in range(2)]
        ygot = [part(D) for _ in range(2)]
        xr = part(D)
        xs = [part(D).bitcast(BF16) for _ in range(2)]
        used[0] = shared_cols
        rtmp = [part(48 * 16) for _ in range(4)]
        rsmall = part(16 * T)
        used[0] = shared_cols - SLAB[1]
        sh_hid = [part(FS) for _ in range(2)]
        sh_act = [part(FS) for _ in range(2)]
        sh_hhi = [part(FS // 2).bitcast(BF16) for _ in range(2)]
        sh_hlo = [part(FS // 2).bitcast(BF16) for _ in range(2)]
        assert used[0] <= shared_cols
        used[0] = 0
        rows = [part(2 * D).bitcast(BF16).rearrange("p (i d) -> p i d", i=2) for _ in range(2)]
        rowsT = [part(D).bitcast(BF16) for _ in range(4)]
        hid = [part(F1) for _ in range(2)]
        sig = [part(2 * F0) for _ in range(2)]
        hid_hi = [part(F1 // 2).bitcast(BF16) for _ in range(4)]
        hid_lo = [part(F1 // 2).bitcast(BF16) for _ in range(4)]
        yrow = [part(2 * D).rearrange("p (i d) -> p i d", i=2) for _ in range(2)]
        hid0, hid0_hi, hid0_lo, sig0 = ([v[i % 2][:, i // 2 * F0:(i // 2 + 1) * F0] for i in range(4)]
                                        for v in (hid, hid_hi, hid_lo, sig))
        b2 = part(8 * D).rearrange("p (e d) -> p e d", e=8)
        used[0] = 0
        ylast = [[part(D) for _ in range(2)] for _ in range(4)]

        whi, wlo = [], []
        for L in range(2):
            n = T * SLAB[L]
            whi.append(arena[:, 0:n].rearrange("p (s f) -> p s f", s=T))
            wlo.append(arena[:, n:2 * n].rearrange("p (s f) -> p s f", s=T))
        o = 2 * T * SLAB[0]
        xT = arena[:, o:o + T * 4 * P].rearrange("p (t c) -> p t c", t=T)
        o += T * 4 * P
        NS = KT * 2 * FS + KT * D
        shi, slo = arena[:, o:o + NS], arena[:, o + NS:o + 2 * NS]
        o += 2 * NS
        sstage = arena[:, o:o + 2 * NS].bitcast(F32)
        o += 2 * NS
        logit = arena[:, o:o + 2 * T * 16].bitcast(F32)
        def chosen(L):
            E, at_ = EXPERTS[L], [0]

            def some(cols, dt=F32):
                v = choice[:, at_[0]:at_[0] + cols]
                at_[0] += cols
                return v.bitcast(dt)
            pair, rest, tmp, rank = (some(2 * E).rearrange("p (t e) -> p t e", t=2) for _ in range(4))
            oh, prod = (some(4 * E).rearrange("p (c t e) -> p c t e", c=2, t=2) for _ in range(2))
            both = some(E, BF16)
            m, r = some(4).rearrange("p (c t) -> p c t", c=2), some(2)
            return pair, rest, tmp, rank, oh, prod, both, m, r

        xg = [nc.dram_tensor(f"xg{L}", [EXPERTS[L] * REGION + SPARE[L] * P, 2 * D], BF16, kind="Internal").ap() for L in range(2)]
        y = [nc.dram_tensor(f"y{L}", [SLOT_TILES[L] * P, D], F32, kind="Internal").ap() for L in range(2)]

        const_in = sem("const_in")
        wat_in = sem("wat_in")
        bv_in = sem("bv_in")
        ctx_in, x_in = sem2("ctx_in"), sem2("x_in")
        stage_in = sem2("stage_in")
        sw_in = sem("sw_in")
        zero_set, zero_out = sem("zero_set"), sem("zero_out")
        set_ok, half_set, cb_ok = sem("set_ok"), sem("half_set"), sem("cb_ok")
        ones_ok = sem("ones_ok")
        st_ok, mv_ok, ve_ok, rstd_ok, xn_ok, pe_T, xnT_ok = (
            sem2(s) for s in ("st_ok", "mv_ok", "ve_ok", "rstd_ok", "xn_ok", "pe_T", "xnT_ok"))
        pe_k, pe_v, pe_q = sem("pe_k"), sem("pe_v"), sem("pe_q")
        k_ok, v_ok, q_ok = sem("k_ok"), sem("v_ok"), sem("q_ok")
        kbd0_ok, kbd1_ok = sem("kbd0_ok"), sem("kbd1_ok")
        pe_s, mx_ok, shift_ok, exp_ok = sem("pe_s"), sem("mx_ok"), sem("shift_ok"), sem("exp_ok")
        pe_pt, pt_ok, pe_pv = sem("pe_pt"), sem("pt_ok"), sem("pe_pv")
        rs_ok, o_ok, pe_oT, oT_ok, pe_o, t_ok, x_ok = (
            sem(s) for s in ("rs_ok", "o_ok", "pe_oT", "oT_ok", "pe_o", "t_ok", "x_ok"))
        hi_ok, lo_ok = sem2("hi_ok"), sem2("lo_ok")
        pe_lg, lg_ok, kept_ok, xr_ok, xshi_ok, xs_ok = (
            sem(s) for s in ("pe_lg", "lg_ok", "kept_ok", "xr_ok", "xshi_ok", "xs_ok"))
        dve_link = sem("dve_link")
        picked, both_ok, pe_rank, rank_read, pair_ok = (
            sem(s) for s in ("picked", "both_ok", "pe_rank", "rank_read", "pair_ok"))
        expo_ok, m_ok, slot_ok, tail_ok = (sem(s) for s in ("expo_ok", "m_ok", "slot_ok", "tail_ok"))
        tail_out = sem2("tail_out")
        xthi_ok, xt_ok, index_ok = sem("xthi_ok"), sem("xt_ok"), sem("index_ok")
        scattered = sem2("scattered")
        sh_up, sh_sig, sh_h, sh_hi, sh_lo, sh_dn, sh_x = (
            sem("sh_" + s) for s in ("up", "sig", "h", "hi", "lo", "dn", "x"))
        sws_ok = sem("sws_ok")
        ex = [{s: sem(f"ex{L}_{s}") for s in
               ("rows0", "rows1", "pe_rT", "rT", "up", "upb", "sig", "h", "ha", "hi", "lo", "dn", "y", "out0", "out1")}
              for L in range(2)]
        got, last_got = sem("got"), [sem(f"last_got{i}") for i in range(4)]
        half_ok, cx_ok = sem("half_ok"), sem("cx_ok")
        now_ok = sem("now_ok")
        b2_in = sem("b2_in")
        stored = sem2("stored")
        gate_sem = {e: sem("gate_" + e) for e in ("act", "dve", "pe", "pool", "sp")}

        def fill_tails(eng, L, first, done):
            with eng.Fori(0, EXPERTS[L] // (1 + L)) as e:
                after = nc.s_assert_within(eng.value_load(tail[0:1, bass.ds((1 + L) * e + first, 1)]), 0, EXPERTS[L] * REGION - P,
                                           skip_runtime_bounds_check_because="a region has P rows more than tokens")
                eng.dma_start(xg[L][bass.ds(after, P), :], zeros[:]).then_inc(done, 16)

        block = ctx.enter_context(nc.Block())

        @block.sync
        def _(sp):
            small = [(cf[:], A["cf"]), (cb32, A["cb"]), (bqk[:].rearrange("p l a k -> p (l a k)"), A["bqk"]),
                     (wr[:].rearrange("p k e -> p (k e)"), A["wr"]), (qmask[:], A["qmask"]), (b1[:], A["b1"]),
                     (gates[:, 0:2], A["g_xattn"].partition_broadcast(P)), (gates[:, 2:4], A["g_ffn"].partition_broadcast(P)),
                     (rb[:], A["L1_ffn_router_b"].partition_broadcast(P))]
            assert len(small) == SMALL

            def load_x(t):
                sp.dma_start(at(x, t.v), A["x"][bass.ds(t.v, 1)].rearrange("a p d -> (a p) d")).then_inc(x_in[t.par], 16)

            def load_ctx(L, t):
                n = t.plus(T * L)
                need(sp, pe_k, n.v - 1)
                sp.dma_start(ctxT[t.par], A["ctxT"][bass.ds(t.v, 1)].rearrange("a p d -> (a p) d")).then_inc(ctx_in[t.par], 16)

            def load_stage(L, t, half):
                n, c = t.plus(T * L), slab_half(L, half)
                need(sp, lo_ok[half], n.v)
                sp.dma_start(stage[:, c], A[f"slab{L}"][bass.ds(t.v, 1)].rearrange("a p d -> (a p) d")[:, c]).then_inc(stage_in[half], 16)

            def load_wat(L):
                sp.dma_start(wat[:].rearrange("p a k d -> p (a k d)"), A[f"wat{L}"]).then_inc(wat_in, 16)

            def load_bias(L):
                for i, name in enumerate(("bv", "bo")):
                    sp.dma_start(bvo[:, i, :], A[f"L{L}_xattn_{name}"].partition_broadcast(P)).then_inc(bv_in, 16)

            load_x(Tile(0, 0))
            load_ctx(0, Tile(0, 0))
            load_wat(0)
            for d, s in small:
                sp.dma_start(d, s).then_inc(const_in, 16)
            load_bias(0)
            load_x(Tile(0, 1))
            load_ctx(0, Tile(0, 1))
            load_stage(0, Tile(0, 0), 0)

            for L in range(2):
                if L:
                    for o in range(2):
                        sp.wait_ge(ex[0][f"out{o}"], 16 * SLOT_TILES[0] // 4)
                    load_ctx(1, Tile(0, 0))
                    load_ctx(1, Tile(0, 1))
                    load_stage(1, Tile(0, 0), 0)

                def attend(t, L=L):
                    load_stage(L, t, 1)
                    if L == 0 and isinstance(t.v, int) and t.v == 3:
                        sp.dma_start(sstage, A["shared_w"]).then_inc(sw_in, 16)
                    if not isinstance(t.v, int) or t.v + 2 < T:
                        if L == 0:
                            need(sp, x_in[t.par], 16 * (t.half + 1))
                            load_x(t.plus(2))
                        load_ctx(L, t.plus(2))
                    some = SPARE[L] * P // T
                    if isinstance(t.v, int) and t.v == 0:
                        sp.wait_ge(zero_set, 1)
                    sp.dma_start(xg[L][bass.ds(some * t.v + EXPERTS[L] * REGION, some), :], zeros[0:some, :]).then_inc(zero_out, 16)
                    if not isinstance(t.v, int) or t.v + 1 < T:
                        load_stage(L, t.plus(1), 0)
                tiles(sp, T, 5, 3, attend)
                sp.wait_ge(x_ok, T * (L + 1))
                if L == 0:
                    load_wat(1)
                    load_bias(1)
                s = ex[L]
                sp.wait_ge(tail_ok, L + 1)
                fill_tails(sp, L, 0, tail_out[0])
                for o in range(2):
                    sp.wait_ge(scattered[o], 32 * T // 2 * (L + 1))
                sp.wait_ge(tail_out[0], 16 * (EXPERTS[0] + L * EXPERTS[1] // 2))
                if L:
                    sp.wait_ge(tail_out[1], 16 * EXPERTS[1] // 2)
                sp.wait_ge(zero_out, 16 * T * (L + 1))
                sp.wait_ge(slot_ok, L + 1)
                def row_of(J, i, L=L):
                    r = sp.value_load(tile_row[0:1, bass.ds(2 * J.v + i, 1)])
                    return nc.s_assert_within(r, 0, EXPERTS[L] * REGION + (SPARE[L] - 1) * P,
                                              skip_runtime_bounds_check_because="the table is clamped when it is made")

                def load_rows(J, L=L, s=s, row_of=row_of):
                    need(sp, s["pe_rT"], 2 * J.v - 2)
                    for i in range(2):
                        sp.dma_start(rows[J.par][:, i, :], xg[L][bass.ds(row_of(J, i), P), :]).then_inc(s[f"rows{J.par}"], 16)

                def store_y(J, L=L, s=s):
                    need(sp, s["y"], 2 * J.v + 2)
                    dst = y[L].rearrange("(j i p) d -> j p i d", i=2, p=P)[bass.ds(J.v, 1)].rearrange("a p i d -> (a p) i d")
                    sp.dma_start(dst, yrow[J.par]).then_inc(s[f"out{J.par}"], 16)

                def load_and_store(J, L=L, load_rows=load_rows, store_y=store_y):
                    more = not isinstance(J.v, int)
                    if more or J.v + 2 < SLOT_TILES[L] // 2:
                        load_rows(J.plus(2))
                    if more or J.v > 0:
                        store_y(J.plus(-1))
                load_rows(Tile(0, 0))
                load_rows(Tile(0, 1))
                if L:
                    sp.dma_start(b2, A["L1_ffn_b2"].rearrange("e d -> (e d)").partition_broadcast(P).rearrange("p (e d) -> p e d", e=8)).then_inc(b2_in, 16)
                tiles(sp, SLOT_TILES[L] // 2, 2, 2, load_and_store)
                store_y(Tile(0, SLOT_TILES[L] // 2 - 1))

            def store(t):
                n = t.plus(T)
                need(sp, cx_ok, n.v + 1)
                sp.dma_start(out[bass.ds(t.v, 1)].rearrange("a p d -> (a p) d"), at(x, t.v)).then_inc(stored[t.par], 16)
            tiles(sp, T, 0, 0, store)
            for s in stored:
                sp.wait_ge(s, 16 * T // 2)

        @block.gpsimd
        def _(pool):
            gate = Gate(pool, gate_sem["pool"])
            pool.memset(zeros[:], 0.0).then_inc(zero_set, 1)
            pool.memset(mhalf[:], -0.5).then_inc(half_set, 1)
            pool.wait_ge(half_set, 1)

            def power(w, n):
                need(pool, ve_ok[w], n.v + 1)
                pool.tensor_tensor(rstd[w][:], vareps[w][:], mhalf[:], ALU.pow).then_inc(rstd_ok[w], 1)

            def keys1(L, t):
                n = t.plus(T * L)
                need(pool, k_ok, n.v + 1)
                need(pool, pe_s, 4 * n.v)
                pool.tensor_tensor(kbd[:, 1, :, :], kT[:, P:2 * P].unsqueeze(1).to_broadcast([P, 8, P]),
                                   headrow.unsqueeze(2).to_broadcast([P, 8, P]), ALU.mult).then_inc(kbd1_ok, 1)

            def split_lo(L, t, half):
                n, c = t.plus(T * L), slab_half(L, half)
                gate((hi_ok[half], n.v + 1))
                pool.tensor_tensor(at(wlo[L], t.v)[:, c], stage[:, c], at(whi[L], t.v)[:, c], ALU.subtract).then_inc(lo_ok[half], 1)

            def fetch(t):
                gate((got, 32 * t.v), (cx_ok, t.v))
                pool.tensor_copy(slot_now[:].unsqueeze(2), slot[:, :, bass.ds(t.v, 1)]).then_inc(now_ok, 1)
                gate((now_ok, t.v + 1))
                for c in range(2):
                    pool.indirect_dma_start(ygot[c], None, y[0],
                                            bass.IndirectOffsetOnAxis(ap=slot_now[:, c:c + 1], axis=0)).then_inc(got, 16)

            def low_rows(L, t):
                n = t.plus(T * L)
                gate((xshi_ok, n.v + 1))
                pool.tensor_tensor(xs[t.par][:, D:2 * D], xr, xs[t.par][:, 0:D], ALU.subtract).then_inc(xs_ok, 1)

            def low_turned(t):
                need(pool, xnT_ok[1], t.v + 1)
                gate((xthi_ok, t.v + 1))
                pool.tensor_tensor(at(xT, t.v)[:, KT * P:], xnT[2 + t.par], at(xT, t.v)[:, 0:KT * P], ALU.subtract).then_inc(xt_ok, 1)

            def scatter(L, t):
                n = t.plus(T * L)
                gate((xs_ok, n.v + 1), (pair_ok, n.half + 1))
                for c in range(2):
                    pool.indirect_dma_start(xg[L], bass.IndirectOffsetOnAxis(ap=slot_pair[:, c, t.par:t.par + 1], axis=0),
                                            xs[t.par], None).then_inc(scattered[t.par], 16)

            pool.wait_ge(const_in, 16 * SMALL)
            for L in range(2):
                if L:
                    for o in range(2):
                        pool.wait_ge(ex[0][f"out{o}"], 16 * SLOT_TILES[0] // 4)
                    pool.wait_ge(index_ok, 1)
                    fetch(Tile(0, 0))
                power(0, Tile(0, T * L))
                if L:
                    fetch(Tile(0, 1))
                keys1(L, Tile(0, 0))
                power(0, Tile(0, T * L + 1))
                if L:
                    fetch(Tile(0, 2))

                def attend(t, L=L):
                    if inside(t, -2):
                        power(1, t.plus(T * L - 2))
                    if inside(t, -1):
                        split_lo(L, t.plus(-1), 1)
                    if inside(t, -5):
                        low_rows(L, t.plus(-5))
                    if L and inside(t, 3):
                        fetch(t.plus(3))
                    if inside(t, 2):
                        power(0, t.plus(T * L + 2))
                    if inside(t, 0):
                        split_lo(L, t, 0)
                    if L == 0 and inside(t, -3):
                        low_turned(t.plus(-3))
                    if inside(t, 1):
                        keys1(L, t.plus(1))
                    if inside(t, -5):
                        scatter(L, t.plus(-5))
                    if L == 0 and isinstance(t.v, int) and t.v == 5:
                        pool.wait_ge(sws_ok, 1)
                        pool.tensor_tensor(slo, sstage, shi, ALU.subtract).then_inc(sws_ok, 1)
                tiles(pool, T + LAG, *PEEL, attend, gate)


            pool.wait_ge(index_ok, 2)
            for o in range(2):
                pool.wait_ge(ex[1][f"out{o}"], 16 * SLOT_TILES[1] // 4)
            for t in range(T):
                need(pool, cx_ok, T + t - 3 if t >= 4 else T)
                for c in range(2):
                    pool.indirect_dma_start(ylast[t % 4][c], None, y[1],
                                            bass.IndirectOffsetOnAxis(ap=slot[:, c, t:t + 1], axis=0)).then_inc(last_got[t % 4], 16)
            gate.close()

        @block.scalar
        def _(act):
            gate = Gate(act, gate_sem["act"])

            def keys(L, t):
                n = t.plus(T * L)
                need(act, pe_k, n.v + 1)
                need(act, kbd0_ok, n.v)
                need(act, kbd1_ok, n.v)
                for m in range(KT):
                    i = act.activation(kT[:, m * P:(m + 1) * P], bank[6][:, m * P:(m + 1) * P], ACT.Identity,
                                       bias=bqk[:, L, 1, m:m + 1])
                i.then_inc(k_ok, 1)

            def queries(L, t):
                n = t.plus(T * L)
                need(act, pe_q, n.v + 1)
                need(act, pe_s, 4 * n.v - 4)
                for m in range(KT):
                    i = act.activation(qT[t.par][:, m * P:(m + 1) * P], bank[6][:, m * P:(m + 1) * P], ACT.Identity,
                                       bias=bqk[:, L, 0, m:m + 1])
                i.then_inc(q_ok, 1)

            def xnT_copy(w, L, t):
                n = t.plus(T * L)
                need(act, pe_T[w], n.v + 1)
                need(act, pe_lg if w else pe_q, n.v - 1)
                if w and L == 0:
                    need(act, xt_ok, t.v - 1)
                    gate((pe_T[1], t.v + 1))
                    act.activation(at(xT, t.v)[:, 0:KT * P], bank[5][:, 0:KT * P], ACT.Copy).then_inc(xthi_ok, 1)
                act.activation(xnT[2 * w + t.par], bank[5][:, 0:KT * P], ACT.Copy).then_inc(xnT_ok[w], 1)

            def high_rows(L, t):
                n = t.plus(T * L)
                gate((kept_ok, 2 * n.v + 2), (xs_ok, n.v), (scattered[t.par], 32 * n.half))
                act.activation(xr, at(x, t.v), ACT.Identity, scale=kept_rstd[:, bass.ds(t.v, 1)],
                               bias=kept_shift[:, bass.ds(t.v, 1)]).then_inc(xr_ok, 1)
                need(act, xr_ok, n.v + 1)
                act.activation(xs[t.par][:, 0:D], xr, ACT.Copy).then_inc(xshi_ok, 1)

            def exps(L, t, g):
                n = t.plus(T * L)
                waits = ((shift_ok, 4 * n.v + g + 1), (pe_pt, 4 * n.v + g - 1))
                if L == 0:
                    for w in waits:
                        need(act, *w)
                    scale = 1.0 / 4
                else:
                    gate(*waits)
                    scale = qscale[:, bass.ds(t.v, 1)]
                for h in range(GH):
                    c = slice(h * P, (h + 1) * P)
                    i = act.activation(prob[g % 2][:, c], bank[g % 2][:, c], ACT.Exp, scale=scale, bias=shift[g % 2][:, h:h + 1])
                i.then_inc(exp_ok, 1)

            def probT_copy(L, t, g):
                n = t.plus(T * L)
                need(act, pe_pt, 4 * n.v + g + 1)
                need(act, pe_pv, 4 * n.v + g - 1)
                act.activation(probT[g % 2], bank[2 + g % 2][:], ACT.Copy).then_inc(pt_ok, 1)

            def oT_copy(L, t):
                n = t.plus(T * L)
                need(act, pe_oT, n.v + 1)
                need(act, pe_o, n.v)
                act.activation(oT, bank[5][:, 0:KT * P], ACT.Copy).then_inc(oT_ok, 1)

            def split_hi(L, t, half):
                n, c = t.plus(T * L), slab_half(L, half)
                gate((stage_in[half], 16 * (n.v + 1)))
                act.activation(at(whi[L], t.v)[:, c], stage[:, c], ACT.Copy).then_inc(hi_ok[half], 1)

            act.wait_ge(const_in, 16 * SMALL)
            act.activation(cb[:], cb32, ACT.Copy).then_inc(cb_ok, 1)
            act.activation(tgate[:], gates[:], ACT.Tanh).then_inc(set_ok, 1)
            for L in range(2):
                keys(L, Tile(0, 0))
                xnT_copy(0, L, Tile(0, 0))
                queries(L, Tile(0, 0))

                def attend(t, L=L):
                    if inside(t, 1):
                        xnT_copy(0, L, t.plus(1))
                    if inside(t, 0):
                        exps(L, t, 0)
                    if inside(t, -1):
                        probT_copy(L, t.plus(-1), 3)
                    if inside(t, -5):
                        high_rows(L, t.plus(-5))
                    if inside(t, 0):
                        exps(L, t, 1)
                    if inside(t, 1):
                        keys(L, t.plus(1))
                    if inside(t, 0):
                        probT_copy(L, t, 0)
                    if inside(t, -2):
                        xnT_copy(1, L, t.plus(-2))
                    if inside(t, 0):
                        split_hi(L, t, 0)
                    if inside(t, -1):
                        oT_copy(L, t.plus(-1))
                    if inside(t, 0):
                        exps(L, t, 2)
                        probT_copy(L, t, 1)
                    if inside(t, 1):
                        queries(L, t.plus(1))
                    if inside(t, 0):
                        exps(L, t, 3)
                        probT_copy(L, t, 2)
                    if inside(t, 0):
                        split_hi(L, t, 1)
                    if L == 0 and isinstance(t.v, int) and t.v == 5:
                        act.wait_ge(sw_in, 16)
                        act.activation(shi, sstage, ACT.Copy).then_inc(sws_ok, 1)
                tiles(act, T + LAG, *PEEL, attend, gate)
                if L:
                    act.wait_ge(tail_ok, 2)
                    fill_tails(act, 1, 1, tail_out[1])
                act.wait_ge(m_ok, 2 * L + 1)
                act.activation(rsmall[:, 2 * T:3 * T], rsmall[:, T:2 * T], ACT.Exp).then_inc(expo_ok, 1)
                if L == 0:
                    act.wait_ge(m_ok, 2)
                    act.activation(rtmp[1][:, 0:T * 16], rtmp[0][:, 0:T * 16], ACT.Exp).then_inc(expo_ok, 1)

                def shared(t):
                    need(act, sh_up, t.v + 1)
                    need(act, sh_h, t.v - 1)
                    act.activation(sh_act[t.par], bank[t.par][:, 2 * P:4 * P], ACT.Silu).then_inc(sh_sig, 1)
                    need(act, sh_h, t.v + 1)
                    need(act, sh_dn, t.v - 1)
                    act.activation(sh_hhi[t.par], sh_hid[t.par], ACT.Copy).then_inc(sh_hi, 1)
                if L == 0:
                    tiles(act, T, 2, 0, shared)

                s = ex[L]

                def turn(j, s=s, L=L):
                    need(act, s["pe_rT"], j.v + 1)
                    need(act, s["upb" if L else "up"], j.v - 3)
                    act.activation(rowsT[j.off % 4], bank[j.par][:, 0:2 * P].bitcast(BF16), ACT.Copy).then_inc(s["rT"], 1)

                def expert0(j, s=s):
                    q = j.off % 4
                    need(act, s["up"], j.v + 1)
                    need(act, s["h"], j.v - 3)
                    act.activation(sig0[q], bank[2 + q][:, P:2 * P], ACT.Silu).then_inc(s["sig"], 1)
                    need(act, s["h"], j.v + 1)
                    need(act, s["dn"], j.v - 3)
                    act.activation(hid0_hi[q], hid0[q], ACT.Copy).then_inc(s["hi"], 1)
                    if not isinstance(j.v, int) or j.v + 2 < SLOT_TILES[0]:
                        turn(j.plus(2))

                experts, number = Experts(nc, act, "act_expert", L), []

                def expert1(j, s=s, experts=experts, number=number):
                    if not isinstance(j.v, int) or j.v + 2 < SLOT_TILES[1]:
                        turn(j.plus(2))
                    if j.off % 4 == 0:
                        number[:] = experts.load(tile_expert, j, F1 // P)
                    e = number[j.off % 4]
                    gate((s["upb"], j.v + 1), (s["lo"], j.v - 1))
                    for m in range(4):
                        i = act.activation(hid[j.par][:, (4 + m) * P:(5 + m) * P], bank[3 + 2 * j.par][:, m * P:(m + 1) * P],
                                           ACT.Relu, bias=column(b1, 4 + m, e, 7 * F1 // P, 1))
                    i.then_inc(s["ha"], 1)
                    need(act, s["ha"], j.v + 1)
                    need(act, s["h"], j.v + 1)
                    need(act, s["dn"], j.v - 3)
                    act.activation(hid_hi[j.off % 4], hid[j.par], ACT.Copy).then_inc(s["hi"], 1)

                act.wait_ge(slot_ok, L + 1)
                turn(Tile(0, 0, 4))
                turn(Tile(0, 1, 4))
                tiles(act, SLOT_TILES[L], 4, 4, expert1 if L else expert0, gate, unroll=4)
            gate.close()

        @block.vector
        def _(dve):
            gate = Gate(dve, gate_sem["dve"])
            links = [0]

            def link(i):
                links[0] += 1
                i.then_inc(dve_link, 1)
                dve.wait_ge(dve_link, links[0])

            def moments(w, L, t, *waits):
                n = t.plus(T * L)
                gate(*waits)
                dve.bn_stats(stats[w][:], at(x, t.v)).then_inc(st_ok[w], 1)
                gate((st_ok[w], n.v + 1))
                dve.bn_aggr(meanvar[w][:], stats[w][:]).then_inc(mv_ok[w], 1)
                need(dve, mv_ok[w], n.v + 1)
                dve.tensor_scalar(vareps[w][:], meanvar[w][:, 1:2], EPS, None, ALU.add).then_inc(ve_ok[w], 1)

            def normalise(w, L, t):
                n = t.plus(T * L)
                need(dve, rstd_ok[w], n.v + 1)
                need(dve, pe_T[w], n.v - 1)
                dve.tensor_scalar(xn[2 * w + t.par], at(x, t.v), meanvar[w][:, 0:1], rstd[w][:], ALU.subtract,
                                  ALU.mult).then_inc(xn_ok[w], 1)
                if w:
                    dve.tensor_scalar(kept_rstd[:, bass.ds(t.v, 1)], rstd[w][:], 1.0, None, ALU.mult).then_inc(kept_ok, 1)
                    dve.tensor_scalar(kept_shift[:, bass.ds(t.v, 1)], meanvar[w][:, 0:1], rstd[w][:], -1.0, ALU.mult,
                                      ALU.mult).then_inc(kept_ok, 1)

            def scores(L, t, g):
                n = t.plus(T * L)
                k = 4 * n.v + g
                need(dve, pe_s, k + 1)
                dve.tensor_reduce(rowmax[g % 2], bank[g % 2][:].rearrange("p (h t) -> p h t", h=GH), AX.X,
                                  ALU.max).then_inc(mx_ok, 1)
                need(dve, mx_ok, k + 1)
                need(dve, exp_ok, k - 1)
                if L == 0:
                    dve.tensor_scalar(shift[g % 2], rowmax[g % 2], -1.0 / 4, None, ALU.mult).then_inc(shift_ok, 1)
                else:
                    dve.tensor_scalar(shift[g % 2], rowmax[g % 2], qscale[:, bass.ds(t.v, 1)], -1.0, ALU.mult,
                                      ALU.mult).then_inc(shift_ok, 1)

            def keys0(L, t):
                n = t.plus(T * L)
                need(dve, k_ok, n.v + 1)
                need(dve, pe_s, 4 * n.v - 2)
                dve.tensor_tensor(kbd[:, 0, :, :], kT[:, 0:P].unsqueeze(1).to_broadcast([P, 8, P]),
                                  headrow.unsqueeze(2).to_broadcast([P, 8, P]), ALU.mult).then_inc(kbd0_ok, 1)

            def values(L, t):
                n = t.plus(T * L)
                need(dve, pe_v, n.v + 1)
                need(dve, pe_pv, 4 * n.v - 4)
                dve.tensor_tensor(vaug[t.par][:, :, 0:HD], bank[7][:, 0:D].rearrange("p (h w) -> p h w", h=H),
                                  bvo[:, 0, :].rearrange("p (h w) -> p h w", h=H), ALU.add).then_inc(v_ok, 1)

            def divide(L, t):
                n = t.plus(T * L)
                o = bank[4][:, 0:H * VW].rearrange("p (h w) -> p h w", h=H)
                need(dve, pe_pv, 4 * n.v + 4)
                dve.reciprocal(rsum.unsqueeze(2), o[:, :, HD:VW]).then_inc(rs_ok, 1)
                need(dve, rs_ok, n.v + 1)
                need(dve, pe_oT, n.v)
                dve.tensor_tensor(on.rearrange("p (h w) -> p h w", h=H), o[:, :, 0:HD],
                                  rsum.unsqueeze(2).to_broadcast([P, H, HD]), ALU.mult).then_inc(o_ok, 1)

            def residual(L, t):
                n = t.plus(T * L)
                need(dve, pe_o, n.v + 1)
                dve.tensor_tensor(proj, bank[7][:, 0:D], bvo[:, 1, :], ALU.add).then_inc(t_ok, 1)
                need(dve, t_ok, n.v + 1)
                dve.scalar_tensor_tensor(out=at(x, t.v), in0=proj, scalar=tgate[:, L:L + 1], in1=at(x, t.v),
                                         op0=ALU.mult, op1=ALU.add).then_inc(x_ok, 1)

            dve.wait_ge(const_in, 16 * SMALL)
            def combine(L, t):
                n = t.plus(T * L)
                if L:
                    need(dve, last_got[t.off % 4], 32 * (t.quarter + 1))
                else:
                    need(dve, got, 32 * (t.v + 1))
                for c, done in enumerate((half_ok, cx_ok)):
                    dve.scalar_tensor_tensor(out=at(x, t.v), in0=(ylast[t.off % 4] if L else ygot)[c], scalar=gsel[:, c, bass.ds(t.v, 1)],
                                             in1=at(x, t.v), op0=ALU.mult, op1=ALU.add).then_inc(done, 1)
                    if c == 0:
                        need(dve, half_ok, n.v + 1)

            def logits(L, t):
                n, E = t.plus(T * L), EXPERTS[L]
                pair = chosen(L)[0][:, t.par, :]
                need(dve, pe_lg, n.v + 1)
                if L == 0:
                    dve.tensor_scalar(pair, bank[6][:, 0:E], 0.0, None, ALU.add)
                    dve.tensor_scalar(at(logit.rearrange("p (t e) -> p t e", t=T), t.v), bank[6][:, 0:E], 0.0, None,
                                      ALU.add).then_inc(lg_ok, 1)
                else:
                    dve.tensor_tensor(pair, bank[6][:, 0:E], rb[:], ALU.add).then_inc(lg_ok, 1)

            def choose(L, t, part):
                n, E = t.plus(T * L), EXPERTS[L]
                pair, rest, tmp, rank, oh, prod, both, m, r = chosen(L)
                revs = rev[L].unsqueeze(1).to_broadcast([P, 2, E])

                def over_e(v):
                    return v.unsqueeze(2).to_broadcast([P, 2, E])

                def step(k, i):
                    i.then_inc(picked, 1)
                    dve.wait_ge(picked, LINKS * n.half + k)

                if part < 2:
                    logits_, k = (pair, 0) if part == 0 else (rest, 6)
                    if part == 0:
                        need(dve, lg_ok, n.v + 2)
                    step(k + 1, dve.tensor_reduce(m[:, part, :], logits_, AX.X, ALU.max))
                    step(k + 2, dve.tensor_tensor(tmp, logits_, over_e(m[:, part, :]), ALU.is_equal))
                    step(k + 3, dve.tensor_tensor(tmp, tmp, revs, ALU.mult))
                    step(k + 4, dve.tensor_reduce(r, tmp, AX.X, ALU.max))
                    step(k + 5, dve.tensor_tensor(oh[:, part], over_e(r), revs, ALU.is_equal))
                    if part == 0:
                        step(6, dve.scalar_tensor_tensor(out=rest, in0=oh[:, 0], scalar=-3e38, in1=pair, op0=ALU.mult, op1=ALU.add))
                    else:
                        dve.tensor_tensor(both.rearrange("p (t e) -> p t e", t=2), oh[:, 0], oh[:, 1], ALU.add).then_inc(both_ok, 1)
                        dve.tensor_scalar(best[:, :, bass.ds(t.v, 2)], m, 1.0, None, ALU.mult)
                elif part == 2:
                    need(dve, pe_rank, n.half + 1)
                    step(12, dve.tensor_tensor(rank, bank[6][:, 32:32 + 2 * E].rearrange("p (t e) -> p t e", t=2),
                                               taken[:, 0:E].unsqueeze(1).to_broadcast([P, 2, E]), ALU.add))
                    dve.tensor_tensor(taken[:, 0:E], taken[:, 0:E], bank[6][:, 96:96 + E], ALU.add).then_inc(rank_read, 1)
                else:
                    step(13, dve.tensor_tensor(prod, oh, rank.unsqueeze(1).to_broadcast([P, 2, 2, E]), ALU.mult))
                    step(14, dve.tensor_reduce(m, prod, AX.X, ALU.add))
                    for o in range(2):
                        need(dve, scattered[o], 32 * n.half)
                    dve.tensor_copy(slot_pair[:], m).then_inc(pair_ok, 1)
                    dve.tensor_scalar(row[:, :, bass.ds(t.v, 2)], m, 1.0, None, ALU.mult)

            dve.wait_ge(set_ok, 1)
            link(dve.tensor_scalar(qscale[:], qmask[:], 0.0, 0.25, ALU.not_equal, ALU.mult))
            for L in range(2):
                def loaded(t, L=L):
                    return (x_in[t.par], 16 * (t.half + 1)) if L == 0 else (cx_ok, t.v + 1)

                if L:
                    for o in range(2):
                        dve.wait_ge(ex[0][f"out{o}"], 16 * SLOT_TILES[0] // 4)
                link(dve.tensor_copy(taken[:, 0:EXPERTS[L]], region[:, 0:EXPERTS[L]]))
                for i in range(2):
                    dve.memset(vaug[i][:, :, HD:VW], 1.0).then_inc(ones_ok, 1)
                t0, t1 = Tile(0, 0), Tile(0, 1)
                if L:
                    combine(0, t0)
                moments(0, L, t0, loaded(t0))
                normalise(0, L, t0)
                if L == 0:
                    dve.wait_ge(bv_in, 32)
                keys0(L, t0)
                values(L, t0)
                if L:
                    combine(0, t1)
                moments(0, L, t1, loaded(t1))
                normalise(0, L, t1)
                def attend(t, L=L, loaded=loaded):
                    even = t.off % 2 == 0
                    if inside(t, 0):
                        scores(L, t, 0)
                    if inside(t, -2):
                        moments(1, L, t.plus(-2), (x_ok, t.plus(T * L - 2).v + 1))
                    if inside(t, -3):
                        logits(L, t.plus(-3))
                    if not even and inside(t, -5):
                        choose(L, t.plus(-5), 2)
                    if even and inside(t, -4):
                        choose(L, t.plus(-4), 0)
                    if inside(t, 0):
                        scores(L, t, 1)
                    if inside(t, -2):
                        normalise(1, L, t.plus(-2))
                    if inside(t, -1):
                        divide(L, t.plus(-1))
                    if L and inside(t, 2):
                        combine(0, t.plus(2))
                    if inside(t, 0):
                        scores(L, t, 2)
                    if inside(t, 1):
                        values(L, t.plus(1))
                        keys0(L, t.plus(1))
                    if inside(t, 2):
                        moments(0, L, t.plus(2), loaded(t.plus(2)))
                    if inside(t, 0):
                        scores(L, t, 3)
                    if inside(t, 2):
                        normalise(0, L, t.plus(2))
                    if inside(t, -1):
                        residual(L, t.plus(-1))
                    if even and inside(t, -4):
                        choose(L, t.plus(-4), 1)
                    if not even and inside(t, -5):
                        choose(L, t.plus(-5), 3)
                tiles(dve, T + LAG, *PEEL, attend, gate)

                E, nj = EXPERTS[L], SLOT_TILES[L]
                dve.wait_ge(rank_read, T // 2 * (L + 1))
                dve.tensor_copy(tail[:, 0:E], taken[:, 0:E]).then_inc(tail_ok, 1)
                small = [rsmall[:, i * T:(i + 1) * T] for i in range(16)]
                count, whole = small[8][:, 0:E], small[9].bitcast(I32)[:, 0:E]
                link(dve.tensor_tensor(count, taken[:, 0:E], region[:, 0:E], ALU.subtract))
                link(dve.tensor_scalar(whole, count, float(P - 1), None, ALU.add))
                link(dve.tensor_scalar(whole, whole, 7, 7, ALU.logical_shift_right, ALU.logical_shift_left))
                ends = [small[10][:, 0:E], small[11][:, 0:E]]
                link(dve.tensor_copy(ends[0], whole))
                link(dve.tensor_scalar(count, ends[0], -1.0, float(REGION), ALU.mult, ALU.add))
                step, a = 1, 0
                while step < E:
                    dve.tensor_copy(ends[1 - a][:, 0:step], ends[a][:, 0:step])
                    link(dve.tensor_tensor(ends[1 - a][:, step:E], ends[a][:, step:E], ends[a][:, 0:E - step], ALU.add))
                    step, a = 2 * step, 1 - a
                over, skip = (rtmp[i][:, 0:nj * E].rearrange("p (j e) -> p j e", j=nj) for i in (2, 3))
                link(dve.tensor_tensor(over, starts[:, 0:nj].unsqueeze(2).to_broadcast([P, nj, E]),
                                       ends[a].unsqueeze(1).to_broadcast([P, nj, E]), ALU.is_ge))
                link(dve.tensor_tensor(skip, over, count.unsqueeze(1).to_broadcast([P, nj, E]), ALU.mult))
                te_f, row_f = rtmp[0][:, 512:512 + nj], rtmp[0][:, 576:576 + nj]
                dve.tensor_reduce(te_f, over, AX.X, ALU.add)
                link(dve.tensor_reduce(row_f, skip, AX.X, ALU.add))
                dve.tensor_scalar(tile_expert[:, 0:nj], te_f, float(E - 1), None, ALU.min)
                link(dve.tensor_tensor(row_f, row_f, starts[:, 0:nj], ALU.add))
                dve.tensor_scalar(tile_row[:, 0:nj], row_f, float(E * REGION + (SPARE[L] - 1) * P), None,
                                  ALU.min).then_inc(slot_ok, 1)

                def before_row(i, E=E):
                    return rtmp[i][:, 0:2 * T * (E - 1)].rearrange("p (j e) -> p j e", e=E - 1)

                def weights_begin(L=L, E=E, small=small):
                    dve.tensor_tensor(small[1], best[:, 1, :], best[:, 0, :], ALU.subtract).then_inc(m_ok, 1)
                    if L == 0:
                        dve.tensor_tensor(rtmp[0][:, 0:T * E].rearrange("p (t e) -> p t e", t=T),
                                          logit.rearrange("p (t e) -> p t e", t=T),
                                          best[:, 0, :].unsqueeze(2).to_broadcast([P, T, E]), ALU.subtract).then_inc(m_ok, 1)

                def weights_end(L=L, E=E, small=small):
                    if L == 0:
                        dve.wait_ge(expo_ok, 2)
                        link(dve.tensor_reduce(small[3], rtmp[1][:, 0:T * E].rearrange("p (t e) -> p t e", t=T), AX.X, ALU.add))
                    else:
                        dve.wait_ge(expo_ok, 3)
                        link(dve.tensor_scalar(small[3], small[2], 1.0, None, ALU.add))
                    link(dve.reciprocal(small[3], small[3]))
                    link(dve.tensor_scalar(gsel[:, 0, :], small[3], tgate[:, 2 + L:3 + L], None, ALU.mult))
                    dve.tensor_tensor(gsel[:, 1, :], gsel[:, 0, :], small[2], ALU.mult)

                def slots_begin(E=E, count=count, over=before_row(2), skip=before_row(3)):
                    rows_f = row[:].rearrange("p c t -> p (c t)")
                    link(dve.tensor_tensor(over, rows_f.unsqueeze(2).to_broadcast([P, 2 * T, E - 1]),
                                           region[:, 1:E].unsqueeze(1).to_broadcast([P, 2 * T, E - 1]), ALU.is_ge))
                    link(dve.tensor_tensor(skip, over, count[:, 0:E - 1].unsqueeze(1).to_broadcast([P, 2 * T, E - 1]), ALU.mult))

                def slots_end(L=L, skip=before_row(3)):
                    link(dve.tensor_reduce(rtmp[0][:, 640:640 + 2 * T], skip, AX.X, ALU.add))
                    dve.tensor_tensor(slot[:].rearrange("p c t -> p (c t)"), row[:].rearrange("p c t -> p (c t)"), rtmp[0][:, 640:640 + 2 * T],
                                      ALU.subtract).then_inc(index_ok, 1)
                    dve.wait_ge(index_ok, L + 1)

                def shared_h(t):
                    need(dve, sh_sig, t.v + 1)
                    need(dve, sh_lo, t.v - 1)
                    dve.tensor_tensor(sh_hid[t.par], bank[t.par][:, 0:2 * P], sh_act[t.par], ALU.mult).then_inc(sh_h, 1)
                    need(dve, sh_hi, t.v + 1)
                    dve.tensor_tensor(sh_hlo[t.par], sh_hid[t.par], sh_hhi[t.par], ALU.subtract).then_inc(sh_lo, 1)

                def shared_x(t):
                    need(dve, sh_dn, t.v + 1)
                    dve.scalar_tensor_tensor(out=at(x, t.v), in0=bank[2 + t.par][:, 0:D], scalar=tgate[:, 2:3],
                                             in1=at(x, t.v), op0=ALU.mult, op1=ALU.add).then_inc(sh_x, 1)

                def shared(t):
                    shared_h(t)
                    if not isinstance(t.v, int) or t.v > 0:
                        shared_x(t.plus(-1))
                if L == 0:
                    dve.wait_ge(xr_ok, T)
                    weights_begin()
                    shared(Tile(0, 0))
                    shared(Tile(0, 1))
                    weights_end()
                    shared(Tile(0, 2))
                    slots_begin()
                    shared(Tile(0, 3))
                    slots_end()
                    with dve.Fori(0, (T - 4) // 2) as r:
                        shared(Tile(r, 4))
                        shared(Tile(r, 5))
                    shared_x(Tile(0, T - 1))
                else:
                    weights_begin()
                    weights_end()
                    slots_begin()
                    slots_end()

                s = ex[L]

                experts, number = Experts(nc, dve, "dve_expert", L), {}

                def result(j, L=L, s=s, number=number):
                    need(dve, s["dn"], j.v + 1)
                    J = j.off % 4 // 2
                    need(dve, s[f"out{J}"], 16 * j.quarter)
                    to = yrow[J][:, j.par, :]
                    if L and isinstance(j.v, int) and j.v == 0:
                        dve.wait_ge(b2_in, 16)
                    if L == 0:
                        dve.tensor_copy(to, bank[6 + j.par][:, 0:D]).then_inc(s["y"], 1)
                    else:
                        dve.tensor_tensor(to, bank[6 + j.par][:, 0:D], column(b2.rearrange("p e d -> p (e d)"), 0, number[j.off][1], 7 * D, D), ALU.add).then_inc(s["y"], 1)

                def expert0(j, s=s, result=result):
                    q = j.off % 4
                    need(dve, s["sig"], j.v + 1)
                    need(dve, s["lo"], j.v - 3)
                    dve.tensor_tensor(hid0[q], bank[2 + q][:, 0:P], sig0[q], ALU.mult).then_inc(s["h"], 1)
                    if not isinstance(j.v, int) or j.v > 0:
                        result(j.plus(-1))
                    need(dve, s["hi"], j.v + 1)
                    need(dve, s["dn"], j.v - 3)
                    dve.tensor_tensor(hid0_lo[q], hid0[q], hid0_hi[q], ALU.subtract).then_inc(s["lo"], 1)

                def expert1(j, s=s, result=result, experts=experts, number=number):
                    more = not isinstance(j.v, int)
                    if j.off == 4 and more or j.off == SLOT_TILES[1] - 4:
                        for i in (1, 2):
                            number[j.off - i] = (None, experts.last(D, i))
                    if j.off % 4 == 0:
                        for i, e in enumerate(experts.load(tile_expert, j, 1)):
                            number[j.off + i] = [dve.snap(e * w) for w in (F1 // P, D)]
                    e = number[j.off][0]
                    need(dve, s["up"], j.v + 1)
                    need(dve, s["lo"], j.v - 1)
                    for m in range(4):
                        i = dve.tensor_scalar(hid[j.par][:, m * P:(m + 1) * P], bank[2 + 2 * j.par][:, m * P:(m + 1) * P],
                                              column(b1, m, e, 7 * F1 // P, 1), 0.0, ALU.add, ALU.max)
                    i.then_inc(s["h"], 1)
                    if more or j.v > 1:
                        result(j.plus(-2))
                    need(dve, s["hi"], j.v + 1)
                    dve.tensor_tensor(hid_lo[j.off % 4], hid[j.par], hid_hi[j.off % 4], ALU.subtract).then_inc(s["lo"], 1)
                    if j.off in (3, 7) and (more or j.off == 3):
                        for i in (1, 2):
                            experts.keep(number[j.off + 1 - i][1], i)

                dve.wait_ge(slot_ok, L + 1)
                tiles(dve, SLOT_TILES[L], 4, 4, expert1 if L else expert0, gate, unroll=4)
                for i in ((2, 1) if L else (1,)):
                    result(Tile(0, SLOT_TILES[L] - i, 4))

            tiles(dve, T, 0, 0, lambda t: combine(1, t), unroll=4)
            dve.wait_ge(cx_ok, 2 * T)
            gate.close()

        @block.tensor
        def _(pe):
            gate = Gate(pe, gate_sem["pe"])

            def turn_x(w, L, t):
                need(pe, xn_ok[w], t.plus(T * L).v + 1)
                for k in range(KT):
                    i = pe.transpose(bank[5][:, k * P:(k + 1) * P], xn[2 * w + t.par][:, k * P:(k + 1) * P], ident)
                i.then_inc(pe_T[w], 1)

            def proj_k(L, t):
                n = t.plus(T * L)
                need(pe, ctx_in[t.par], 16 * (n.half + 1))
                need(pe, q_ok, n.v)
                if inside(t, -4):
                    need(pe, lg_ok, n.v - 3)
                elif L:
                    need(pe, lg_ok, T)
                if t.par == 0 and inside(t, -6):
                    need(pe, rank_read, n.half - 2)
                elif L:
                    need(pe, rank_read, T // 2)
                for m in range(KT):
                    for k in range(KT):
                        i = pe.matmul(bank[6][:, m * P:(m + 1) * P], wat[:, 1, k, m * P:(m + 1) * P],
                                      ctxT[t.par][:, k * P:(k + 1) * P], start=(k == 0), stop=(k == KT - 1))
                i.then_inc(pe_k, 1)

            def proj_v(L, t):
                n = t.plus(T * L)
                need(pe, ctx_in[t.par], 16 * (n.half + 1))
                need(pe, t_ok, n.v - 2 if inside(t, -3) else T * L)
                for k in range(KT):
                    i = pe.matmul(bank[7][:, 0:D], ctxT[t.par][:, k * P:(k + 1) * P], wat[:, 2, k, :],
                                  start=(k == 0), stop=(k == KT - 1))
                i.then_inc(pe_v, 1)

            def proj_q(L, t):
                n = t.plus(T * L)
                need(pe, xnT_ok[0], n.v + 1)
                need(pe, k_ok, n.v + 1)
                for m in range(KT):
                    for k in range(KT):
                        i = pe.matmul(bank[6][:, m * P:(m + 1) * P], wat[:, 0, k, m * P:(m + 1) * P],
                                      xnT[t.par][:, k * P:(k + 1) * P], start=(k == 0), stop=(k == KT - 1))
                i.then_inc(pe_q, 1)

            def score(L, t, g):
                n = t.plus(T * L)
                m = g // 2
                need(pe, q_ok, n.v + 1)
                need(pe, kbd1_ok if m else kbd0_ok, n.v + 1)
                need(pe, exp_ok, 4 * n.v + g - 1)
                i = pe.matmul(bank[g % 2][:], qT[t.par][:, m * P:(m + 1) * P],
                              kbd[:, m, 4 * (g % 2):4 * (g % 2) + 4, :].rearrange("p h t -> p (h t)"),
                              start=True, stop=(L == 1))
                if L == 0:
                    i = pe.matmul(bank[g % 2][:], identb, causal, start=False, stop=True)
                i.then_inc(pe_s, 1)

            def turn_p(L, t, g):
                n = t.plus(T * L)
                need(pe, exp_ok, 4 * n.v + g + 1)
                need(pe, pt_ok, 4 * n.v + g - 1)
                for h in range(GH):
                    i = pe.transpose(bank[2 + g % 2][:, h * P:(h + 1) * P], prob[g % 2][:, h * P:(h + 1) * P], ident)
                i.then_inc(pe_pt, 1)

            def weigh_v(L, t, g):
                n = t.plus(T * L)
                need(pe, pt_ok, 4 * n.v + g + 1)
                if g == 0:
                    if isinstance(t.v, int) and t.v == 0:
                        pe.wait_ge(ones_ok, 2 * (L + 1))
                    need(pe, v_ok, n.v + 1)
                    need(pe, o_ok, n.v)
                for h in range(GH):
                    c = (GH * g + h) * VW
                    i = pe.matmul(bank[4][:, c:c + VW], probT[g % 2][:, h * P:(h + 1) * P], vaug[t.par][:, GH * g + h, :],
                                  start=True, stop=True)
                i.then_inc(pe_pv, 1)

            def turn_o(L, t):
                n = t.plus(T * L)
                need(pe, o_ok, n.v + 1)
                if inside(t, -1):
                    need(pe, xnT_ok[1], n.v)
                else:
                    need(pe, xnT_ok[0], n.v + 3)
                for k in range(KT):
                    i = pe.transpose(bank[5][:, k * P:(k + 1) * P], on[:, k * P:(k + 1) * P], ident)
                i.then_inc(pe_oT, 1)

            def proj_o(L, t):
                n = t.plus(T * L)
                need(pe, oT_ok, n.v + 1)
                need(pe, v_ok, n.v + 3 if inside(t, 2) else T * (L + 1))
                for k in range(KT):
                    i = pe.matmul(bank[7][:, 0:D], oT[:, k * P:(k + 1) * P], wat[:, 3, k, :],
                                  start=(k == 0), stop=(k == KT - 1))
                i.then_inc(pe_o, 1)

            def bank6_free(L, t):
                n = t.plus(T * L)
                need(pe, q_ok, n.v + 4 if inside(t, 3) else T * (L + 1))
                if not inside(t, 3):
                    need(pe, lg_ok, min(n.v, T * (L + 1)))
                    need(pe, rank_read, T // 2 * L + (t.v - 3) // 2 + 1)

            def rank(L, t, tile):
                n, E = t.plus(T * L), EXPERTS[L]
                both = chosen(L)[6]
                bank6_free(L, tile)
                need(pe, both_ok, n.half + 1)
                ranks, totals = bank[6][:, 32:32 + 2 * E], bank[6][:, 96:96 + E]
                pe.matmul(ranks, earlier, both, start=True, stop=False, skip_group_check=True)
                pe.matmul(ranks[:, E:2 * E], onesb, both[:, 0:E], start=False, stop=True, skip_group_check=True)
                pe.matmul(totals, onesb, both[:, 0:E], start=True, stop=False, skip_group_check=True)
                i = pe.matmul(totals, onesb, both[:, E:2 * E], start=False, stop=True, skip_group_check=True)
                i.then_inc(pe_rank, 1)

            def route(L, t):
                n, E, e0 = t.plus(T * L), EXPERTS[L], 16 * L
                need(pe, xnT_ok[1], n.v + 1)
                bank6_free(L, t)
                for k in range(KT):
                    i = pe.matmul(bank[6][:, 0:E], xnT[2 + t.par][:, k * P:(k + 1) * P], wr[:, k, e0:e0 + E],
                                  start=(k == 0), stop=(k == KT - 1))
                i.then_inc(pe_lg, 1)

            for L in range(2):
                pe.wait_ge(wat_in, 16 * (L + 1))
                t0 = Tile(0, 0)
                E = EXPERTS[L]
                proj_v(L, t0)
                proj_k(L, t0)
                if L == 0:
                    pe.wait_ge(const_in, 16 * SMALL)
                    pe.wait_ge(cb_ok, 1)
                turn_x(0, L, t0)
                proj_q(L, t0)

                def attend(t, L=L):
                    if inside(t, 0):
                        score(L, t, 0)
                    if inside(t, 1):
                        need(pe, oT_ok, t.plus(T * L - 1).v if inside(t, -2) else T * L)
                        turn_x(0, L, t.plus(1))
                        proj_v(L, t.plus(1))
                    if t.off % 2 and inside(t, -5):
                        rank(L, t.plus(-5), t.plus(-3))
                    if inside(t, -3):
                        route(L, t.plus(-3))
                    if inside(t, -1):
                        turn_p(L, t.plus(-1), 3)
                        weigh_v(L, t.plus(-1), 2)
                    if inside(t, 0):
                        score(L, t, 1)
                    if inside(t, 1):
                        proj_k(L, t.plus(1))
                    if inside(t, 0):
                        turn_p(L, t, 0)
                    if inside(t, -1):
                        weigh_v(L, t.plus(-1), 3)
                    if inside(t, -2):
                        need(pe, xnT_ok[0], t.plus(T * L + 2).v if inside(t, 1) else T * (L + 1))
                        if not inside(t, 1):
                            need(pe, oT_ok, t.plus(T * L - 1).v)
                        turn_x(1, L, t.plus(-2))
                    if inside(t, 0):
                        score(L, t, 2)
                    if inside(t, 1):
                        proj_q(L, t.plus(1))
                    if inside(t, -1):
                        turn_o(L, t.plus(-1))
                    if inside(t, 0):
                        turn_p(L, t, 1)
                        weigh_v(L, t, 0)
                        score(L, t, 3)
                    if inside(t, -1):
                        proj_o(L, t.plus(-1))
                    if inside(t, 0):
                        turn_p(L, t, 2)
                        weigh_v(L, t, 1)
                tiles(pe, T + LAG, *PEEL, attend)

                w1h, w1l = (w[:, 0:KT * 2 * FS].rearrange("p (k f) -> p k f", k=KT) for w in (shi, slo))
                w2h, w2l = (w[:, KT * 2 * FS:].rearrange("p (k f) -> p k f", k=KT) for w in (shi, slo))

                def shared_down(t):
                    need(pe, sh_lo, t.v + 1)
                    need(pe, sh_x, t.v - 1)
                    for k in range(KT):
                        f = slice(k * P, (k + 1) * P)
                        for q, (a, b) in enumerate(((sh_hhi, w2h), (sh_hlo, w2h), (sh_hhi, w2l))):
                            i = pe.matmul(bank[2 + t.par][:, 0:D], a[t.par][:, f], b[:, k, :],
                                          start=(k == 0 and q == 0), stop=(k == KT - 1 and q == 2))
                    i.then_inc(sh_dn, 1)

                def shared(t):
                    need(pe, sh_h, t.v - 1)
                    xt = at(xT, t.v)
                    for m in range(4):
                        for k in range(KT):
                            hi, lo = xt[:, k * P:(k + 1) * P], xt[:, (KT + k) * P:(KT + k + 1) * P]
                            f = slice(m * P, (m + 1) * P)
                            for q, (w, v) in enumerate(((w1h, hi), (w1h, lo), (w1l, hi))):
                                i = pe.matmul(bank[t.par][:, m * P:(m + 1) * P], w[:, k, f], v,
                                              start=(k == 0 and q == 0), stop=(k == KT - 1 and q == 2))
                    i.then_inc(sh_up, 1)
                    if not isinstance(t.v, int) or t.v > 0:
                        shared_down(t.plus(-1))
                if L == 0:
                    pe.wait_ge(sws_ok, 2)
                    pe.wait_ge(xt_ok, T)
                    pe.wait_ge(lg_ok, T)
                    tiles(pe, T, 2, 0, shared)
                    shared_down(Tile(0, T - 1))
                    pe.wait_ge(sh_x, T)

                s = ex[L]
                pe.wait_ge(slot_ok, L + 1)

                def turn_rows(j, s=s):
                    J = j.off % 4 // 2
                    need(pe, s[f"rows{J}"], 32 * (j.quarter + 1))
                    need(pe, s["rT"], j.v - 1)
                    to = bank[j.par][:, 0:2 * P].bitcast(BF16)
                    for c in range(4):
                        i = pe.transpose(to[:, c * P:(c + 1) * P], rows[J][:, j.par, c * P:(c + 1) * P], identb)
                    i.then_inc(s["pe_rT"], 1)

                slabs = SLAB[L] * (1 + L)
                most = (EXPERTS[L] - 1) * slabs
                w_hi, w_lo = (arena[:, i * T * SLAB[L]:(i + 1) * T * SLAB[L]] for i in range(2))

                def up(e, j, L, m, k, to):
                    c = m * P + k * (SLAB[1] if L else 2 * F0)
                    hi, lo = (rowsT[j.off % 4][:, i * P:(i + 1) * P] for i in (k, KT + k))
                    for q, (w, v) in enumerate(((w_hi, hi), (w_hi, lo), (w_lo, hi))):
                        i = pe.matmul(to, column(w, c, e, most, P), v, start=(k == 0 and q == 0),
                                      stop=(k == KT - 1 and q == 2))
                    return i

                def down(e, j, k, L=L):
                    if L == 0:
                        nk, c = 1, KT * 2 * F0
                        a_hi, a_lo = hid0_hi[j.off % 4], hid0_lo[j.off % 4]
                    else:
                        nk, c = F1 // P, k // 4 * SLAB[1] + F1 + (k % 4) * D
                        a_hi, a_lo = (v[j.off % 4][:, k * P:(k + 1) * P] for v in (hid_hi, hid_lo))
                    for q, (a, w) in enumerate(((a_hi, w_hi), (a_lo, w_hi), (a_hi, w_lo))):
                        i = pe.matmul(bank[6 + j.par][:, 0:D], a, column(w, c, e, most, D),
                                      start=(k == 0 and q == 0), stop=(k == nk - 1 and q == 2))
                    return i

                def hidden_ready(j, s=s):
                    need(pe, s["y"], j.v - 1)
                    need(pe, s["lo"], j.v + 1)

                experts, number = Experts(nc, pe, "pe_expert", L), {}

                def begin(j, L=L, s=s, turn_rows=turn_rows, experts=experts, number=number, slabs=slabs):
                    more = not isinstance(j.v, int)
                    if j.off == 4 and more or j.off == SLOT_TILES[L] - 4:
                        for i in range(1, 1 + L + 1):
                            number[j.off - i] = experts.last(slabs, i)
                    if j.off % 4 == 0:
                        number.update((j.off + i, e) for i, e in enumerate(experts.load(tile_expert, j, slabs)))
                    need(pe, s["h"], j.v - (1 if L else 3))
                    if more or j.v + 2 < SLOT_TILES[L]:
                        turn_rows(j.plus(2))
                    else:
                        need(pe, s["rT"], j.v + 1)

                def end(j, L=L, experts=experts, number=number):
                    if j.off == 3 or j.off == 7 and not isinstance(j.v, int):
                        for i in range(1, 1 + L + 1):
                            experts.keep(number[j.off + 1 - i], i)

                def expert0(j, s=s, begin=begin, end=end, up=up, down=down, hidden_ready=hidden_ready, number=number):
                    begin(j)
                    for m in range(2):
                        for k in range(KT):
                            i = up(number[j.off], j, 0, m, k, bank[2 + j.off % 4][:, m * P:(m + 1) * P])
                    i.then_inc(s["up"], 1)
                    if not isinstance(j.v, int) or j.v > 0:
                        hidden_ready(j.plus(-1))
                        down(number[j.off - 1], j.plus(-1), 0).then_inc(s["dn"], 1)
                    end(j)

                def expert1(j, s=s, begin=begin, end=end, up=up, down=down, hidden_ready=hidden_ready, number=number):
                    before = not isinstance(j.v, int) or j.v > 1
                    begin(j)
                    for m in range(8):
                        if m == 4:
                            gate((s["ha"], j.v - 1))
                        for k in range(KT):
                            i = up(number[j.off], j, 1, m, k, bank[2 + m // 4 + 2 * j.par][:, m % 4 * P:(m % 4 + 1) * P])
                        if m % 4 == 3:
                            i.then_inc(s["up" if m == 3 else "upb"], 1)
                        if before:
                            if m == 0:
                                hidden_ready(j.plus(-2))
                            i = down(number[j.off - 2], j.plus(-2), m)
                    if before:
                        i.then_inc(s["dn"], 1)
                    end(j)
                turn_rows(Tile(0, 0, 4))
                turn_rows(Tile(0, 1, 4))
                tiles(pe, SLOT_TILES[L], 4, 4, expert1 if L else expert0, gate, unroll=4)
                for i in ((2, 1) if L else (1,)):
                    j = Tile(0, SLOT_TILES[L] - i, 4)
                    hidden_ready(j)
                    for k in range(F1 // P if L else 1):
                        i = down(number[j.off], j, k)
                    i.then_inc(s["dn"], 1)
                pe.wait_ge(s["y"], SLOT_TILES[L])
            gate.close()


SMALL = 9


def laid_out(inputs):
    import numpy as np
    v = {k: np.asarray(a) for k, a in inputs.items()}
    c = np.ascontiguousarray
    f = {}
    for name in ("x", "g_xattn", "g_ffn", "L1_ffn_router_b", "L1_ffn_b2", "L0_xattn_bv", "L0_xattn_bo",
                 "L1_xattn_bv", "L1_xattn_bo"):
        f[name] = c(v[name])

    def down(w):
        return w.reshape(KT, P, -1).transpose(1, 0, 2)
    f["ctxT"] = c(v["ctx_1024"].reshape(T, P, KT, P).transpose(0, 3, 2, 1).reshape(T, P, KT * P))
    for L in range(2):
        w = [v[f"L{L}_xattn_W{n}"] for n in "qkvo"]
        if L:
            w = [a.T for a in w]
        f[f"wat{L}"] = c(np.stack([down(a) for a in w], 1).reshape(P, -1))
    f["bqk"] = c(np.stack([v[f"L{L}_xattn_b{n}"].reshape(KT, P).T for L in range(2) for n in "qk"], 1).reshape(P, -1))
    f["wr"] = c(np.concatenate([down(v["L0_ffn_Wg"].T), down(v["L1_ffn_router_w"])], 2).reshape(P, -1))
    f["qmask"] = c(v["mask_BxS_ik0"].T)
    f["b1"] = c(v["L1_ffn_b1"].reshape(8, F1 // P, P).transpose(2, 0, 1).reshape(P, -1))
    f["slab0"] = c(np.concatenate([v["L0_ffn_W1"].reshape(16, KT, P, 2 * F0).transpose(0, 2, 1, 3).reshape(16, P, -1),
                                   v["L0_ffn_W2"]], 2))
    f["slab1"] = c(np.concatenate([v["L1_ffn_W1"].reshape(16, P, F1),
                                   v["L1_ffn_W2"].reshape(16, 4, P, D).transpose(0, 2, 1, 3).reshape(16, P, 4 * D)], 2))
    f["shared_w"] = c(np.concatenate([down(v["L0_ffn_Ws1"]).reshape(P, -1), down(v["L0_ffn_Ws2"]).reshape(P, -1)], 1))
    p, q = np.arange(P)[:, None], np.arange(P)[None, :]
    f["cf"] = c(np.concatenate([np.eye(P), p // HD == np.arange(8)[None, :], np.broadcast_to(16 - np.arange(16), (P, 16)),
                                np.broadcast_to(8 - np.arange(8), (P, 8)), np.broadcast_to(128 * np.arange(48), (P, 48)),
                                np.broadcast_to(REGION * np.arange(16), (P, 16))],
                               1).astype(np.float32))
    f["cb"] = c(np.concatenate([np.eye(P), np.ones((P, P)), p < q, np.tile(np.where(q > p, NEG, 0.0), (1, GH))],
                               1).astype(np.float32))
    return f


def kernel(**inputs):
    import concourse.bacc as bacc
    from concourse.bass_utils import run_bass_kernel_spmd
    nc = bacc.Bacc("TRN2", target_bir_lowering=False, num_devices=1)
    arrays, args = {}, {}
    for name, a in laid_out(inputs).items():
        arrays[f"in_{name}"] = a
        args[name] = nc.dram_tensor(f"in_{name}", a.shape, mybir.dt.from_np(a.dtype), kind="ExternalInput").ap()
    o = nc.dram_tensor("out_x", (T, P, D), F32, kind="ExternalOutput").ap()
    build(nc, args, o)
    r = run_bass_kernel_spmd(nc, [arrays], core_ids=[0])
    return r.results[0]["out_x"]
```
